# Optimizing a Trainium2 kernel written in Bass

```python
import numpy as np
import jax
import jax.numpy as jnp

def _softmax(x, axis=-1):
    return jax.nn.softmax(x, axis=axis)

def _gelu(x):
    return jax.nn.gelu(x, approximate=True)

def _silu(x):
    return jax.nn.silu(x)

def _sigmoid(x):
    return jax.nn.sigmoid(x)

def _layernorm(x, axis=-1, eps=1e-05):
    m = jnp.mean(x, axis=axis, keepdims=True)
    v = jnp.var(x, axis=axis, keepdims=True)
    return (x - m) / jnp.sqrt(v + eps)

def _scatter_add(tgt, idx, src, axis=0):
    return tgt.at[idx].add(src)

def _segment_sum(src, seg, n):
    return jax.ops.segment_sum(src, seg, n)
kernel_name = 'mk_seq_postln_d1_jaxref_r8_c134c4'

def setup_inputs(seed: int=0):
    np.random.seed(seed)
    _w = jnp.asarray

    def _L0_attn_setup():
        import math
        import jax, jax.numpy as jnp
        import numpy as np
        B, T, DIM = (2, 256, 256)
        HEADS, HEAD_DIM = (16, 128)
        KV_GROUPS = 4
        N_KV = HEADS // KV_GROUPS
        LATENT = 64
        SEL_TOPK, SEL_HEADS, SEL_DIM = (64, 1, 64)
        SOFTCAP = 30.0
        EPS = 1e-06

        def _alibi_slopes(n):

            def pot(p):
                start = 2.0 ** (-2.0 ** (-(math.log2(p) - 3)))
                return [start * start ** i for i in range(p)]
            if math.log2(n).is_integer():
                return pot(n)
            cp = 2 ** int(math.floor(math.log2(n)))
            s = pot(cp)
            s += _alibi_slopes(2 * cp)[0::2][:n - cp]
            return s

        def _alibi_bias(h, t):
            slopes = jnp.asarray(_alibi_slopes(h), jnp.float32)
            pos = jnp.arange(t)
            dist = jnp.clip(pos[:, None] - pos[None, :], 0, None).astype(jnp.float32)
            return -slopes[:, None, None] * dist

        def _rope_emb(t, d):
            inv = 1.0 / 10000.0 ** (jnp.arange(0, d, 2, dtype=jnp.float32) / d)
            f = jnp.arange(t, dtype=jnp.float32)[:, None] * inv[None, :]
            return jnp.concatenate([f, f], axis=-1)

        def _apply_rotary(x, emb):
            cos = jnp.cos(emb)[None, :, None, :]
            sin = jnp.sin(emb)[None, :, None, :]
            x1, x2 = (x[..., 0::2], x[..., 1::2])
            c, s = (cos[..., 0::2], sin[..., 0::2])
            r = jnp.stack([x1 * c - x2 * s, x1 * s + x2 * c], axis=-1)
            return r.reshape(x.shape)

        def _rmsnorm(x, w):
            return x * jax.lax.rsqrt(jnp.mean(x * x, axis=-1, keepdims=True) + EPS) * w

        def _forward(x, w_q, b_q, w_down, b_down, w_up, b_up, w_o, b_o, qn_w, kn_w, gate_w, gate_b):
            b, t, _ = x.shape
            q = (x @ w_q + b_q).reshape(b, t, HEADS, HEAD_DIM)
            kv = (x @ w_down + b_down) @ w_up + b_up
            k = kv[..., :N_KV * HEAD_DIM].reshape(b, t, N_KV, HEAD_DIM)
            v = kv[..., N_KV * HEAD_DIM:].reshape(b, t, N_KV, HEAD_DIM)
            q = _rmsnorm(q, qn_w)
            k = _rmsnorm(k, kn_w)
            emb = _rope_emb(t, HEAD_DIM)
            q = _apply_rotary(q, emb)
            k = _apply_rotary(k, emb)
            k = jnp.repeat(k, KV_GROUPS, axis=2)
            v = jnp.repeat(v, KV_GROUPS, axis=2)
            q = q.transpose(0, 2, 1, 3)
            k = k.transpose(0, 2, 1, 3)
            v = v.transpose(0, 2, 1, 3)
            qs = jax.lax.stop_gradient(q[:, :SEL_HEADS, :, :SEL_DIM].astype(jnp.float32))
            ks = jax.lax.stop_gradient(k[:, :SEL_HEADS, :, :SEL_DIM].astype(jnp.float32))
            s = jnp.einsum('bhqd,bhkd->bhqk', qs, ks) / math.sqrt(SEL_DIM)
            tri = jnp.triu(jnp.ones((t, t), bool), 1)
            s = jnp.where(tri, -jnp.inf, s)
            idx = jax.lax.top_k(s, SEL_TOPK)[1]
            sel = jnp.zeros((b, SEL_HEADS, t, t), bool)
            bi = jnp.arange(b)[:, None, None, None]
            hi = jnp.arange(SEL_HEADS)[None, :, None, None]
            ti = jnp.arange(t)[None, None, :, None]
            sel = sel.at[bi, hi, ti, idx].set(True)
            sel = sel | jnp.eye(t, dtype=bool)[None, None]
            sel = sel & ~tri
            sel = jnp.any(sel, axis=1, keepdims=True)
            amask = jnp.where(sel, 0.0, -jnp.inf).astype(jnp.float32)
            scores = jnp.einsum('bhqd,bhkd->bhqk', q, k) / math.sqrt(HEAD_DIM)
            scores = jnp.tanh(scores / SOFTCAP) * SOFTCAP
            scores = scores + _alibi_bias(HEADS, t)[None] + amask
            attn = jax.nn.softmax(scores, axis=-1)
            y = jnp.einsum('bhqk,bhkd->bhqd', attn, v)
            gate = jax.nn.sigmoid(jnp.einsum('bhtd,hde->bhte', y, gate_w) + gate_b[None, :, None, :])
            y = (y * gate).transpose(0, 2, 1, 3).reshape(b, t, HEADS * HEAD_DIM)
            return y @ w_o + b_o
        key = jax.random.key(seed)
        ks = jax.random.split(key, 6)
        sd = 0.02
        return {'x': jax.random.normal(ks[0], (B, T, DIM), jnp.float32), 'w_q': jax.random.normal(ks[1], (DIM, HEADS * HEAD_DIM), jnp.float32) * sd, 'b_q': jnp.zeros((HEADS * HEAD_DIM,), jnp.float32), 'w_down': jax.random.normal(ks[2], (DIM, LATENT), jnp.float32) * sd, 'b_down': jnp.zeros((LATENT,), jnp.float32), 'w_up': jax.random.normal(ks[3], (LATENT, 2 * N_KV * HEAD_DIM), jnp.float32) * sd, 'b_up': jnp.zeros((2 * N_KV * HEAD_DIM,), jnp.float32), 'w_o': jax.random.normal(ks[4], (HEADS * HEAD_DIM, DIM), jnp.float32) * sd, 'b_o': jnp.zeros((DIM,), jnp.float32), 'qn_w': jnp.ones((HEAD_DIM,), jnp.float32), 'kn_w': jnp.ones((HEAD_DIM,), jnp.float32), 'gate_w': jax.random.normal(ks[5], (HEADS, HEAD_DIM, HEAD_DIM), jnp.float32) * (1.0 / math.sqrt(HEAD_DIM)), 'gate_b': jnp.zeros((HEADS, HEAD_DIM), jnp.float32)}
    _L0_attn_in = _L0_attn_setup()

    def _L0_ffn_setup():
        import jax, jax.numpy as jnp
        import numpy as np
        EPS = 1e-08

        def _bit_quant(w):
            scale = jnp.maximum(jnp.mean(jnp.abs(w)), EPS)
            w_ternary = jnp.clip(jnp.round(w / scale), -1.0, 1.0)
            return w + jax.lax.stop_gradient(w_ternary - w)
        key = jax.random.key(seed)
        k = jax.random.split(key, 5)
        emb, dff = (256, 1024)
        B, S = (4, 256)
        x = jax.random.normal(k[0], (B, S, emb), dtype=jnp.float32)
        w1 = jax.random.normal(k[1], (dff, emb), dtype=jnp.float32) * 0.02
        b1 = jax.random.normal(k[2], (dff,), dtype=jnp.float32) * 0.02
        w2 = jax.random.normal(k[3], (emb, dff), dtype=jnp.float32) * 0.02
        b2 = jax.random.normal(k[4], (emb,), dtype=jnp.float32) * 0.02
        return {'x': x, 'w1': w1, 'b1': b1, 'w2': w2, 'b2': b2}
    _L0_ffn_in = _L0_ffn_setup()
    _d = {'L0_attn_x': _L0_attn_in['x'], 'L0_attn_w_q': _L0_attn_in['w_q'], 'L0_attn_b_q': _L0_attn_in['b_q'], 'L0_attn_w_down': _L0_attn_in['w_down'], 'L0_attn_b_down': _L0_attn_in['b_down'], 'L0_attn_w_up': _L0_attn_in['w_up'], 'L0_attn_b_up': _L0_attn_in['b_up'], 'L0_attn_w_o': _L0_attn_in['w_o'], 'L0_attn_b_o': _L0_attn_in['b_o'], 'L0_attn_qn_w': _L0_attn_in['qn_w'], 'L0_attn_kn_w': _L0_attn_in['kn_w'], 'L0_attn_gate_w': _L0_attn_in['gate_w'], 'L0_attn_gate_b': _L0_attn_in['gate_b'], 'L0_ffn_w1': _L0_ffn_in['w1'], 'L0_ffn_b1': _L0_ffn_in['b1'], 'L0_ffn_w2': _L0_ffn_in['w2'], 'L0_ffn_b2': _L0_ffn_in['b2']}
    _x0 = _d['L0_attn_x']
    _d['L0_attn_x'] = jax.random.normal(jax.random.fold_in(jax.random.key(seed), 1), (4, 512, 256), dtype=_x0.dtype)
    del _x0
    return _d

def reference(L0_attn_x, L0_attn_w_q, L0_attn_b_q, L0_attn_w_down, L0_attn_b_down, L0_attn_w_up, L0_attn_b_up, L0_attn_w_o, L0_attn_b_o, L0_attn_qn_w, L0_attn_kn_w, L0_attn_gate_w, L0_attn_gate_b, L0_ffn_w1, L0_ffn_b1, L0_ffn_w2, L0_ffn_b2):

    def _L0_attn_ref(x, w_q, b_q, w_down, b_down, w_up, b_up, w_o, b_o, qn_w, kn_w, gate_w, gate_b):
        import math
        import jax, jax.numpy as jnp
        import numpy as np
        B, T, DIM = (2, 256, 256)
        HEADS, HEAD_DIM = (16, 128)
        KV_GROUPS = 4
        N_KV = HEADS // KV_GROUPS
        LATENT = 64
        SEL_TOPK, SEL_HEADS, SEL_DIM = (64, 1, 64)
        SOFTCAP = 30.0
        EPS = 1e-06

        def _alibi_slopes(n):

            def pot(p):
                start = 2.0 ** (-2.0 ** (-(math.log2(p) - 3)))
                return [start * start ** i for i in range(p)]
            if math.log2(n).is_integer():
                return pot(n)
            cp = 2 ** int(math.floor(math.log2(n)))
            s = pot(cp)
            s += _alibi_slopes(2 * cp)[0::2][:n - cp]
            return s

        def _alibi_bias(h, t):
            slopes = jnp.asarray(_alibi_slopes(h), jnp.float32)
            pos = jnp.arange(t)
            dist = jnp.clip(pos[:, None] - pos[None, :], 0, None).astype(jnp.float32)
            return -slopes[:, None, None] * dist

        def _rope_emb(t, d):
            inv = 1.0 / 10000.0 ** (jnp.arange(0, d, 2, dtype=jnp.float32) / d)
            f = jnp.arange(t, dtype=jnp.float32)[:, None] * inv[None, :]
            return jnp.concatenate([f, f], axis=-1)

        def _apply_rotary(x, emb):
            cos = jnp.cos(emb)[None, :, None, :]
            sin = jnp.sin(emb)[None, :, None, :]
            x1, x2 = (x[..., 0::2], x[..., 1::2])
            c, s = (cos[..., 0::2], sin[..., 0::2])
            r = jnp.stack([x1 * c - x2 * s, x1 * s + x2 * c], axis=-1)
            return r.reshape(x.shape)

        def _rmsnorm(x, w):
            return x * jax.lax.rsqrt(jnp.mean(x * x, axis=-1, keepdims=True) + EPS) * w

        def _forward(x, w_q, b_q, w_down, b_down, w_up, b_up, w_o, b_o, qn_w, kn_w, gate_w, gate_b):
            b, t, _ = x.shape
            q = (x @ w_q + b_q).reshape(b, t, HEADS, HEAD_DIM)
            kv = (x @ w_down + b_down) @ w_up + b_up
            k = kv[..., :N_KV * HEAD_DIM].reshape(b, t, N_KV, HEAD_DIM)
            v = kv[..., N_KV * HEAD_DIM:].reshape(b, t, N_KV, HEAD_DIM)
            q = _rmsnorm(q, qn_w)
            k = _rmsnorm(k, kn_w)
            emb = _rope_emb(t, HEAD_DIM)
            q = _apply_rotary(q, emb)
            k = _apply_rotary(k, emb)
            k = jnp.repeat(k, KV_GROUPS, axis=2)
            v = jnp.repeat(v, KV_GROUPS, axis=2)
            q = q.transpose(0, 2, 1, 3)
            k = k.transpose(0, 2, 1, 3)
            v = v.transpose(0, 2, 1, 3)
            qs = jax.lax.stop_gradient(q[:, :SEL_HEADS, :, :SEL_DIM].astype(jnp.float32))
            ks = jax.lax.stop_gradient(k[:, :SEL_HEADS, :, :SEL_DIM].astype(jnp.float32))
            s = jnp.einsum('bhqd,bhkd->bhqk', qs, ks) / math.sqrt(SEL_DIM)
            tri = jnp.triu(jnp.ones((t, t), bool), 1)
            s = jnp.where(tri, -jnp.inf, s)
            idx = jax.lax.top_k(s, SEL_TOPK)[1]
            sel = jnp.zeros((b, SEL_HEADS, t, t), bool)
            bi = jnp.arange(b)[:, None, None, None]
            hi = jnp.arange(SEL_HEADS)[None, :, None, None]
            ti = jnp.arange(t)[None, None, :, None]
            sel = sel.at[bi, hi, ti, idx].set(True)
            sel = sel | jnp.eye(t, dtype=bool)[None, None]
            sel = sel & ~tri
            sel = jnp.any(sel, axis=1, keepdims=True)
            amask = jnp.where(sel, 0.0, -jnp.inf).astype(jnp.float32)
            scores = jnp.einsum('bhqd,bhkd->bhqk', q, k) / math.sqrt(HEAD_DIM)
            scores = jnp.tanh(scores / SOFTCAP) * SOFTCAP
            scores = scores + _alibi_bias(HEADS, t)[None] + amask
            attn = jax.nn.softmax(scores, axis=-1)
            y = jnp.einsum('bhqk,bhkd->bhqd', attn, v)
            gate = jax.nn.sigmoid(jnp.einsum('bhtd,hde->bhte', y, gate_w) + gate_b[None, :, None, :])
            y = (y * gate).transpose(0, 2, 1, 3).reshape(b, t, HEADS * HEAD_DIM)
            return y @ w_o + b_o
        return _forward(x, w_q, b_q, w_down, b_down, w_up, b_up, w_o, b_o, qn_w, kn_w, gate_w, gate_b)

    def _L0_ffn_ref(x, w1, b1, w2, b2):
        import jax, jax.numpy as jnp
        import numpy as np
        EPS = 1e-08

        def _bit_quant(w):
            scale = jnp.maximum(jnp.mean(jnp.abs(w)), EPS)
            w_ternary = jnp.clip(jnp.round(w / scale), -1.0, 1.0)
            return w + jax.lax.stop_gradient(w_ternary - w)
        w1q = _bit_quant(w1)
        w2q = _bit_quant(w2)
        h = jnp.einsum('bsd,fd->bsf', x, w1q) + b1
        h = jax.nn.gelu(h, approximate=False)
        return jnp.einsum('bsf,df->bsd', h, w2q) + b2
    x = L0_attn_x
    x = _layernorm(x + _L0_attn_ref(x, L0_attn_w_q, L0_attn_b_q, L0_attn_w_down, L0_attn_b_down, L0_attn_w_up, L0_attn_b_up, L0_attn_w_o, L0_attn_b_o, L0_attn_qn_w, L0_attn_kn_w, L0_attn_gate_w, L0_attn_gate_b), axis=-1)
    x = _layernorm(x + _L0_ffn_ref(x, L0_ffn_w1, L0_ffn_b1, L0_ffn_w2, L0_ffn_b2), axis=-1)
    return x

_drawn_inputs = setup_inputs


def setup_inputs(seed=0):
    import zlib

    import numpy as np

    out = dict(_drawn_inputs(seed))
    spreads = {'L0_attn_b_q': (0.0, 0.8),
     'L0_attn_b_down': (0.0, 0.8),
     'L0_attn_b_up': (0.0, 0.1),
     'L0_attn_b_o': (0.0, 0.1),
     'L0_attn_qn_w': (1.0, 0.6),
     'L0_attn_kn_w': (1.0, 0.6),
     'L0_attn_gate_b': (0.0, 0.8)}
    factors = {'L0_attn_w_q': 8.0,
     'L0_attn_w_down': 4.68,
     'L0_attn_w_up': 4.133,
     'L0_attn_gate_w': 8.0,
     'L0_ffn_b1': 39.397,
     'L0_ffn_b2': 64.0}
    for name, (base, spread) in spreads.items():
        noise = np.random.default_rng([zlib.crc32(name.encode()), seed]).standard_normal(out[name].shape)
        drawn = base * np.exp(spread * noise) if base else spread * noise
        out[name] = jnp.asarray(drawn.astype(out[name].dtype))
    for name, factor in factors.items():
        out[name] = (out[name] * factor).astype(out[name].dtype)
    return out
```

```python
from contextlib import ExitStack

import numpy as np

import concourse.bass as bass
from concourse import mybir

F32 = mybir.dt.float32
F32R = mybir.dt.float32r
BF16 = mybir.dt.bfloat16
ALU = mybir.AluOpType
ACT = mybir.ActivationFunctionType
AX_X = mybir.AxisListType.X

P = 128
B, T, DIM = 4, 512, 256
HEADS, HD = 16, 128
NKV = 4
GROUP = HEADS // NKV
LATENT = 64
TOPK = 64
SEL_DIM = 64
SOFTCAP = 30.0
RMS_EPS = 1e-6
LN_EPS = 1e-5
QUANT_EPS = 1e-8
DFF = 1024
NT = T // P
KD = DIM // P
NF = DFF // P
NQ = HEADS * HD
NK = NKV * HD
STEPS = HEADS
LEAD = 6
NTILES = B * HEADS
PIECE = [T - P * kt for kt in range(NT)]
OFF = [0, T, 2 * T, T + PIECE[1]]
CW = sum(PIECE)
BIG = 1.0e5
MASKED = -1.0e30
TAKEN = -3.0e38
ROUNDS = TOPK // 8
ORDER = [64 * a + 2 * i + c for a in range(2) for c in range(2) for i in range(32)]
PARTNER = [64 * a + 2 * i + 1 - c for a in range(2) for c in range(2) for i in range(32)]
C_COS, C_SIN, C_DIST, C_CAUSAL, C_EYE, C_OFFDIAG = 0, NT * P, 2 * NT * P, 2 * NT * P + CW, \
    2 * NT * P + CW + P, 2 * NT * P + CW + 2 * P
C_END = C_OFFDIAG + P


def slope(h):
    start = 2.0 ** (-2.0 ** (-(np.log2(HEADS) - 3)))
    return float(start * start ** h)


def constants():
    t = np.zeros((P, C_END), np.float32)
    inv = (np.float32(1.0) / np.power(np.float32(10000.0), np.arange(0, HD, 2, dtype=np.float32) / np.float32(HD))).astype(np.float32)
    f = np.arange(T, dtype=np.float32)[:, None] * inv[None, :]
    emb = np.concatenate([f, f], -1)[:, 0::2].astype(np.float64)
    cos, sin = np.cos(emb), np.sin(emb)
    pair = np.array([ORDER[i] // 2 for i in range(HD)])
    odd = np.array([ORDER[i] % 2 for i in range(HD)])
    c = cos[:, pair]
    s = sin[:, pair] * np.where(odd, 1.0, -1.0)
    t[:, C_COS:C_SIN] = c.reshape(NT, P, HD).transpose(1, 0, 2).reshape(P, -1)
    t[:, C_SIN:C_DIST] = s.reshape(NT, P, HD).transpose(1, 0, 2).reshape(P, -1)
    key = np.arange(P)[:, None]
    for kt in range(NT):
        d = np.arange(PIECE[kt])[None, :] - key
        t[:, C_DIST + OFF[kt]:C_DIST + OFF[kt] + PIECE[kt]] = np.where(d >= 0, d, BIG)
    t[:, C_CAUSAL:C_EYE] = np.where(np.arange(P)[None, :] > key, MASKED, 0.0)
    t[:, C_EYE:C_OFFDIAG] = np.eye(P)
    t[:, C_OFFDIAG:C_END] = 1.0 - np.eye(P)
    return t


def layer_program(nc, x, w_q, w_down, w_up, w_o, gate_w, w1, w2, biases, gate_b, b_down, b1,
                  norm_w, table, out):
    xs = nc.dram_tensor("xT_scratch", (B, P, 2, KD, T), F32, kind="Internal").ap()
    ks = nc.dram_tensor("kT_scratch", (B, P, NKV, T), F32, kind="Internal").ap()
    vs = nc.dram_tensor("v_scratch", (B, P, NT, NK), F32, kind="Internal").ap()
    ss = nc.dram_tensor("sel_scratch", (B, NT, P, T), F32, kind="Internal").ap()

    with ExitStack() as ctx:
        def sb(name, shape, dt=F32):
            return ctx.enter_context(nc.sbuf_tensor(name, shape, dt))

        def sem(name):
            return ctx.enter_context(nc.semaphore(name))

        wqh = sb("wq_hi", [P, KD, NQ], F32R)
        wql = sb("wq_lo", [P, KD, NQ], F32R)
        xh = sb("xT_hi", [P, KD, T], F32R)
        xl = sb("xT_lo", [P, KD, T], F32R)
        kT = sb("kT", [P, NKV, T])
        V = sb("V", [P, NT, NK])
        gw = sb("gate_w", [P, HEADS, HD])
        wo = sb("w_o_half", [P, HEADS, DIM])
        qT = sb("qT", [P, 2, GROUP, T])
        D = sb("distance", [P, CW])
        nselT = sb("not_selected_T", [P, NT, T], BF16)
        nsel = sb("not_selected", [P, T], BF16)
        work = sb("sel_work", [P, 2, T])
        th = sb("softcapped", [P, CW])
        pr = sb("probs", [P, 2, CW])
        rs = sb("prob_sums", [P, T - P])
        sq = sb("squares", [P, NK + HD])
        t1 = sb("rot_cos", [P, NK + HD])
        t2 = sb("rot_sin", [P, NK + HD])
        qn = sb("rotated", [P, NK + HD])
        yn = sb("y_normed", [P, T])
        rb = sb("recip_den_rows", [P, T])
        gt = sb("gate_tanh", [P, T])
        yg = sb("y_gated", [P, T])
        r1 = sb("residual", [P, B * NT, DIM])
        con = sb("constants", [P, C_END])
        rope = sb("rope_tables", [P, 4, NT, HD])
        brow = sb("bias_rows", [64, NQ + 2 * DIM], F32R)
        onesr = sb("ones_r", [64, P], F32R)
        fw = sb("small_weights_r", [P, 4096], F32R)
        identb = sb("ident_bf16", [P, P], BF16)
        gb = sb("gate_bias_half", [P, HEADS])
        bd = sb("b_down", [P, 1])
        b1s = sb("b1", [P, NF])
        ssq = sb("sum_squares", [P, 8])
        msq = sb("mean_squares", [P, 8])
        rstd = sb("rstd", [P, 8])
        mhalf = sb("minus_half", [P, 8])
        ones1 = sb("ones_col", [P, 2])
        den4 = sb("recip_den", [P, NT])
        top8 = sb("top8", [P, 8])
        stats = sb("bn_stats", [P, NT, 6])
        mv = sb("mean_var", [P, NT, 2])
        wsum = sb("w_abs_sums", [P, 2])
        wscale = sb("w_half_scale", [P, 4])
        onesq = sb("ones_square", [P, P])

        ident = con[:, C_EYE:C_OFFDIAG]
        stage = r1[:, :, :].rearrange("p a d -> p (a d)")
        prf = pr[:, :, :].rearrange("p a c -> p (a c)")
        up_in = prf[:, 0:2 * NK]
        down_in = prf[:, 2 * NK:2 * NK + KD * P].rearrange("p (k n) -> p k n", k=KD)
        xin = prf[:, CW:CW + NT * DIM].rearrange("p (j d) -> p j d", j=NT)
        braw = wo[0:1, :, :].rearrange("p a d -> p (a d)")
        wA, wB = fw[:, 0:2 * NK], fw[:, 2 * NK:4 * NK]
        latA, latB = fw[:, 4 * NK:4 * NK + T], fw[:, 4 * NK + T:4 * NK + 2 * T]
        wdr = fw[:, 4 * NK + 2 * T:4 * NK + 2 * T + 2 * KD * P].rearrange("p (a k n) -> p a k n", a=2, k=KD)
        latf = yn[:, :]
        nw = gt[:, :].rearrange("p (w d) -> p w d", w=4)
        q0T = yg[:, :]
        qT_flat = qT[:, :, :, :].rearrange("p a g t -> p (a g t)")
        w1f, w2f = qT_flat[:, 0:KD * DFF], qT_flat[:, KD * DFF:]
        w1q = fw[:, 0:KD * DFF].rearrange("p (k f) -> p k f", k=KD)
        w2q = fw[:, KD * DFF:].rearrange("p (k n) -> p k n", k=NF)
        wscr = wo[:, 0:8, :].rearrange("p a d -> p (a d)")
        x1 = qT_flat[:, 0:NT * DIM].rearrange("p (j d) -> p j d", j=NT)
        hr = wqh[:, 0, :].rearrange("p (a c t) -> p a c t", a=2, c=2)
        gw_flat = gw[:, :, :].rearrange("p h e -> p (h e)")
        r2 = gw_flat[:, 0:NT * DIM].rearrange("p (j d) -> p j d", j=NT)
        ffn_y = gw_flat[:, NT * DIM:].rearrange("p (j d) -> p j d", j=NT)

        ps = ctx.enter_context(nc.psum_tensor("psum", [P, 8, 512], F32))
        sc_ps = ps[:, 0:3, :].rearrange("p a b -> p (a b)")
        z_ps, x_ps, y_ps = ps[:, 3, :], ps[:, 4, :], ps[:, 5, :]
        o_ps = ps[:, 6:8, :]

        w_in = sem("w_in")
        con_in = sem("con_in")
        small_in = sem("small_in")
        braw_in = sem("braw_in")
        wo_in = sem("wo_in")
        gw_in = sem("gw_in")
        r1_in = sem("r1_in")
        x_in = sem("x_in")
        wq_split = sem("wq_split")
        setup_act = sem("setup_act")
        setup_dve = sem("setup_dve")
        setup_pool = sem("setup_pool")
        tables_done = sem("tables_done")
        brow_done = sem("brow_done")
        xtr_done = sem("xtr_done")
        xhi_done = sem("xhi_done")
        xlo_done = sem("xlo_done")
        lat_mm = sem("lat_mm")
        latf_done = sem("latf_done")
        latB_done = sem("latB_done")
        latA_link = sem("latA_link")
        latA_done = sem("latA_done")
        k_mm = sem("k_mm")
        v_mm = sem("v_mm")
        q0_mm = sem("q0_mm")
        ksq_done = sem("ksq_done")
        kss_done = sem("kss_done")
        kt1_done = sem("kt1_done")
        kt2_done = sem("kt2_done")
        v_ev = sem("v_ev")
        krope_link = sem("krope_link")
        kn_done = sem("kn_done")
        ktr_done = sem("ktr_done")
        ktr_ev = sem("ktr_ev")
        s_mm = sem("s_mm")
        s_ev = sem("s_ev")
        xs_out = sem("xs_out")
        small_split = sem("small_split")
        ks_out = sem("ks_out")
        vs_out = sem("vs_out")
        qp_done = sem("qp_done")
        sq_done = sem("sq_done")
        ss_done = sem("ss_done")
        t1_done = sem("t1_done")
        t2_done = sem("t2_done")
        qn_done = sem("qn_done")
        rope_link = sem("rope_link")
        tr_done = sem("tr_done")
        qT_done = sem("qT_done")
        sc_done = sem("sc_done")
        th_done = sem("th_done")
        u_done = sem("u_done")
        p_done = sem("p_done")
        rs_done = sem("rs_done")
        rsum_link = sem("rsum_link")
        pv_done = sem("pv_done")
        den_done = sem("den_done")
        rden_done = sem("rden_done")
        rb_done = sem("rb_done")
        rbe_done = sem("rbe_done")
        yn_done = sem("yn_done")
        gate_done = sem("gate_done")
        gt_done = sem("gt_done")
        yg_done = sem("yg_done")
        wo_done = sem("wo_done")
        res_done = sem("res_done")
        topk_link = sem("topk_link")
        ns_done = sem("ns_done")
        mt_done = sem("mt_done")
        mc_done = sem("mc_done")
        D_done = sem("D_done")
        fw_in = sem("fw_in")
        fabs_done = sem("fabs_done")
        fsum_mm = sem("fsum_mm")
        fscale_link = sem("fscale_link")
        ternary_link = sem("ternary_link")
        ffnw_done = sem("ffnw_done")
        ln_link = sem("ln_link")
        st_done = sem("st_done")
        frstd_done = sem("frstd_done")
        fpool_link = sem("fpool_link")
        x1_done = sem("x1_done")
        fxt_done = sem("fxt_done")
        fxhi_done = sem("fxhi_done")
        fxlo_done = sem("fxlo_done")
        h_mm = sem("h_mm")
        h_done = sem("h_done")
        h2_done = sem("h2_done")
        hlo_done = sem("hlo_done")
        f2_mm = sem("f2_mm")
        r2_done = sem("r2_done")
        st2_done = sem("st2_done")
        frstd2_done = sem("frstd2_done")
        y_done = sem("y_done")
        y_out = sem("y_out")
        passed_dve = sem("passed_dve")
        passed_pool = sem("passed_pool")
        xT_in = [sem(f"xT_in{j}") for j in range(NT)]
        kT_in = [sem(f"kT_in{g}") for g in range(NKV)]
        v_in = [sem(f"v_in{g}") for g in range(NKV)]
        s_in = [sem(f"s_in{i}") for i in range(2)]
        s_out = [sem(f"s_out{i}") for i in range(2)]

        block = ctx.enter_context(nc.Block())

        def batches(eng, body, split_last):
            n = B - 1 if split_last else B
            body(0, False)
            with eng.Fori(1, n) as b:
                body(b, False)
            if split_last:
                body(B - 1, True)

        def heads_view(ap, h):
            return ap.rearrange("p (h d) -> p h d", h=h)

        def blocks_view(ap, h, c):
            return ap.rearrange("p (h a c i) -> p h a c i", h=h, a=2, c=2)[:, :, :, c, :]

        def table_blocks(which, j, c, h):
            v = rope[:, which, j, :].rearrange("p (a c i) -> p a c i", a=2, c=2)[:, :, c, :]
            return v.unsqueeze(1).broadcast_to([P, h, 2, 32])

        TOPK_AT = {0: (0, 0, 4), 1: (0, 4, 8), 2: (1, 0, 3), 3: (1, 3, 6), 4: (1, 6, 8), 5: (2, 0, 3),
                   6: (2, 3, 6), 7: (2, 6, 8), 8: (3, 0, 2), 9: (3, 2, 4), 10: (3, 4, 6), 11: (3, 6, 8)}
        TURN_AT = {2: 0, 5: 1, 8: 2, 12: 3}
        TOPK_LINKS = 2 * ROUNDS + 1

        @block.sync
        def _(sp):
            sp.dma_start(stage.rearrange("p (k n) -> p k n", k=KD),
                         w_q.rearrange("(k p) n -> p k n", p=P)).then_inc(w_in, 16)
            sp.dma_start(con[:], table).then_inc(con_in, 16)
            sp.dma_start(braw[:, 0:biases.shape[1]], biases).then_inc(braw_in, 16)
            sp.dma_start(up_in[0:LATENT, :], w_up).then_inc(small_in, 16)
            sp.dma_start(up_in[LATENT:P, :], w_up).then_inc(small_in, 16)
            sp.dma_start(down_in[:, :, 0:LATENT], w_down.rearrange("(k p) n -> p k n", p=P)).then_inc(small_in, 16)
            sp.dma_start(down_in[:, :, LATENT:P], w_down.rearrange("(k p) n -> p k n", p=P)).then_inc(small_in, 16)
            sp.dma_start(nw, norm_w.partition_broadcast(P)).then_inc(small_in, 16)
            sp.dma_start(gb[:], gate_b).then_inc(small_in, 16)
            sp.dma_start(bd[:], b_down).then_inc(small_in, 16)
            sp.dma_start(b1s[:], b1).then_inc(small_in, 16)
            sp.dma_start(gw[:], gate_w.rearrange("h d e -> d h e")).then_inc(gw_in, 16)

            def keys(b, last):
                sp.wait_ge(xtr_done, b * KD)
                sp.dma_start(xin, x[bass.ds(b, 1)].rearrange("a (j p) d -> p (a j) d", p=P)).then_inc(x_in, 16)
                sp.wait_ge(xlo_done, b * KD + KD)
                sp.dma_start(xs[bass.ds(b, 1), :, 0].rearrange("a p k t -> p (a k) t"), xh[:].bitcast(F32)).then_inc(xs_out, 16)
                sp.dma_start(xs[bass.ds(b, 1), :, 1].rearrange("a p k t -> p (a k) t"), xl[:].bitcast(F32)).then_inc(xs_out, 16)
                for j in range(NT):
                    sp.wait_ge(s_ev, b * NT + j + 1)
                    sp.dma_start(ss[bass.ds(b, 1), j, :, 0:P * (j + 1)].rearrange("a p t -> (a p) t"),
                                 work[:, j % 2, 0:P * (j + 1)]).then_inc(s_out[j % 2], 16)
                sp.wait_ge(v_ev, b * NT + NT)
                sp.dma_start(vs[bass.ds(b, 1)].rearrange("a p k n -> p (a k) n"), V[:]).then_inc(vs_out, 16)
                sp.wait_ge(ktr_ev, b * NT + NT)
                sp.dma_start(ks[bass.ds(b, 1)].rearrange("a p g t -> p (a g) t"), kT[:]).then_inc(ks_out, 16)

            batches(sp, keys, False)

            def load_x(b, j):
                sp.dma_start(xh[:, :, P * j:P * (j + 1)].bitcast(F32),
                             xs[bass.ds(b, 1), :, 0, :, P * j:P * (j + 1)].rearrange("a p k t -> p (a k) t")).then_inc(xT_in[j], 16)
                sp.dma_start(xl[:, :, P * j:P * (j + 1)].bitcast(F32),
                             xs[bass.ds(b, 1), :, 1, :, P * j:P * (j + 1)].rearrange("a p k t -> p (a k) t")).then_inc(xT_in[j], 16)

            def load_k(b, g):
                sp.dma_start(kT[:, g, :], ks[bass.ds(b, 1), :, g].rearrange("a p t -> (a p) t")).then_inc(kT_in[g], 16)

            def load_v(b, g):
                sp.dma_start(V[:, :, HD * g:HD * (g + 1)],
                             vs[bass.ds(b, 1), :, :, HD * g:HD * (g + 1)].rearrange("a p k n -> p (a k) n")).then_inc(v_in[g], 16)

            def load_s(b, qt):
                w = P * (qt + 1)
                sp.dma_start(work[:, qt % 2, 0:w],
                             ss[bass.ds(b, 1), qt, :, 0:w].rearrange("a p t -> (a p) t")).then_inc(s_in[qt % 2], 16)

            sp.wait_ge(xs_out, 32 * B)
            for i in range(2):
                sp.wait_ge(s_out[i], 16 * (NT // 2) * B)
            sp.wait_ge(vs_out, 16 * B)
            sp.wait_ge(ks_out, 16 * B)
            for j in range(NT):
                load_x(0, j)
            load_s(0, 0)
            load_s(0, 1)
            load_k(0, 0)
            load_v(0, 0)
            for g in range(1, NKV):
                load_k(0, g)
                load_v(0, g)
            sp.wait_ge(brow_done, 3)
            sp.dma_start(wo[:], w_o.rearrange("(h d) n -> d h n", d=HD)).then_inc(wo_in, 16)
            sp.wait_ge(wq_split, 1)
            sp.dma_start(r1[:], x.rearrange("b (j p) d -> p (b j) d", p=P)).then_inc(r1_in, 16)
            sp.wait_ge(ns_done, 1)
            load_s(0, 2)
            sp.wait_ge(ns_done, 2)
            load_s(0, 3)

            def heads(b, last):
                if last:
                    return
                n = b * STEPS
                sp.wait_ge(ns_done, b * NT + 3)
                load_s(b + 1, 0)
                sp.wait_ge(ns_done, b * NT + 4)
                load_s(b + 1, 1)
                sp.wait_ge(sc_done, n + 4)
                load_k(b + 1, 0)
                sp.wait_ge(ns_done, b * NT + NT + 1)
                load_s(b + 1, 2)
                sp.wait_ge(pv_done, n + 4)
                load_v(b + 1, 0)
                sp.wait_ge(ns_done, b * NT + NT + 2)
                load_s(b + 1, 3)
                for j in range(NT):
                    sp.wait_ge(qp_done, n + 12 + j + 1)
                    load_x(b + 1, j)
                    if j == 1:
                        sp.wait_ge(sc_done, n + 8)
                        load_k(b + 1, 1)
                        sp.wait_ge(pv_done, n + 8)
                        load_v(b + 1, 1)
                for g in range(2, NKV):
                    sp.wait_ge(sc_done, n + GROUP * (g + 1))
                    load_k(b + 1, g)
                    sp.wait_ge(pv_done, n + GROUP * (g + 1))
                    load_v(b + 1, g)

            batches(sp, heads, True)

            sp.wait_ge(qp_done, NTILES)
            sp.wait_ge(sc_done, NTILES)
            sp.dma_start(w1f.rearrange("p (k f) -> p k f", k=KD),
                         w1.rearrange("(k p) f -> p k f", p=P)).then_inc(fw_in, 16)
            sp.dma_start(w2f.rearrange("p (k n) -> p k n", k=NF),
                         w2.rearrange("(k p) n -> p k n", p=P)).then_inc(fw_in, 16)

            def ffn(b, last):
                sp.wait_ge(y_done, b * NT + NT)
                sp.dma_start(out[bass.ds(b, 1)].rearrange("a (j p) d -> p (a j) d", p=P),
                             ffn_y).then_inc(y_out, 16)

            batches(sp, ffn, False)
            sp.wait_ge(y_out, 16 * B)

        @block.tensor
        def _(pe):
            def mm(o, lhsT, rhs, start, stop):
                return pe.matmul(o, lhsT, rhs, start=start, stop=stop, skip_group_check=True)

            def project(o, cols, j, bias_cols):
                tok = slice(P * j, P * (j + 1))
                for k in range(KD):
                    mm(o, xh[:, k, tok], wqh[:, k, cols], k == 0, False)
                    mm(o, xl[:, k, tok], wqh[:, k, cols], False, False)
                    mm(o, xh[:, k, tok], wql[:, k, cols], False, False)
                return mm(o, onesr[:], brow[:, bias_cols], False, True)

            pe.wait_ge(con_in, 16)
            pe.wait_ge(setup_dve, 1)
            pe.wait_ge(brow_done, 3)
            pe.wait_ge(setup_act, 5)
            pe.wait_ge(wq_split, 1)
            pe.wait_ge(small_split, 1)

            def keys(b, last):
                pe.wait_ge(x_in, b * 16 + 16)
                pe.wait_ge(xlo_done, b * KD)
                for k in range(KD):
                    for j in range(NT):
                        m = pe.transpose(ps[:, k, P * j:P * (j + 1)], xin[:, j, P * k:P * (k + 1)], ident)
                    m.then_inc(xtr_done, 1)
                pe.wait_ge(xlo_done, b * KD + KD)
                pe.wait_ge(s_ev, b * NT)
                for k in range(KD):
                    mm(ps[:, 2, :], wdr[:, 0, k, :], xh[:, k, :], k == 0, False)
                    mm(ps[:, 2, :], wdr[:, 1, k, :], xh[:, k, :], False, False)
                    m = mm(ps[:, 2, :], wdr[:, 0, k, :], xl[:, k, :], False, k == KD - 1)
                m.then_inc(lat_mm, 1)
                pe.wait_ge(latA_done, b + 1)
                pe.wait_ge(latB_done, b + 1)
                for j in range(NT + 1):
                    i = b * NT + j
                    tok = slice(P * j, P * (j + 1))
                    if j < NT:
                        pe.wait_ge(kt2_done, i)
                        mm(ps[:, 3, :], latA[:, tok], wA[:, 0:NK], True, False)
                        mm(ps[:, 3, :], latB[:, tok], wB[:, 0:NK], False, True).then_inc(k_mm, 1)
                        project(ps[:, 5, 0:HD], slice(0, HD), j, slice(0, HD)).then_inc(q0_mm, 1)
                        pe.wait_ge(v_ev, i)
                        mm(ps[:, 4, :], latA[:, tok], wA[:, NK:2 * NK], True, False)
                        mm(ps[:, 4, :], latB[:, tok], wB[:, NK:2 * NK], False, True).then_inc(v_mm, 1)
                    if j >= 1:
                        p = slice(P * (j - 1), P * j)
                        pe.wait_ge(kn_done, i)
                        pe.wait_ge(ktr_ev, i - 1)
                        for g in range(NKV):
                            pe.transpose(ps[:, 6, P * g:P * (g + 1)], qn[:, HD * g:HD * (g + 1)], ident)
                        pe.transpose(ps[:, 7, 0:P], qn[:, NK:NK + HD], ident).then_inc(ktr_done, 1)
                        pe.wait_ge(ktr_ev, i)
                        pe.wait_ge(s_ev, i - 1)
                        pe.wait_ge(latf_done, b + 1)
                        mm(ps[:, 2, 0:P * j], q0T[0:SEL_DIM, p], kT[0:SEL_DIM, 0, 0:P * j], True, True).then_inc(s_mm, 1)

            batches(pe, keys, False)

            def scores(b, s):
                g, n = s // GROUP, b * STEPS + s
                pe.wait_ge(qT_done, b * STEPS + GROUP * (g + 1))
                pe.wait_ge(kT_in[g], b * 16 + 16)
                pe.wait_ge(th_done, n)
                for kt in range(NT):
                    m = mm(sc_ps[:, OFF[kt]:OFF[kt] + PIECE[kt]], kT[:, g, P * kt:P * (kt + 1)],
                           qT[:, g % 2, s % GROUP, P * kt:T], True, True)
                m.then_inc(sc_done, 1)

            def values(b, s):
                g, n = s // GROUP, b * STEPS + s
                pe.wait_ge(p_done, n + 1)
                pe.wait_ge(v_in[g], b * 16 + 16)
                pe.wait_ge(yn_done, n)
                for kt in range(NT):
                    m = mm(y_ps[:, P * kt:T], V[:, kt, HD * g:HD * (g + 1)],
                           pr[:, s % 2, OFF[kt]:OFF[kt] + PIECE[kt]], kt == 0, kt == NT - 1)
                m.then_inc(pv_done, 1)

            def denominators(b, s, last):
                n = b * STEPS + s
                pe.wait_ge(rs_done, n + 1)
                pe.wait_ge(qT_done, n + LEAD - 1 if not last or s + LEAD - 1 <= STEPS else NTILES)
                if s in TURN_AT and not last:
                    pe.wait_ge(mc_done, b * NT + NT + TURN_AT[s] + 1)
                for qt in range(NT):
                    lhsT = pr[:, s % 2, 0:P] if qt == 0 else rs[:, P * (qt - 1):P * qt]
                    m = mm(x_ps[:, qt:qt + 1], lhsT, ones1[:, 0:1], True, True)
                m.then_inc(den_done, 1)

            def query(b, s, m_):
                j, u = s % NT, s // NT
                pe.wait_ge(xT_in[j], b * 32 + 32)
                if not (isinstance(m_, int) and m_ < LEAD):
                    pe.wait_ge(gt_done, m_ - LEAD)
                pe.wait_ge(t2_done, m_)
                cols = slice(GROUP * HD * u, GROUP * HD * (u + 1))
                project(z_ps, cols, j, cols).then_inc(qp_done, 1)

            def rows_of_reciprocals(b, s):
                n = b * STEPS + s
                pe.wait_ge(rden_done, n + 1)
                for qt in range(NT):
                    m = pe.transpose(x_ps[:, P * qt:P * (qt + 1)], den4[:, qt:qt + 1].broadcast_to([P, P]), ident)
                m.then_inc(rb_done, 1)

            def output(b, s):
                n = b * STEPS + s
                if s == 0:
                    pe.wait_ge(res_done, b)
                    for a in range(2):
                        mm(o_ps[:, a, :].rearrange("p (c d) -> p c d", c=2), onesr[:],
                           brow[:, NQ:NQ + DIM].unsqueeze(1).broadcast_to([64, 2, DIM]), True, False)
                pe.wait_ge(yg_done, n + 1)
                for j in range(NT):
                    m = mm(o_ps[:, j // 2, DIM * (j % 2):DIM * (j % 2 + 1)], yg[:, P * j:P * (j + 1)], wo[:, s, :],
                           False, s == STEPS - 1)
                m.then_inc(wo_done, 1)

            def turn_queries(m_, after):
                pe.wait_ge(qn_done, m_ + 1)
                pe.wait_ge(qT_done, m_)
                pe.wait_ge(rbe_done, after)
                for h in range(GROUP):
                    m = pe.transpose(x_ps[:, P * h:P * (h + 1)], qn[:, HD * h:HD * (h + 1)], ident)
                m.then_inc(tr_done, 1)

            def gate(b, s, last):
                n = b * STEPS + s
                pe.wait_ge(yn_done, n + 1)
                pe.wait_ge(t2_done, n + LEAD + 1 if not last or s + LEAD < STEPS else NTILES)
                mm(z_ps, gw[:, s, :], yn[:], True, True).then_inc(gate_done, 1)

            def turn_mask(tile, qt, evacs):
                pe.wait_ge(ns_done, tile + 1)
                pe.wait_ge(qT_done, evacs)
                xb = x_ps.bitcast(BF16)
                for kt in range(qt + 1):
                    m = pe.transpose(xb[:, P * kt:P * (kt + 1)], nsel[:, P * kt:P * (kt + 1)], identb[:])
                m.then_inc(mt_done, 1)

            for m_ in range(LEAD):
                query(0, m_, m_)
                if m_ >= 1:
                    pe.wait_ge(mc_done, min(m_ - 1, NT))
                    turn_queries(m_ - 1, 0)
                    if m_ - 1 < NT:
                        turn_mask(m_ - 1, m_ - 1, m_)
            scores(0, 0)
            pe.wait_ge(gw_in, 16)
            pe.wait_ge(setup_pool, 2)

            def heads(b, last):
                for s in range(STEPS):
                    n = b * STEPS + s
                    if s + 1 < STEPS:
                        scores(b, s + 1)
                    elif not last:
                        scores(b + 1, 0)
                    if s in TURN_AT and not last:
                        turn_mask(b * NT + NT + TURN_AT[s], TURN_AT[s], n + LEAD - 1)
                    values(b, s)
                    denominators(b, s, last)
                    if s + LEAD < STEPS:
                        query(b, s + LEAD, n + LEAD)
                    elif not last:
                        query(b + 1, s + LEAD - STEPS, n + LEAD)
                    rows_of_reciprocals(b, s)
                    if s >= 1:
                        output(b, s - 1)
                    if s + LEAD - 1 < STEPS or not last:
                        turn_queries(n + LEAD - 1, n + 1)
                    gate(b, s, last)
                output(b, STEPS - 1)

            batches(pe, heads, True)

            pe.wait_ge(fabs_done, 2)
            mm(ps[:, 0, 0:2], onesq[:], wsum[:], True, True).then_inc(fsum_mm, 1)
            pe.wait_ge(ffnw_done, 2)

            def ffn(b, last):
                pe.wait_ge(x1_done, b * NT + NT)
                pe.wait_ge(fxlo_done, b * KD)
                for k in range(KD):
                    for j in range(NT):
                        m = pe.transpose(ps[:, k, P * j:P * (j + 1)], x1[:, j, P * k:P * (k + 1)], ident)
                    m.then_inc(fxt_done, 1)
                pe.wait_ge(fxlo_done, b * KD + KD)
                pe.wait_ge(r2_done, b * 2)
                for f in range(NF + 1):
                    i = b * NF + f
                    if f < NF:
                        pe.wait_ge(h2_done, i - 1 if f else i)
                        for k in range(KD):
                            mm(ps[:, 2 + f % 2, :], w1q[:, k, P * f:P * (f + 1)], xh[:, k, :], k == 0, False)
                            m = mm(ps[:, 2 + f % 2, :], w1q[:, k, P * f:P * (f + 1)], xl[:, k, :], False, k == KD - 1)
                        m.then_inc(h_mm, 1)
                    if f == 0:
                        for a in range(2):
                            mm(ps[:, 4 + a, :].rearrange("p (c d) -> p c d", c=2), onesr[:],
                               brow[:, NQ + DIM:NQ + 2 * DIM].unsqueeze(1).broadcast_to([64, 2, DIM]), True, False)
                    else:
                        pe.wait_ge(hlo_done, i)
                        for j in range(NT):
                            for part in range(2):
                                m = mm(ps[:, 4 + j // 2, DIM * (j % 2):DIM * (j % 2 + 1)],
                                       hr[:, (f - 1) % 2, part, P * j:P * (j + 1)], w2q[:, f - 1, :], False, f == NF)
                        m.then_inc(f2_mm, 1)

            batches(pe, ffn, False)

        @block.scalar
        def _(act):
            act.wait_ge(w_in, 16)
            for k in range(KD):
                nc.scalar.activation(wqh[:, k, :], stage[:, NQ * k:NQ * (k + 1)], ACT.Copy).then_inc(setup_act, 1)
            act.wait_ge(small_in, 16 * 8)
            nc.scalar.activation(wA, up_in, ACT.Copy).then_inc(setup_act, 1)
            nc.scalar.activation(wdr[:, 0], down_in, ACT.Copy).then_inc(setup_act, 1)
            nc.scalar.mul(gb[:], gb[:], 0.5).then_inc(setup_act, 1)

            def keys(b, last):
                act.wait_ge(xs_out, b * 32)
                act.wait_ge(q0_mm, b * NT)
                for k in range(KD):
                    act.wait_ge(xtr_done, b * KD + k + 1)
                    nc.scalar.activation(xh[:, k, :], ps[:, k, :], ACT.Copy).then_inc(xhi_done, 1)
                act.wait_ge(lat_mm, b + 1)
                act.wait_ge(latA_done, b)
                act.wait_ge(latB_done, b)
                nc.scalar.activation(latf, ps[:, 2, :], ACT.Identity, bias=bd[:]).then_inc(latf_done, 1)
                act.wait_ge(latf_done, b + 1)
                act.wait_ge(v_mm, b * NT)
                nc.scalar.activation(latB[0:LATENT, :], latf[0:LATENT, :], ACT.Copy).then_inc(latB_done, 1)
                for j in range(NT + 1):
                    i = b * NT + j
                    if j < NT:
                        act.wait_ge(k_mm, i + 1)
                        act.wait_ge(kss_done, i)
                        nc.scalar.activation(sq[:, 0:NK], ps[:, 3, :], ACT.Square)
                        act.wait_ge(q0_mm, i + 1)
                        nc.scalar.activation(sq[:, NK:], ps[:, 5, 0:HD], ACT.Square).then_inc(ksq_done, 1)
                        act.wait_ge(v_mm, i + 1)
                        act.wait_ge(vs_out, b * 16)
                        nc.scalar.activation(V[:, j, :], ps[:, 4, :], ACT.Copy).then_inc(v_ev, 1)
                    if j >= 1:
                        act.wait_ge(ktr_done, i)
                        act.wait_ge(ks_out, b * 16)
                        act.wait_ge(s_mm, i - 1)
                        tok = slice(P * (j - 1), P * j)
                        nc.scalar.activation(kT[:, :, tok], heads_view(ps[:, 6, :], NKV), ACT.Copy)
                        nc.scalar.activation(q0T[:, tok], ps[:, 7, 0:P], ACT.Copy).then_inc(ktr_ev, 1)

            batches(act, keys, False)

            def softcap(b, s):
                n = b * STEPS + s
                act.wait_ge(sc_done, n + 1)
                act.wait_ge(p_done, n)
                nc.scalar.activation(th[:], sc_ps[:, 0:CW], ACT.Tanh,
                                     scale=1.0 / (SOFTCAP * HD ** 0.5)).then_inc(th_done, 1)

            def exps(b, s):
                n = b * STEPS + s
                act.wait_ge(u_done, n + 1)
                if not (isinstance(n, int) and n == 0):
                    act.wait_ge(pv_done, n - 1)
                    act.wait_ge(den_done, n - 1)
                    act.wait_ge(rs_done, n - 1)
                nc.scalar.activation(pr[:, s % 2, :], th[:], ACT.Exp, scale=SOFTCAP).then_inc(p_done, 1)

            def squares(m_):
                act.wait_ge(qp_done, m_ + 1)
                act.wait_ge(ss_done, m_)
                nc.scalar.activation(sq[:, 0:NK], z_ps, ACT.Square).then_inc(sq_done, 1)

            def store_rows(b, s):
                n = b * STEPS + s
                act.wait_ge(rb_done, n + 1)
                act.wait_ge(yn_done, n)
                nc.scalar.activation(rb[:], x_ps, ACT.Copy).then_inc(rbe_done, 1)

            def store_queries(m_, u, j, scores_before):
                act.wait_ge(tr_done, m_ + 1)
                act.wait_ge(sc_done, scores_before)
                nc.scalar.activation(qT[:, u % 2, :, P * j:P * (j + 1)], heads_view(x_ps, GROUP),
                                     ACT.Copy).then_inc(qT_done, 1)

            def gate_tanh(b, s):
                n = b * STEPS + s
                act.wait_ge(gate_done, n + 1)
                act.wait_ge(yg_done, n)
                nc.scalar.activation(gt[:], z_ps, ACT.Tanh, scale=0.5, bias=gb[:, s:s + 1]).then_inc(gt_done, 1)

            act.wait_ge(setup_act, 5)
            for m_ in range(LEAD):
                squares(m_)
                if m_ >= 1:
                    store_queries(m_ - 1, (m_ - 1) // NT, (m_ - 1) % NT, 0)
            softcap(0, 0)
            exps(0, 0)

            def heads(b, last):
                for s in range(STEPS):
                    n = b * STEPS + s
                    if s + 1 < STEPS:
                        softcap(b, s + 1)
                        exps(b, s + 1)
                    elif not last:
                        softcap(b + 1, 0)
                        exps(b + 1, 0)
                    if s + LEAD < STEPS or not last:
                        squares(n + LEAD)
                    store_rows(b, s)
                    if s + LEAD - 1 < STEPS or not last:
                        m_ = s + LEAD - 1
                        store_queries(n + LEAD - 1, m_ // NT, m_ % NT, b * STEPS + NT * (m_ // NT) - NT)
                    gate_tanh(b, s)

            batches(act, heads, True)

            def ffn(b, last):
                for k in range(KD):
                    act.wait_ge(fxt_done, b * KD + k + 1)
                    act.wait_ge(h_mm, b * NF)
                    nc.scalar.activation(xh[:, k, :], ps[:, k, :], ACT.Copy).then_inc(fxhi_done, 1)
                for f in range(NF):
                    i = b * NF + f
                    act.wait_ge(h_mm, i + 1)
                    act.wait_ge(hlo_done, i - 1 if f else i)
                    nc.scalar.activation(pr[:, f % 2, 0:T], ps[:, 2 + f % 2, :], ACT.Gelu, bias=b1s[:, f:f + 1]).then_inc(h_done, 1)
                    act.wait_ge(f2_mm, i - 1 if f else i)
                    nc.scalar.activation(hr[:, f % 2, 0, :], ps[:, 2 + f % 2, :], ACT.Gelu, bias=b1s[:, f:f + 1]).then_inc(h2_done, 1)

            batches(act, ffn, False)

        @block.vector
        def _(dve):
            nc.vector.memset(brow[:].bitcast(F32), 0.0).then_inc(brow_done, 1)
            nc.vector.memset(onesr[:].bitcast(F32), 1.0)
            nc.vector.memset(ones1[:], 1.0)
            nc.vector.memset(onesq[:], 1.0)
            nc.vector.memset(latB[LATENT:P, :].bitcast(F32), 1.0)
            nc.vector.memset(wB[LATENT:P, :].bitcast(F32), 0.0)
            dve.wait_ge(con_in, 16)
            nc.vector.tensor_copy(identb[:], ident).then_inc(setup_dve, 1)
            NB = NQ + 2 * DIM
            dve.wait_ge(braw_in, 16)
            dve.wait_ge(brow_done, 1)
            dve.wait_ge(setup_dve, 1)
            nc.vector.tensor_copy(brow[0:1, :], braw[:, 0:NB])
            nc.vector.tensor_copy(wB[64:65, :], braw[:, NB:NB + 2 * NK]).then_inc(brow_done, 1)
            dve.wait_ge(brow_done, 2)
            nc.vector.tensor_tensor(brow[32:33, :], braw[:, 0:NB], brow[0:1, :].bitcast(F32), ALU.subtract)
            nc.vector.tensor_copy(th[0:1, 0:2 * NK], wB[64:65, :].bitcast(F32)).then_inc(setup_dve, 1)
            dve.wait_ge(setup_dve, 2)
            nc.vector.tensor_tensor(wB[96:97, :], braw[:, NB:NB + 2 * NK], th[0:1, 0:2 * NK],
                                    ALU.subtract).then_inc(brow_done, 1)
            dve.wait_ge(setup_act, KD)
            nc.vector.tensor_tensor(wql[:, :, :].rearrange("p k n -> p (k n)"), stage,
                                    wqh[:, :, :].rearrange("p k n -> p (k n)").bitcast(F32), ALU.subtract).then_inc(wq_split, 1)
            dve.wait_ge(setup_act, KD + 2)
            nc.vector.tensor_tensor(wB[0:LATENT, :], up_in[0:LATENT, :], wA[0:LATENT, :].bitcast(F32), ALU.subtract)
            nc.vector.tensor_tensor(wdr[:, 1], down_in, wdr[:, 0].bitcast(F32), ALU.subtract).then_inc(small_split, 1)
            dve.wait_ge(small_in, 16 * 8)
            for w in range(4):
                c0 = C_COS if w % 2 == 0 else C_SIN
                m = nc.vector.tensor_tensor(rope[:, w], con[:, c0:c0 + NT * P].rearrange("p (j d) -> p j d", j=NT),
                                            nw[:, w, :].unsqueeze(1).broadcast_to([P, NT, HD]), ALU.mult)
            m.then_inc(tables_done, 1)
            dve.wait_ge(tables_done, 1)

            def rotate(dst0, src, h, which, j, first_sem=None):
                w = h * HD
                m = nc.vector.tensor_tensor(heads_view(t1[:, dst0:dst0 + w], h), heads_view(src, h),
                                            rope[:, which, j, :].unsqueeze(1).broadcast_to([P, h, HD]), ALU.mult)
                if first_sem:
                    m.then_inc(first_sem, 1)

            def partners(dst0, src, h, which, j, last_sem):
                w = h * HD
                for c in range(2):
                    m = nc.vector.tensor_tensor(blocks_view(t2[:, dst0:dst0 + w], h, c), blocks_view(src, h, 1 - c),
                                                table_blocks(which + 1, j, c, h), ALU.mult)
                if last_sem:
                    m.then_inc(last_sem, 1)

            def keys(b, last):
                for k in range(KD):
                    dve.wait_ge(xhi_done, b * KD + k + 1)
                    dve.wait_ge(xs_out, b * 32)
                    nc.vector.tensor_tensor(xl[:, k, :], ps[:, k, :], xh[:, k, :].bitcast(F32), ALU.subtract).then_inc(xlo_done, 1)
                dve.wait_ge(latf_done, b + 1)
                dve.wait_ge(v_mm, b * NT)
                nc.vector.tensor_copy(latA, latf).then_inc(latA_link, 1)
                dve.wait_ge(latA_link, b + 1)
                nc.vector.tensor_tensor(latA[LATENT:P, :], latf[LATENT:P, :], latA[LATENT:P, :].bitcast(F32),
                                        ALU.subtract).then_inc(latA_done, 1)
                for j in range(NT + 1):
                    i = b * NT + j
                    if j < NT:
                        dve.wait_ge(ksq_done, i + 1)
                        dve.wait_ge(kn_done, i)
                        rotate(0, ps[:, 3, :], NKV, 2, j)
                        rotate(NK, ps[:, 5, 0:HD], 1, 0, j)
                        partners(0, ps[:, 3, :], NKV, 2, j, None)
                        partners(NK, ps[:, 5, 0:HD], 1, 0, j, kt2_done)
                        nc.vector.tensor_reduce(ssq[:, 0:NKV + 1], heads_view(sq[:], NKV + 1), AX_X, ALU.add).then_inc(kss_done, 1)
                    if j >= 1:
                        dve.wait_ge(s_mm, i)
                        dve.wait_ge(s_out[(j - 1) % 2], b * 32 + 16 * ((j - 1) // 2))
                        w = P * (j - 1)
                        if w:
                            nc.vector.tensor_copy(work[:, (j - 1) % 2, 0:w], ps[:, 2, 0:w])
                        nc.vector.tensor_tensor(work[:, (j - 1) % 2, w:w + P], ps[:, 2, w:w + P],
                                                con[:, C_CAUSAL:C_EYE], ALU.add).then_inc(s_ev, 1)

            batches(dve, keys, False)

            def topk(tb, qt, first, end):
                w = P * (qt + 1)
                base = (tb * NT + qt) * TOPK_LINKS
                if first == 0:
                    dve.wait_ge(s_in[qt % 2], tb * 32 + 16 * (qt // 2) + 16)
                for r in range(first, end):
                    dve.wait_ge(topk_link, base + 2 * r)
                    dve.sem_inc(passed_dve, 1)
                    nc.vector.max(top8[:], work[:, qt % 2, 0:w]).then_inc(topk_link, 1)
                    dve.wait_ge(topk_link, base + 2 * r + 1)
                    dve.sem_inc(passed_dve, 1)
                    nc.vector.match_replace(work[:, qt % 2, 0:w], top8[:], work[:, qt % 2, 0:w], TAKEN).then_inc(topk_link, 1)
                if end == ROUNDS:
                    dve.wait_ge(topk_link, base + 2 * ROUNDS)
                    dve.wait_ge(mt_done, tb * NT + qt)
                    nc.vector.tensor_scalar(nsel[:, 0:w], work[:, qt % 2, 0:w], 0.5 * TAKEN, None, ALU.is_gt).then_inc(topk_link, 1)
                    dve.wait_ge(topk_link, base + TOPK_LINKS)
                    nc.vector.tensor_tensor(nsel[:, w - P:w], nsel[:, w - P:w], con[:, C_OFFDIAG:C_END],
                                            ALU.mult).then_inc(ns_done, 1)

            def store_mask(tb, qt):
                dve.wait_ge(mt_done, tb * NT + qt + 1)
                nc.vector.tensor_copy(nselT[:, 0:qt + 1, P * qt:P * (qt + 1)],
                                      x_ps.bitcast(BF16)[:, 0:P * (qt + 1)].rearrange("p (k q) -> p k q", q=P)).then_inc(mc_done, 1)

            def distances(tb, u_before):
                dve.wait_ge(mc_done, tb * NT + NT)
                dve.wait_ge(u_done, u_before)
                for kt in range(NT):
                    o = slice(OFF[kt], OFF[kt] + PIECE[kt])
                    m = nc.vector.scalar_tensor_tensor(D[:, o], nselT[:, kt, P * kt:T], BIG,
                                                       con[:, C_DIST + OFF[kt]:C_DIST + OFF[kt] + PIECE[kt]], ALU.mult, ALU.add)
                m.then_inc(D_done, 1)
                dve.wait_ge(D_done, tb + 1)

            def biased(b, s):
                n = b * STEPS + s
                dve.wait_ge(th_done, n + 1)
                nc.vector.scalar_tensor_tensor(th[:], D[:], -slope(s) / SOFTCAP, th[:], ALU.mult, ALU.add).then_inc(u_done, 1)

            def rotate_cos(m_, j):
                dve.wait_ge(sq_done, m_ + 1)
                dve.wait_ge(qn_done, m_)
                rotate(0, z_ps, GROUP, 0, j, t1_done)

            def rotate_sin(m_, j):
                partners(0, z_ps, GROUP, 0, j, t2_done)
                dve.wait_ge(rope_link, 3 * m_)
                nc.vector.tensor_reduce(ssq[:, 0:GROUP], heads_view(sq[:, 0:NK], GROUP), AX_X, ALU.add).then_inc(ss_done, 1)

            def reciprocals(b, s):
                n = b * STEPS + s
                dve.wait_ge(den_done, n + 1)
                dve.wait_ge(rb_done, n)
                nc.vector.reciprocal(den4[:], x_ps[:, 0:NT]).then_inc(rden_done, 1)

            def normalise(b, s):
                n = b * STEPS + s
                dve.wait_ge(rbe_done, n + 1)
                dve.wait_ge(pv_done, n + 1)
                dve.wait_ge(gate_done, n)
                dve.wait_ge(yg_done, n)
                nc.vector.tensor_tensor(yn[:], y_ps, rb[:], ALU.mult).then_inc(yn_done, 1)

            def gated(b, s):
                n = b * STEPS + s
                dve.wait_ge(gt_done, n + 1)
                dve.wait_ge(yn_done, n + 1)
                dve.wait_ge(wo_done, n)
                nc.vector.scalar_tensor_tensor(yg[:], gt[:], 1.0, yn[:], ALU.add, ALU.mult).then_inc(yg_done, 1)

            for m_ in range(LEAD):
                rotate_cos(m_, m_ % NT)
                rotate_sin(m_, m_ % NT)
                if 1 <= m_ <= NT:
                    store_mask(0, m_ - 1)
                if m_ < NT:
                    topk(0, m_, 0, ROUNDS)
            distances(0, 0)
            biased(0, 0)

            def heads(b, last):
                for s in range(STEPS):
                    n = b * STEPS + s
                    if s >= 1:
                        gated(b, s - 1)
                    if not last:
                        if s in TURN_AT:
                            store_mask(b + 1, TURN_AT[s])
                        if s in TOPK_AT:
                            topk(b + 1, *TOPK_AT[s])
                        if s == STEPS - 1:
                            distances(b + 1, n + 1)
                    if s + 1 < STEPS:
                        biased(b, s + 1)
                    elif not last:
                        biased(b + 1, 0)
                    reciprocals(b, s)
                    more = s + LEAD < STEPS or not last
                    if more:
                        rotate_cos(n + LEAD, (s + LEAD) % NT)
                    normalise(b, s)
                    if more:
                        rotate_sin(n + LEAD, (s + LEAD) % NT)
                gated(b, STEPS - 1)
                dve.wait_ge(wo_done, b * STEPS + STEPS)
                dve.wait_ge(r1_in, 16)
                for a in range(2):
                    r = r1[:, bass.ds(b * NT + 2 * a, 2), :] if not isinstance(b, int) else r1[:, NT * b + 2 * a:NT * b + 2 * a + 2, :]
                    m = nc.vector.tensor_tensor(r, r, o_ps[:, a, :].rearrange("p (c d) -> p c d", c=2), ALU.add)
                m.then_inc(res_done, 1)

            batches(dve, heads, True)

            dve.wait_ge(fw_in, 32)
            dve.wait_ge(wo_done, NTILES)
            for i, w in enumerate((w1f, w2f)):
                nc.vector.scalar_tensor_tensor(wscr, w, -1.0, w, ALU.mult, ALU.max).then_inc(ternary_link, 1)
                dve.wait_ge(ternary_link, i + 1)
                nc.vector.tensor_reduce(wsum[:, i:i + 1], wscr, AX_X, ALU.add).then_inc(fabs_done, 1)
                dve.wait_ge(fabs_done, i + 1)
            dve.wait_ge(fsum_mm, 1)
            nc.vector.tensor_scalar(wscale[:, 0:2], ps[:, 0, 0:2], 1.0 / (DFF * DIM), QUANT_EPS, ALU.mult, ALU.max).then_inc(fscale_link, 1)
            dve.wait_ge(fscale_link, 1)
            nc.vector.tensor_scalar(wscale[:, 2:4], wscale[:, 0:2], -0.5, None, ALU.mult)
            nc.vector.tensor_scalar(wscale[:, 0:2], wscale[:, 0:2], 0.5, None, ALU.mult).then_inc(fscale_link, 1)
            dve.wait_ge(fscale_link, 2)
            for i, w in enumerate((w1f, w2f)):
                nc.vector.tensor_scalar(wscr, w, wscale[:, 2 + i:3 + i], None, ALU.is_lt).then_inc(ternary_link, 1)
                dve.wait_ge(ternary_link, 3 + i)
                nc.vector.scalar_tensor_tensor(fw[:, 2048 * i:2048 * (i + 1)], w, wscale[:, i:i + 1], wscr,
                                               ALU.is_gt, ALU.subtract).then_inc(ffnw_done, 1)
                dve.wait_ge(ffnw_done, i + 1)

            def normalised(dst, src, b, which, done, free, free_at):
                for j in range(NT):
                    m = nc.vector.bn_stats(stats[:, j, :], src(j))
                m.then_inc(ln_link, 1)
                dve.wait_ge(ln_link, b * 2 + which + 1)
                dve.wait_ge(fpool_link, b * 2 + which)
                dve.sem_inc(passed_dve, 1)
                for j in range(NT):
                    m = nc.vector.bn_aggr(mv[:, j, :], stats[:, j, :])
                m.then_inc(st_done, 1)
                dve.wait_ge(frstd_done, b * 2 + which + 1)
                dve.wait_ge(free, free_at)
                for j in range(NT):
                    nc.vector.tensor_scalar(dst[:, j, :], src(j), mv[:, j, 0:1], rstd[:, j:j + 1],
                                            ALU.subtract, ALU.mult).then_inc(done, 1)

            def ffn(b, last):
                normalised(x1, lambda j: r1[:, bass.ds(b * NT + j, 1), :].rearrange("p a d -> p (a d)"), b, 0,
                           x1_done, ffnw_done, 2)
                for k in range(KD):
                    dve.wait_ge(fxhi_done, b * KD + k + 1)
                    dve.wait_ge(h_mm, b * NF)
                    nc.vector.tensor_tensor(xl[:, k, :], ps[:, k, :], xh[:, k, :].bitcast(F32), ALU.subtract).then_inc(fxlo_done, 1)
                for f in range(NF):
                    i = b * NF + f
                    dve.wait_ge(h_done, i + 1)
                    dve.wait_ge(h2_done, i + 1)
                    dve.wait_ge(f2_mm, i - 1 if f else i)
                    nc.vector.tensor_tensor(hr[:, f % 2, 1, :], pr[:, f % 2, 0:T], hr[:, f % 2, 0, :].bitcast(F32),
                                            ALU.subtract).then_inc(hlo_done, 1)
                dve.wait_ge(f2_mm, b * NF + NF)
                for a in range(2):
                    nc.vector.tensor_tensor(r2[:, 2 * a:2 * a + 2, :], ps[:, 4 + a, :].rearrange("p (c d) -> p c d", c=2),
                                            x1[:, 2 * a:2 * a + 2, :], ALU.add).then_inc(r2_done, 1)
                dve.wait_ge(r2_done, b * 2 + 2)
                normalised(ffn_y, lambda j: r2[:, j, :], b, 1, y_done, y_out, b * 16)

            batches(dve, ffn, False)

        @block.gpsimd
        def _(pool):
            nc.gpsimd.memset(mhalf[:], -0.5).then_inc(setup_pool, 1)
            pool.wait_ge(setup_pool, 1)

            def rope_tile(m_, h, link, start, ready, done, free, free_at):
                pool.wait_ge(start, m_ + 1)
                pool.wait_ge(done, m_)
                pool.sem_inc(passed_pool, 1)
                nc.gpsimd.tensor_scalar(msq[:, 0:h], ssq[:, 0:h], 1.0 / HD, RMS_EPS, ALU.mult, ALU.add).then_inc(link, 1)
                pool.wait_ge(link, 3 * m_ + 1)
                nc.gpsimd.tensor_tensor(rstd[:, 0:h], msq[:, 0:h], mhalf[:, 0:h], ALU.pow).then_inc(link, 1)
                pool.wait_ge(ready, m_ + 1)
                pool.wait_ge(free, free_at)
                w = h * HD
                nc.gpsimd.tensor_tensor(qn[:, 0:w], t1[:, 0:w], t2[:, 0:w], ALU.add).then_inc(link, 1)
                pool.wait_ge(link, 3 * m_ + 3)
                nc.gpsimd.tensor_tensor(heads_view(qn[:, 0:w], h), heads_view(qn[:, 0:w], h),
                                        rstd[:, 0:h].unsqueeze(2).broadcast_to([P, h, HD]), ALU.mult).then_inc(done, 1)

            def keys(b, last):
                for j in range(NT):
                    i = b * NT + j
                    rope_tile(i, NKV + 1, krope_link, kss_done, kt2_done, kn_done, ktr_done, i)

            batches(pool, keys, False)

            def sums(b, s):
                n = b * STEPS + s
                pool.wait_ge(p_done, n + 1)
                pool.wait_ge(den_done, n)
                p = pr[:, s % 2, :]
                nc.gpsimd.tensor_tensor(rs[:, 0:PIECE[1]], p[:, P:T], p[:, OFF[1]:OFF[1] + PIECE[1]], ALU.add).then_inc(rsum_link, 1)
                pool.wait_ge(rsum_link, 2 * n + 1)
                nc.gpsimd.tensor_tensor(rs[:, P:PIECE[1]], rs[:, P:PIECE[1]], p[:, OFF[2]:OFF[2] + PIECE[2]], ALU.add).then_inc(rsum_link, 1)
                pool.wait_ge(rsum_link, 2 * n + 2)
                nc.gpsimd.tensor_tensor(rs[:, 2 * P:PIECE[1]], rs[:, 2 * P:PIECE[1]], p[:, OFF[3]:OFF[3] + PIECE[3]], ALU.add).then_inc(rs_done, 1)

            def query_tile(m_):
                rope_tile(m_, GROUP, rope_link, ss_done, t2_done, qn_done, tr_done, m_)

            pool.wait_ge(kn_done, B * NT)
            for m_ in range(LEAD - 1):
                query_tile(m_)
            pool.wait_ge(wo_in, 16)
            nc.gpsimd.tensor_scalar(wo[:], wo[:], 0.5, None, ALU.mult).then_inc(setup_pool, 1)
            sums(0, 0)

            def heads(b, last):
                for s in range(STEPS):
                    if s + LEAD - 1 < STEPS or not last:
                        query_tile(b * STEPS + s + LEAD - 1)
                    if s + 1 < STEPS:
                        sums(b, s + 1)
                    elif not last:
                        sums(b + 1, 0)

            batches(pool, heads, True)

            def ffn(b, last):
                for which in range(2):
                    pool.wait_ge(st_done, b * 2 + which + 1)
                    pool.sem_inc(passed_pool, 1)
                    nc.gpsimd.tensor_scalar(msq[:, 0:NT], mv[:, :, 1], LN_EPS, None, ALU.add).then_inc(fpool_link, 1)
                    pool.wait_ge(fpool_link, b * 2 + which + 1)
                    nc.gpsimd.tensor_tensor(rstd[:, 0:NT], msq[:, 0:NT], mhalf[:, 0:NT], ALU.pow).then_inc(frstd_done, 1)

            batches(pool, ffn, False)


def kernel(**inputs):
    import concourse.bacc as bacc
    from concourse.bass_utils import run_bass_kernel_spmd

    a = {k[3:]: np.asarray(v) for k, v in inputs.items()}
    order, partner = np.array(ORDER), np.array(PARTNER)

    def by_head(v, n):
        h = v[..., :n * HD].reshape(*v.shape[:-1], n, HD)[..., order]
        return np.concatenate([h.reshape(*v.shape[:-1], n * HD), v[..., n * HD:]], -1)

    qn, kn = a["attn_qn_w"], a["attn_kn_w"]
    arrays = {
        "x": a["attn_x"],
        "w_q": by_head(a["attn_w_q"], HEADS),
        "w_down": a["attn_w_down"],
        "w_up": by_head(a["attn_w_up"], NKV),
        "w_o": a["attn_w_o"],
        "gate_w": a["attn_gate_w"],
        "w1": a["ffn_w1"].T,
        "w2": a["ffn_w2"].T,
        "biases": np.concatenate([by_head(a["attn_b_q"], HEADS), a["attn_b_o"], a["ffn_b2"],
                                  by_head(a["attn_b_up"], NKV)])[None],
        "gate_b": a["attn_gate_b"].T,
        "b_down": np.concatenate([a["attn_b_down"]] * 2)[:, None],
        "b1": a["ffn_b1"].reshape(NF, P).T,
        "norm_w": np.stack([qn[order], qn[partner], kn[order], kn[partner]]),
        "table": constants(),
    }
    arrays = {f"in_{k}": np.ascontiguousarray(v) for k, v in arrays.items()}
    nc = bacc.Bacc("TRN2", target_bir_lowering=False, num_devices=1)
    args = [nc.dram_tensor(k, v.shape, mybir.dt.from_np(v.dtype), kind="ExternalInput").ap() for k, v in arrays.items()]
    out = nc.dram_tensor("out", (B, T, DIM), F32, kind="ExternalOutput").ap()
    layer_program(nc, *args, out)
    r = run_bass_kernel_spmd(nc, [arrays], core_ids=[0])
    return r.results[0]["out"]
```

```python
from contextlib import ExitStack

import numpy as np

import concourse.bass as bass
from concourse import mybir

F32 = mybir.dt.float32
F32R = mybir.dt.float32r
BF16 = mybir.dt.bfloat16
ALU = mybir.AluOpType
ACT = mybir.ActivationFunctionType
AX_X = mybir.AxisListType.X

P = 128
B, T, DIM = 4, 512, 256
HEADS, HD = 16, 128
NKV = 4
GROUP = HEADS // NKV
LATENT = 64
TOPK = 64
SEL_DIM = 64
SOFTCAP = 30.0
RMS_EPS = 1e-6
LN_EPS = 1e-5
QUANT_EPS = 1e-8
DFF = 1024
NT = T // P
KD = DIM // P
NF = DFF // P
NQ = HEADS * HD
NK = NKV * HD
STEPS = HEADS
LEAD = 6
NTILES = B * HEADS
PIECE = [T - P * kt for kt in range(NT)]
OFF = [0, T, 2 * T, T + PIECE[1]]
CW = sum(PIECE)
BIG = 1.0e5
MASKED = -1.0e30
TAKEN = -3.0e38
ROUNDS = TOPK // 8
ORDER = [64 * a + 2 * i + c for a in range(2) for c in range(2) for i in range(32)]
PARTNER = [64 * a + 2 * i + 1 - c for a in range(2) for c in range(2) for i in range(32)]
C_DIST, C_CAUSAL, C_EYE, C_OFFDIAG = 0, CW, CW + P, CW + 2 * P
C_END = CW + 3 * P


def slope(h):
    start = 2.0 ** (-2.0 ** (-(np.log2(HEADS) - 3)))
    return float(start * start ** h)


def constants():
    t = np.zeros((P, C_END), np.float32)
    inv = (np.float32(1.0) / np.power(np.float32(10000.0), np.arange(0, HD, 2, dtype=np.float32) / np.float32(HD))).astype(np.float32)
    f = np.arange(T, dtype=np.float32)[:, None] * inv[None, :]
    emb = np.concatenate([f, f], -1)[:, 0::2].astype(np.float64)
    cos, sin = np.cos(emb), np.sin(emb)
    pair = np.array([ORDER[i] // 2 for i in range(HD)])
    odd = np.array([ORDER[i] % 2 for i in range(HD)])
    c = cos[:, pair]
    s = sin[:, pair] * np.where(odd, 1.0, -1.0)
    trig = np.stack([c, s]).reshape(2, NT, P, HD).transpose(2, 0, 1, 3).astype(np.float32)
    key = np.arange(P)[:, None]
    for kt in range(NT):
        d = np.arange(PIECE[kt])[None, :] - key
        t[:, C_DIST + OFF[kt]:C_DIST + OFF[kt] + PIECE[kt]] = np.where(d >= 0, d, BIG)
    t[:, C_CAUSAL:C_EYE] = np.where(np.arange(P)[None, :] > key, MASKED, 0.0)
    t[:, C_EYE:C_OFFDIAG] = np.eye(P)
    t[:, C_OFFDIAG:C_END] = 1.0 - np.eye(P)
    return t, trig


def layer_program(nc, x, w_q, w_down, w_up, w_o, gate_w, w1, w2, biases, gate_b, b_down, b1,
                  norm_w, table, trig, out):
    xs = nc.dram_tensor("xT_scratch", (B, P, 2, KD, T), F32, kind="Internal").ap()
    ks = nc.dram_tensor("kT_scratch", (B, P, NKV, T), F32, kind="Internal").ap()
    vs = nc.dram_tensor("v_scratch", (B, P, NT, NK), F32, kind="Internal").ap()
    ss = nc.dram_tensor("sel_scratch", (B, NT, P, T), F32, kind="Internal").ap()

    with ExitStack() as ctx:
        def sb(name, shape, dt=F32):
            return ctx.enter_context(nc.sbuf_tensor(name, shape, dt))

        def sem(name):
            return ctx.enter_context(nc.semaphore(name))

        wqh = sb("wq_hi", [P, KD, NQ], F32R)
        wql = sb("wq_lo", [P, KD, NQ], F32R)
        xh = sb("xT_hi", [P, KD, T], F32R)
        xl = sb("xT_lo", [P, KD, T], F32R)
        kT = sb("kT", [P, NKV, T])
        V = sb("V_and_twos", [P, NT, NKV, HD + 1])
        gw = sb("gate_w", [P, HEADS, HD])
        wo = sb("w_o", [P, HEADS, DIM])
        qT = sb("qT", [P, 2, GROUP, T])
        D = sb("distance", [P, CW])
        nselT = sb("not_selected_T", [P, NT, T], BF16)
        nsel = sb("not_selected", [P, 2, T], BF16)
        work = sb("sel_work", [P, 2, T])
        s_out_sb = sb("sel_scores", [P, 2, T])
        th = sb("softcapped", [P, CW])
        pr = sb("probs", [P, 2, CW])
        sq = sb("squares", [P, NK + HD])
        t1 = sb("rot_cos", [P, NK + HD])
        t2 = sb("rot_sin", [P, NK + HD])
        qn = sb("rotated", [P, NK + HD])
        yn = sb("y_T", [P, T])
        yq = sb("y_rows", [P, NT, HD])
        gt = sb("gate_tanh", [P, T])
        yg = sb("y_gated", [P, T])
        r1 = sb("residual", [P, B * NT, DIM])
        con = sb("constants", [P, C_END])
        rope = sb("rope_tables", [P, 4, NT, HD])
        brow = sb("bias_rows", [64, NQ + 2 * DIM], F32R)
        onesr = sb("ones_r", [64, P], F32R)
        fw = sb("small_weights_r", [P, 4096], F32R)
        identb = sb("ident_bf16", [P, P], BF16)
        gb = sb("gate_bias_half", [P, HEADS])
        bd = sb("b_down", [P, 1])
        b1s = sb("b1", [P, NF])
        ssq = sb("sum_squares", [P, 8])
        msq = sb("mean_squares", [P, 8])
        rstd = sb("rstd", [P, 16])
        mhalf = sb("minus_half", [P, 8])
        den4 = sb("recip_den", [P, NT])
        top8 = sb("top8", [P, 8])
        stats = sb("bn_stats", [P, 2, NT, 6])
        mv = sb("mean_var", [P, 2, NT, 2])
        wsum = sb("w_abs_sums", [P, 2])
        wscale = sb("w_half_scale", [P, 4])
        onesq = sb("ones_square", [P, P])

        ident = con[:, C_EYE:C_OFFDIAG]
        stage = r1[:, :, :].rearrange("p a d -> p (a d)")
        prf = pr[:, :, :].rearrange("p a c -> p (a c)")
        up_in = prf[:, 0:2 * NK]
        down_in = prf[:, 2 * NK:2 * NK + KD * P].rearrange("p (k n) -> p k n", k=KD)
        xin = prf[:, CW:CW + NT * DIM].rearrange("p (j d) -> p j d", j=NT)
        braw = wo[0:1, :, :].rearrange("p a d -> p (a d)")
        wA, wB = fw[:, 0:2 * NK], fw[:, 2 * NK:4 * NK]
        latA, latB = fw[:, 4 * NK:4 * NK + T], fw[:, 4 * NK + T:4 * NK + 2 * T]
        wdr = fw[:, 4 * NK + 2 * T:4 * NK + 2 * T + 2 * KD * P].rearrange("p (a k n) -> p a k n", a=2, k=KD)
        latf = yn[:, :]
        nw = gt[:, :].rearrange("p (w d) -> p w d", w=4)
        q0T = yg[:, :]
        LAG = 2
        QN = (qn[:, :], th[:, 0:NK + HD])
        K_BANKS = ((3, 5), (0, 1))
        qT_flat = qT[:, :, :, :].rearrange("p a g t -> p (a g t)")
        wraw = rope[:, :, :, :].rearrange("p w j d -> p (w j d)")
        w1q = wql[:, 0, :].rearrange("p (k f) -> p k f", k=KD)
        w2q = wql[:, 1, :].rearrange("p (k n) -> p k n", k=NF)
        wscr = nselT[:, :, :].rearrange("p k t -> p (k t)")
        trig_in = qT_flat[:, 0:2 * NT * HD].rearrange("p (c j d) -> p c j d", c=2, j=NT)
        x1 = work[:, :, :].rearrange("p a (c d) -> p (a c) d", d=DIM)
        hr = wqh[:, :, :].rearrange("p s (a c t) -> p (s a) c t", a=2, c=2)
        HSLOTS, FFN_LAG = 4, 2
        H_BANKS = (2, 3, 6, 7)
        hf = prf[:, 0:HSLOTS * T].rearrange("p (s t) -> p s t", s=HSLOTS)
        gw_flat = gw[:, :, :].rearrange("p h e -> p (h e)")
        r2 = gw_flat[:, 0:NT * DIM].rearrange("p (j d) -> p j d", j=NT)
        ffn_y = gw_flat[:, NT * DIM:].rearrange("p (j d) -> p j d", j=NT)

        ps = ctx.enter_context(nc.psum_tensor("psum", [P, 8, 512], F32))
        sc_ps = ps[:, 0:3, :].rearrange("p a b -> p (a b)")
        z_ps, x_ps = ps[:, 3, :], ps[:, 4, :]
        y_ps = ps[:, 5, 0:(NT - 1) * (HD + 1)].rearrange("p (j d) -> p j d", j=NT - 1)
        y3_ps = x_ps[:, 0:HD + 1]
        o_ps = ps[:, 6:8, :]

        w_in = sem("w_in")
        con_in = sem("con_in")
        trig_loaded = sem("trig_loaded")
        misc_in = sem("misc_in")
        small_in = sem("small_in")
        braw_in = sem("braw_in")
        wo_in = sem("wo_in")
        gw_in = sem("gw_in")
        r1_in = sem("r1_in")
        x_in = sem("x_in")
        wq_split = sem("wq_split")
        setup_act = sem("setup_act")
        setup_dve = sem("setup_dve")
        setup_pool = sem("setup_pool")
        tables_done = sem("tables_done")
        rows_zeroed = sem("rows_zeroed")
        brow_done = sem("brow_done")
        brow_link = sem("brow_link")
        xtr_done = sem("xtr_done")
        xhi_done = sem("xhi_done")
        xlo_done = sem("xlo_done")
        lat_mm = sem("lat_mm")
        latf_done = sem("latf_done")
        latB_done = sem("latB_done")
        latA_link = sem("latA_link")
        latA_done = sem("latA_done")
        k_mm = sem("k_mm")
        v_mm = sem("v_mm")
        q0_mm = sem("q0_mm")
        ksq_done = sem("ksq_done")
        kss_done = sem("kss_done")
        kt1_done = sem("kt1_done")
        kt2_done = sem("kt2_done")
        v_ev = sem("v_ev")
        krope_link = sem("krope_link")
        kn_done = sem("kn_done")
        ktr_done = sem("ktr_done")
        ktr_ev = sem("ktr_ev")
        s_mm = sem("s_mm")
        s_ev = sem("s_ev")
        xs_out = sem("xs_out")
        small_split = sem("small_split")
        ks_out = sem("ks_out")
        vs_out = sem("vs_out")
        qp_done = sem("qp_done")
        sq_done = sem("sq_done")
        ss_done = sem("ss_done")
        t1_done = sem("t1_done")
        t2_done = sem("t2_done")
        qn_done = sem("qn_done")
        rope_link = sem("rope_link")
        tr_done = sem("tr_done")
        qT_done = sem("qT_done")
        sc_done = sem("sc_done")
        th_done = sem("th_done")
        u_done = sem("u_done")
        p_done = sem("p_done")
        pv_done = sem("pv_done")
        rden_link = sem("rden_link")
        yq_done = sem("yq_done")
        yt_done = sem("yt_done")
        yn_done = sem("yn_done")
        gate_done = sem("gate_done")
        gt_done = sem("gt_done")
        yg_done = sem("yg_done")
        wo_done = sem("wo_done")
        res_done = sem("res_done")
        topk_link = sem("topk_link")
        ns_done = sem("ns_done")
        mt_done = sem("mt_done")
        mc_done = sem("mc_done")
        D_done = sem("D_done")
        fw_in = sem("fw_in")
        fabs_done = sem("fabs_done")
        fsum_mm = sem("fsum_mm")
        fscale_link = sem("fscale_link")
        ternary_link = sem("ternary_link")
        ffnw_done = sem("ffnw_done")
        ln1_link = sem("ln1_link")
        ln2_link = sem("ln2_link")
        st1_done = sem("st1_done")
        frstd1_done = sem("frstd1_done")
        fpool1_link = sem("fpool1_link")
        fpool2_link = sem("fpool2_link")
        x1r_done = sem("x1r_done")
        x1_done = sem("x1_done")
        fxt_done = sem("fxt_done")
        fxhi_done = sem("fxhi_done")
        fxlo_done = sem("fxlo_done")
        h_mm = sem("h_mm")
        h_done = sem("h_done")
        h2_done = sem("h2_done")
        hlo_done = sem("hlo_done")
        f2_mm = sem("f2_mm")
        r2_done = sem("r2_done")
        st2_done = sem("st2_done")
        frstd2_done = sem("frstd2_done")
        y_done = sem("y_done")
        y_out = sem("y_out")
        passed_dve = sem("passed_dve")
        passed_pool = sem("passed_pool")
        xT_in = [sem(f"xT_in{j}") for j in range(NT)]
        kT_in = [sem(f"kT_in{g}") for g in range(NKV)]
        v_in = [sem(f"v_in{g}") for g in range(NKV)]
        s_in = [sem(f"s_in{i}") for i in range(2)]
        s_out = [sem(f"s_out{i}") for i in range(2)]

        block = ctx.enter_context(nc.Block())

        def batches(eng, body, split_last):
            n = B - 1 if split_last else B
            body(0, False)
            with eng.Fori(1, n) as b:
                body(b, False)
            if split_last:
                body(B - 1, True)

        def heads_view(ap, h):
            return ap.rearrange("p (h d) -> p h d", h=h)

        def blocks_view(ap, h, c):
            return ap.rearrange("p (h a c i) -> p h a c i", h=h, a=2, c=2)[:, :, :, c, :]

        def table_blocks(which, j, c, h):
            v = rope[:, which, j, :].rearrange("p (a c i) -> p a c i", a=2, c=2)[:, :, c, :]
            return v.unsqueeze(1).broadcast_to([P, h, 2, 32])

        ALL = 2 * ROUNDS + 1
        EARLY = {1: [(0, 3, 8)], 2: [(0, 11, 16)], 3: [(1, 1, 5)], 4: [(1, 8, 12)], 5: [(1, 15, ALL), (2, 0, 1)],
                 6: [(2, 3, 6)], 7: [(2, 8, 11)], 8: [(2, 13, 16)], 9: [(3, 1, 3)], 10: [(3, 5, 7)],
                 11: [(3, 9, 11)], 12: [(3, 13, 15)]}
        LATE = {0: [(0, 0, 3)], 1: [(0, 8, 11)], 2: [(0, 16, ALL), (1, 0, 1)], 3: [(1, 5, 8)], 4: [(1, 12, 15)],
                5: [(2, 1, 3)], 6: [(2, 6, 8)], 7: [(2, 11, 13)], 8: [(2, 16, ALL), (3, 0, 1)], 9: [(3, 3, 5)],
                10: [(3, 7, 9)], 11: [(3, 11, 13)], 12: [(3, 15, ALL)]}
        FIRST_TOPK_KEYS = {0: (0, 0, 8), 1: (0, 8, ALL), 2: (1, 0, 6), 3: (1, 6, 12), 4: (1, 12, ALL)}
        FIRST_TOPK = {0: (2, 0, 14), 1: (2, 14, ALL), 2: (3, 0, 6), 3: (3, 6, 12), 4: (3, 12, ALL)}
        MASK_AFTER = {1: 0, 2: 1, 3: 2, 5: 3}
        TURN_AT = {3: 0, 6: 1, 9: 2, 13: 3}
        TOPK_LINKS = 2 * ROUNDS + 1
        SCALE_AT = (11, 13)

        @block.sync
        def _(sp):
            def load_batch(b):
                sp.dma_start(xin, x[bass.ds(b, 1)].rearrange("a (j p) d -> p (a j) d", p=P)).then_inc(x_in, 16)

            load_batch(0)
            sp.dma_start(con[:], table).then_inc(con_in, 16)
            sp.dma_start(down_in[:, :, 0:LATENT], w_down.rearrange("(k p) n -> p k n", p=P)).then_inc(small_in, 16)
            sp.dma_start(down_in[:, :, LATENT:P], w_down.rearrange("(k p) n -> p k n", p=P)).then_inc(small_in, 16)
            sp.dma_start(up_in[0:LATENT, :], w_up).then_inc(small_in, 16)
            sp.dma_start(up_in[LATENT:P, :], w_up).then_inc(small_in, 16)
            sp.dma_start(bd[:], b_down).then_inc(small_in, 16)
            sp.dma_start(braw[:, 0:biases.shape[1]], biases).then_inc(braw_in, 16)
            sp.dma_start(trig_in, trig).then_inc(trig_loaded, 16)
            sp.dma_start(nw, norm_w.partition_broadcast(P)).then_inc(trig_loaded, 16)
            sp.dma_start(stage.rearrange("p (k n) -> p k n", k=KD),
                         w_q.rearrange("(k p) n -> p k n", p=P)).then_inc(w_in, 16)
            sp.dma_start(gb[:], gate_b).then_inc(misc_in, 16)
            sp.dma_start(b1s[:], b1).then_inc(misc_in, 16)
            sp.dma_start(gw[:], gate_w.rearrange("h d e -> d h e")).then_inc(gw_in, 16)

            def load_x(b, j):
                sp.dma_start(xh[:, :, P * j:P * (j + 1)].bitcast(F32),
                             xs[bass.ds(b, 1), :, 0, :, P * j:P * (j + 1)].rearrange("a p k t -> p (a k) t")).then_inc(xT_in[j], 16)
                sp.dma_start(xl[:, :, P * j:P * (j + 1)].bitcast(F32),
                             xs[bass.ds(b, 1), :, 1, :, P * j:P * (j + 1)].rearrange("a p k t -> p (a k) t")).then_inc(xT_in[j], 16)

            def load_s(b, qt):
                w = P * (qt + 1)
                sp.dma_start(work[:, qt % 2, 0:w],
                             ss[bass.ds(b, 1), qt, :, 0:w].rearrange("a p t -> (a p) t")).then_inc(s_in[qt % 2], 16)

            def keys(b, last):
                if last:
                    for i in range(2):
                        sp.wait_ge(s_out[i], 16 * (NT // 2))
                    load_s(0, 0)
                    load_s(0, 1)
                sp.wait_ge(xlo_done, b * KD + KD)
                sp.dma_start(xs[bass.ds(b, 1), :, 0].rearrange("a p k t -> p (a k) t"), xh[:].bitcast(F32)).then_inc(xs_out, 16)
                sp.dma_start(xs[bass.ds(b, 1), :, 1].rearrange("a p k t -> p (a k) t"), xl[:].bitcast(F32)).then_inc(xs_out, 16)
                if not last:
                    load_batch(b + 1)
                for j in range(NT):
                    sp.wait_ge(s_ev, b * NT + j + 1)
                    sp.dma_start(ss[bass.ds(b, 1), j, :, 0:P * (j + 1)].rearrange("a p t -> (a p) t"),
                                 s_out_sb[:, j % 2, 0:P * (j + 1)]).then_inc(s_out[j % 2], 16)
                    if j == 1:
                        sp.wait_ge(v_ev, b * NT + NT)
                        sp.dma_start(vs[bass.ds(b, 1)].rearrange("a p k (g d) -> p (a k) g d", g=NKV),
                                     V[:, :, :, 0:HD]).then_inc(vs_out, 16)
                    if last and j == 1:
                        sp.wait_ge(ns_done, 1)
                        load_s(0, 2)
                        sp.wait_ge(xs_out, 32 * B)
                        sp.wait_ge(q0_mm, B * NT)
                        for t in range(NT):
                            load_x(0, t)
                sp.wait_ge(ktr_ev, b * NT + NT)
                sp.dma_start(ks[bass.ds(b, 1)].rearrange("a p g t -> p (a g) t"), kT[:]).then_inc(ks_out, 16)

            batches(sp, keys, True)

            def load_k(b, g):
                sp.dma_start(kT[:, g, :], ks[bass.ds(b, 1), :, g].rearrange("a p t -> (a p) t")).then_inc(kT_in[g], 16)

            def load_v(b, g):
                sp.dma_start(V[:, :, g, 0:HD],
                             vs[bass.ds(b, 1), :, :, HD * g:HD * (g + 1)].rearrange("a p k n -> p (a k) n")).then_inc(v_in[g], 16)

            sp.wait_ge(ns_done, 2)
            load_s(0, 3)
            sp.wait_ge(xs_out, 32 * B)
            for i in range(2):
                sp.wait_ge(s_out[i], 16 * (NT // 2) * B)
            sp.wait_ge(vs_out, 16 * B)
            sp.wait_ge(ks_out, 16 * B)
            load_k(0, 0)
            load_v(0, 0)
            for g in range(1, NKV):
                load_k(0, g)
                load_v(0, g)
            sp.wait_ge(brow_done, 4)
            sp.dma_start(wo[:], w_o.rearrange("(h d) n -> d h n", d=HD)).then_inc(wo_in, 16)
            sp.wait_ge(wq_split, KD + 1)
            sp.dma_start(r1[:], x.rearrange("b (j p) d -> p (b j) d", p=P)).then_inc(r1_in, 16)

            def heads(b, last):
                if last:
                    return
                n = b * STEPS
                sp.wait_ge(ns_done, b * NT + 3)
                load_s(b + 1, 0)
                sp.wait_ge(ns_done, b * NT + 4)
                load_s(b + 1, 1)
                sp.wait_ge(sc_done, n + 4)
                load_k(b + 1, 0)
                sp.wait_ge(ns_done, b * NT + NT + 1)
                load_s(b + 1, 2)
                sp.wait_ge(pv_done, n + 4)
                load_v(b + 1, 0)
                sp.wait_ge(ns_done, b * NT + NT + 2)
                load_s(b + 1, 3)
                for j in range(NT):
                    sp.wait_ge(qp_done, n + 12 + j + 1)
                    load_x(b + 1, j)
                    if j == 1:
                        sp.wait_ge(sc_done, n + 8)
                        load_k(b + 1, 1)
                        sp.wait_ge(pv_done, n + 8)
                        load_v(b + 1, 1)
                for g in range(2, NKV):
                    sp.wait_ge(sc_done, n + GROUP * (g + 1))
                    load_k(b + 1, g)
                    sp.wait_ge(pv_done, n + GROUP * (g + 1))
                    load_v(b + 1, g)

            batches(sp, heads, True)

            sp.wait_ge(t2_done, NTILES)
            sp.dma_start(wraw.rearrange("p (k f) -> p k f", k=KD),
                         w1.rearrange("(k p) f -> p k f", p=P)).then_inc(fw_in, 16)
            sp.wait_ge(ffnw_done, 1)
            sp.dma_start(wraw.rearrange("p (k n) -> p k n", k=NF),
                         w2.rearrange("(k p) n -> p k n", p=P)).then_inc(fw_in, 16)

            def ffn(b, last):
                sp.wait_ge(y_done, b * NT + NT)
                sp.dma_start(out[bass.ds(b, 1)].rearrange("a (j p) d -> p (a j) d", p=P),
                             ffn_y).then_inc(y_out, 16)

            batches(sp, ffn, False)
            sp.wait_ge(y_out, 16 * B)

        @block.tensor
        def _(pe):
            def mm(o, lhsT, rhs, start, stop):
                return pe.matmul(o, lhsT, rhs, start=start, stop=stop, skip_group_check=True)

            def project(o, cols, j, bias_cols):
                tok = slice(P * j, P * (j + 1))
                for k in range(KD):
                    mm(o, xh[:, k, tok], wqh[:, k, cols], k == 0, False)
                    mm(o, xl[:, k, tok], wqh[:, k, cols], False, False)
                    mm(o, xh[:, k, tok], wql[:, k, cols], False, False)
                return mm(o, onesr[:], brow[:, bias_cols], False, True)

            pe.wait_ge(con_in, 16)

            def turn_x(b):
                pe.wait_ge(x_in, b * 16 + 16)
                pe.wait_ge(xlo_done, b * KD)
                pe.wait_ge(kt2_done, b * NT)
                for k in range(KD):
                    for j in range(NT):
                        m = pe.transpose(ps[:, k, P * j:P * (j + 1)], xin[:, j, P * k:P * (k + 1)], ident)
                    m.then_inc(xtr_done, 1)

            def latent(b):
                pe.wait_ge(xlo_done, b * KD + KD)
                for k in range(KD):
                    mm(ps[:, 5, :], wdr[:, 0, k, :], xh[:, k, :], k == 0, False)
                    mm(ps[:, 5, :], wdr[:, 1, k, :], xh[:, k, :], False, False)
                    m = mm(ps[:, 5, :], wdr[:, 0, k, :], xl[:, k, :], False, k == KD - 1)
                m.then_inc(lat_mm, 1)

            turn_x(0)
            pe.wait_ge(small_split, 1)
            latent(0)
            pe.wait_ge(setup_act, 3)
            pe.wait_ge(wq_split, 1)
            pe.wait_ge(brow_done, 3)

            def keys(b, last):
                pe.wait_ge(latA_done, b + 1)
                pe.wait_ge(latB_done, b + 1)
                for j in range(NT + LAG):
                    i = b * NT + j
                    tok = slice(P * j, P * (j + 1))
                    if j == NT + 1 and not last:
                        latent(b + 1)
                    if j >= LAG:
                        t = i - LAG
                        pe.wait_ge(kn_done, t + 1)
                        pe.wait_ge(ktr_ev, t)
                        rotated = QN[j % 2]
                        for g in range(NKV):
                            pe.transpose(ps[:, 6, P * g:P * (g + 1)], rotated[:, HD * g:HD * (g + 1)], ident)
                        pe.transpose(ps[:, 7, 0:P], rotated[:, NK:NK + HD], ident).then_inc(ktr_done, 1)
                    if j < NT:
                        k_bank, q_bank = K_BANKS[j % 2]
                        if not (isinstance(i, int) and i < 2):
                            pe.wait_ge(kt2_done, i - 1)
                        mm(ps[:, k_bank, :], latA[:, tok], wA[:, 0:NK], True, False)
                        mm(ps[:, k_bank, :], latB[:, tok], wB[:, 0:NK], False, True).then_inc(k_mm, 1)
                        project(ps[:, q_bank, 0:HD], slice(0, HD), j, slice(0, HD)).then_inc(q0_mm, 1)
                        pe.wait_ge(v_ev, i)
                        mm(ps[:, 4, :], latA[:, tok], wA[:, NK:2 * NK], True, False)
                        mm(ps[:, 4, :], latB[:, tok], wB[:, NK:2 * NK], False, True).then_inc(v_mm, 1)
                    elif j == NT and not last:
                        turn_x(b + 1)
                    if j >= LAG:
                        p = slice(P * (j - LAG), P * (j - LAG + 1))
                        pe.wait_ge(ktr_ev, t + 1)
                        pe.wait_ge(s_ev, t)
                        mm(ps[:, 2, 0:p.stop], q0T[0:SEL_DIM, p], kT[0:SEL_DIM, 0, 0:p.stop], True, True).then_inc(s_mm, 1)

            batches(pe, keys, True)

            def scores(b, s):
                g, n = s // GROUP, b * STEPS + s
                pe.wait_ge(qT_done, b * STEPS + GROUP * (g + 1))
                pe.wait_ge(kT_in[g], b * 16 + 16)
                pe.wait_ge(th_done, n)
                for kt in range(NT):
                    m = mm(sc_ps[:, OFF[kt]:OFF[kt] + PIECE[kt]], kT[:, g, P * kt:P * (kt + 1)],
                           qT[:, g % 2, s % GROUP, P * kt:T], True, True)
                m.then_inc(sc_done, 1)

            def values(b, s, last):
                g, n = s // GROUP, b * STEPS + s
                pe.wait_ge(p_done, n + 1)
                pe.wait_ge(v_in[g], b * 16 + 16)
                pe.wait_ge(yq_done, n)
                for qt in range(NT):
                    if qt == NT - 1:
                        pe.wait_ge(qT_done, n + LEAD - 1 if not last or s + LEAD - 1 <= STEPS else NTILES)
                        if s in TURN_AT and not last:
                            pe.wait_ge(mc_done, b * NT + NT + TURN_AT[s] + 1)
                    for kt in range(qt + 1):
                        q = OFF[kt] + P * (qt - kt)
                        m = mm(y_ps[:, qt, :] if qt < NT - 1 else y3_ps, pr[:, s % 2, q:q + P], V[:, kt, g, :],
                               kt == 0, kt == qt)
                m.then_inc(pv_done, 1)

            def query(b, s, m_):
                j, u = s % NT, s // NT
                pe.wait_ge(xT_in[j], b * 32 + 32)
                if not (isinstance(m_, int) and m_ < LEAD):
                    pe.wait_ge(gt_done, m_ - LEAD)
                pe.wait_ge(t2_done, m_)
                cols = slice(GROUP * HD * u, GROUP * HD * (u + 1))
                project(z_ps, cols, j, cols).then_inc(qp_done, 1)

            def turn_y(b, s):
                n = b * STEPS + s
                pe.wait_ge(yq_done, n + 1)
                for qt in range(NT):
                    m = pe.transpose(x_ps[:, P * qt:P * (qt + 1)], yq[:, qt, :], ident)
                m.then_inc(yt_done, 1)

            def output(b, s, half):
                n = b * STEPS + s
                if s == 0 and half == 0:
                    pe.wait_ge(res_done, b)
                    for a in range(2):
                        mm(o_ps[:, a, :].rearrange("p (c d) -> p c d", c=2), onesr[:],
                           brow[:, NQ:NQ + DIM].unsqueeze(1).broadcast_to([64, 2, DIM]), True, False)
                pe.wait_ge(yg_done, n + 1)
                for j in (2 * half, 2 * half + 1):
                    m = mm(o_ps[:, half, DIM * (j % 2):DIM * (j % 2 + 1)], yg[:, P * j:P * (j + 1)], wo[:, s, :],
                           False, s == STEPS - 1)
                if half:
                    m.then_inc(wo_done, 1)

            def turn_queries(m_, after):
                pe.wait_ge(qn_done, m_ + 1)
                pe.wait_ge(qT_done, m_)
                pe.wait_ge(yn_done, after)
                for h in range(GROUP):
                    m = pe.transpose(x_ps[:, P * h:P * (h + 1)], qn[:, HD * h:HD * (h + 1)], ident)
                m.then_inc(tr_done, 1)

            def gate(b, s, last):
                n = b * STEPS + s
                pe.wait_ge(yn_done, n + 1)
                pe.wait_ge(t2_done, n + LEAD + 1 if not last or s + LEAD < STEPS else NTILES)
                mm(z_ps, gw[:, s, :], yn[:], True, True).then_inc(gate_done, 1)

            def turn_mask(tile, qt, evacs):
                pe.wait_ge(ns_done, tile + 1)
                pe.wait_ge(qT_done, evacs)
                xb = x_ps.bitcast(BF16)
                for kt in range(qt + 1):
                    m = pe.transpose(xb[:, P * kt:P * (kt + 1)], nsel[:, qt % 2, P * kt:P * (kt + 1)], identb[:])
                m.then_inc(mt_done, 1)

            for m_ in range(LEAD):
                query(0, m_, m_)
                if m_ >= 1:
                    pe.wait_ge(mc_done, sum(k < m_ for k in MASK_AFTER))
                    turn_queries(m_ - 1, 0)
                    if m_ in MASK_AFTER:
                        if m_ == 1:
                            pe.wait_ge(setup_dve, 1)
                        turn_mask(MASK_AFTER[m_], MASK_AFTER[m_], m_)
            scores(0, 0)
            pe.wait_ge(gw_in, 16)
            pe.wait_ge(wo_in, 16)

            def heads(b, last):
                first = isinstance(b, int) and b == 0
                for s in range(STEPS):
                    n = b * STEPS + s
                    if s + 1 < STEPS:
                        scores(b, s + 1)
                    elif not last:
                        scores(b + 1, 0)
                    if s in TURN_AT and not last:
                        turn_mask(b * NT + NT + TURN_AT[s], TURN_AT[s], n + LEAD - 1)
                    values(b, s, last)
                    if s + LEAD < STEPS:
                        query(b, s + LEAD, n + LEAD)
                    elif not last:
                        query(b + 1, s + LEAD - STEPS, n + LEAD)
                    if s >= 1:
                        output(b, s - 1, 0)
                    elif not first:
                        output(b - 1, STEPS - 1, 0)
                    if last and s in SCALE_AT:
                        i = SCALE_AT.index(s)
                        pe.wait_ge(fabs_done, i + 1)
                        pe.wait_ge(yq_done, n + 1)
                        mm(x_ps[:, 0:1], onesq[:], wsum[:, i:i + 1], True, True).then_inc(fsum_mm, 1)
                        pe.wait_ge(fscale_link, 2 * i + 1)
                    turn_y(b, s)
                    if s >= 1:
                        output(b, s - 1, 1)
                    elif not first:
                        output(b - 1, STEPS - 1, 1)
                    if s + LEAD - 1 < STEPS or not last:
                        turn_queries(n + LEAD - 1, n + 1)
                    gate(b, s, last)

            batches(pe, heads, True)
            output(B - 1, STEPS - 1, 0)
            output(B - 1, STEPS - 1, 1)

            def turn_x1(b):
                pe.wait_ge(x1_done, b * NT + NT)
                pe.wait_ge(fxlo_done, b * KD)
                for k in range(KD):
                    for j in range(NT):
                        m = pe.transpose(ps[:, k, P * j:P * (j + 1)], x1[:, j, P * k:P * (k + 1)], ident)
                    m.then_inc(fxt_done, 1)

            pe.wait_ge(th_done, NTILES)
            turn_x1(0)
            pe.wait_ge(ffnw_done, 2)
            pe.wait_ge(yq_done, NTILES)

            def ffn(b, last):
                pe.wait_ge(fxlo_done, b * KD + KD)
                for f in range(NF + FFN_LAG):
                    i = b * NF + f
                    if f < NF:
                        if not (isinstance(i, int) and i < HSLOTS):
                            pe.wait_ge(h2_done, i - HSLOTS + 1)
                        for k in range(KD):
                            mm(ps[:, H_BANKS[f % HSLOTS], :], w1q[:, k, P * f:P * (f + 1)], xh[:, k, :], k == 0, False)
                            m = mm(ps[:, H_BANKS[f % HSLOTS], :], w1q[:, k, P * f:P * (f + 1)], xl[:, k, :], False, k == KD - 1)
                        m.then_inc(h_mm, 1)
                    elif f == NF and not last:
                        turn_x1(b + 1)
                    if f == FFN_LAG:
                        pe.wait_ge(r2_done, b * 2)
                        for a in range(2):
                            mm(ps[:, 4 + a, :].rearrange("p (c d) -> p c d", c=2), onesr[:],
                               brow[:, NQ + DIM:NQ + 2 * DIM].unsqueeze(1).broadcast_to([64, 2, DIM]), True, False)
                    if f >= FFN_LAG:
                        g = f - FFN_LAG
                        pe.wait_ge(hlo_done, i - FFN_LAG + 1)
                        for j in range(NT):
                            for part in range(2):
                                m = mm(ps[:, 4 + j // 2, DIM * (j % 2):DIM * (j % 2 + 1)],
                                       hr[:, g % HSLOTS, part, P * j:P * (j + 1)], w2q[:, g, :], False, g == NF - 1)
                        m.then_inc(f2_mm, 1)

            batches(pe, ffn, True)

        @block.scalar
        def _(act):
            def split_wq(k, cols):
                nc.scalar.activation(wqh[:, k, cols], stage[:, NQ * k + cols.start:NQ * k + cols.stop], ACT.Copy).then_inc(setup_act, 1)

            def split_x(b):
                act.wait_ge(xs_out, b * 32)
                act.wait_ge(q0_mm, b * NT)
                for k in range(KD):
                    act.wait_ge(xtr_done, b * KD + k + 1)
                    nc.scalar.activation(xh[:, k, :], ps[:, k, :], ACT.Copy).then_inc(xhi_done, 1)

            act.wait_ge(small_in, 16 * 5)
            nc.scalar.activation(wdr[:, 0], down_in, ACT.Copy).then_inc(setup_act, 1)
            split_x(0)
            nc.scalar.activation(wA, up_in, ACT.Copy).then_inc(setup_act, 1)

            def latent(b):
                act.wait_ge(lat_mm, b + 1)
                act.wait_ge(latA_done, b)
                act.wait_ge(latB_done, b)
                nc.scalar.activation(latf, ps[:, 5, :], ACT.Identity, bias=bd[:]).then_inc(latf_done, 1)
                act.wait_ge(latf_done, b + 1)
                act.wait_ge(v_mm, b * NT)
                nc.scalar.activation(latB[0:LATENT, :], latf[0:LATENT, :], ACT.Copy).then_inc(latB_done, 1)

            latent(0)
            act.wait_ge(w_in, 16)
            nc.scalar.activation(wqh[:, :, 0:HD], stage.rearrange("p (k n) -> p k n", k=KD)[:, :, 0:HD],
                                 ACT.Copy).then_inc(setup_act, 1)

            def keys(b, last):
                for j in range(NT + LAG):
                    i = b * NT + j
                    if j == NT + 1 and not last:
                        latent(b + 1)
                    if j >= LAG:
                        t = i - LAG
                        act.wait_ge(ktr_done, t + 1)
                        act.wait_ge(ks_out, b * 16)
                        act.wait_ge(s_mm, t)
                        tok = slice(P * (j - LAG), P * (j - LAG + 1))
                        nc.scalar.activation(kT[:, :, tok], heads_view(ps[:, 6, :], NKV), ACT.Copy)
                        nc.scalar.activation(q0T[:, tok], ps[:, 7, 0:P], ACT.Copy).then_inc(ktr_ev, 1)
                    if j < NT:
                        k_bank, q_bank = K_BANKS[j % 2]
                        act.wait_ge(k_mm, i + 1)
                        act.wait_ge(kss_done, i)
                        nc.scalar.activation(sq[:, 0:NK], ps[:, k_bank, :], ACT.Square)
                        act.wait_ge(q0_mm, i + 1)
                        nc.scalar.activation(sq[:, NK:], ps[:, q_bank, 0:HD], ACT.Square).then_inc(ksq_done, 1)
                    if j == NT and not last:
                        split_x(b + 1)
                    if 1 <= j <= NT:
                        act.wait_ge(krope_link, 3 * i)
                        rotated = QN[(j - 1) % 2]
                        for h in range(NKV + 1):
                            m = nc.scalar.mul(rotated[:, HD * h:HD * (h + 1)], rotated[:, HD * h:HD * (h + 1)],
                                              rstd[:, 8 * ((j - 1) % 2) + h:8 * ((j - 1) % 2) + h + 1])
                        m.then_inc(kn_done, 1)
                    if j < NT:
                        act.wait_ge(v_mm, i + 1)
                        act.wait_ge(vs_out, b * 16)
                        nc.scalar.activation(V[:, j, :, 0:HD], heads_view(ps[:, 4, :], NKV), ACT.Copy).then_inc(v_ev, 1)
                    if isinstance(b, int) and b == 0 and 1 <= j <= KD:
                        split_wq(j - 1, slice(HD, NQ))

            batches(act, keys, True)

            def softcap(b, s):
                n = b * STEPS + s
                act.wait_ge(sc_done, n + 1)
                act.wait_ge(p_done, n)
                nc.scalar.activation(th[:], sc_ps[:, 0:CW], ACT.Tanh,
                                     scale=1.0 / (SOFTCAP * HD ** 0.5)).then_inc(th_done, 1)

            def exps(b, s):
                n = b * STEPS + s
                act.wait_ge(u_done, n + 1)
                if not (isinstance(n, int) and n < 2):
                    act.wait_ge(pv_done, n - 1)
                nc.scalar.activation(pr[:, s % 2, :], th[:], ACT.Exp, scale=SOFTCAP).then_inc(p_done, 1)

            def squares(m_):
                act.wait_ge(qp_done, m_ + 1)
                act.wait_ge(ss_done, m_)
                nc.scalar.activation(sq[:, 0:NK], z_ps, ACT.Square).then_inc(sq_done, 1)

            def sums_of_squares(m_):
                act.wait_ge(qp_done, m_ + 1)
                if not (isinstance(m_, int) and m_ == 0):
                    act.wait_ge(rope_link, 3 * m_ - 2)
                act.wait_ge(ss_done, m_)
                for h in range(GROUP):
                    m = nc.scalar.activation(sq[:, HD * h:HD * (h + 1)], z_ps[:, HD * h:HD * (h + 1)], ACT.Square,
                                             accum_out=ssq[:, h:h + 1])
                m.then_inc(ss_done, 1)


            def store_y(b, s):
                n = b * STEPS + s
                act.wait_ge(yt_done, n + 1)
                act.wait_ge(gate_done, n)
                act.wait_ge(yg_done, n)
                nc.scalar.activation(yn[:], x_ps, ACT.Copy).then_inc(yn_done, 1)

            def store_queries(m_, u, j, scores_before):
                act.wait_ge(tr_done, m_ + 1)
                act.wait_ge(sc_done, scores_before)
                nc.scalar.activation(qT[:, u % 2, :, P * j:P * (j + 1)], heads_view(x_ps, GROUP),
                                     ACT.Copy).then_inc(qT_done, 1)

            def gate_tanh(b, s):
                n = b * STEPS + s
                act.wait_ge(gate_done, n + 1)
                act.wait_ge(yg_done, n)
                nc.scalar.activation(gt[:], z_ps, ACT.Tanh, bias=gb[:, s:s + 1]).then_inc(gt_done, 1)

            act.wait_ge(misc_in, 32)
            nc.scalar.mul(gb[:], gb[:], 0.5).then_inc(setup_act, 1)
            act.wait_ge(setup_act, 3 + KD + 1)
            for m_ in range(LEAD):
                sums_of_squares(m_)
                if m_ >= 1:
                    store_queries(m_ - 1, (m_ - 1) // NT, (m_ - 1) % NT, 0)
            softcap(0, 0)
            exps(0, 0)

            def heads(b, last):
                for s in range(STEPS):
                    n = b * STEPS + s
                    if s + 1 < STEPS:
                        softcap(b, s + 1)
                    elif not last:
                        softcap(b + 1, 0)
                    if s + LEAD < STEPS or not last:
                        squares(n + LEAD)
                    store_y(b, s)
                    if s + 1 < STEPS:
                        exps(b, s + 1)
                    elif not last:
                        exps(b + 1, 0)
                    if s + LEAD - 1 < STEPS or not last:
                        m_ = s + LEAD - 1
                        store_queries(n + LEAD - 1, m_ // NT, m_ % NT, b * STEPS + NT * (m_ // NT) - NT)
                    gate_tanh(b, s)
                    if last and s + 1 in SCALE_AT:
                        i = SCALE_AT.index(s + 1)
                        act.wait_ge(fw_in, 16 * i + 16)
                        act.wait_ge(D_done, B)
                        act.wait_ge(ternary_link, i)
                        nc.scalar.activation(wscr, wraw, ACT.Abs, accum_out=wsum[:, i:i + 1]).then_inc(fabs_done, 1)

            batches(act, heads, True)

            def split_x1(b):
                for k in range(KD):
                    act.wait_ge(fxt_done, b * KD + k + 1)
                    act.wait_ge(h_mm, b * NF)
                    nc.scalar.activation(xh[:, k, :], ps[:, k, :], ACT.Copy).then_inc(fxhi_done, 1)

            split_x1(0)

            def ffn(b, last):
                for f in range(NF):
                    i = b * NF + f
                    act.wait_ge(h_mm, i + 1)
                    if not (isinstance(i, int) and i < HSLOTS):
                        act.wait_ge(hlo_done, i - HSLOTS + 1)
                    nc.scalar.activation(hf[:, f % HSLOTS, :], ps[:, H_BANKS[f % HSLOTS], :], ACT.Gelu, bias=b1s[:, f:f + 1]).then_inc(h_done, 1)
                    if not (isinstance(i, int) and i < HSLOTS):
                        act.wait_ge(f2_mm, i - HSLOTS + 1)
                    nc.scalar.activation(hr[:, f % HSLOTS, 0, :], ps[:, H_BANKS[f % HSLOTS], :], ACT.Gelu, bias=b1s[:, f:f + 1]).then_inc(h2_done, 1)
                if not last:
                    split_x1(b + 1)

            batches(act, ffn, True)

        @block.vector
        def _(dve):
            nc.vector.memset(V[:, :, :, HD:HD + 1], 2.0)
            nc.vector.memset(wB[LATENT:P, :].bitcast(F32), 0.0)
            nc.vector.memset(latB[LATENT:P, :].bitcast(F32), 1.0)
            nc.vector.memset(onesr[:].bitcast(F32), 1.0)
            nc.vector.memset(onesq[:], 1.0)
            nc.vector.memset(brow[:].bitcast(F32), 0.0).then_inc(rows_zeroed, 1)
            dve.wait_ge(con_in, 16)
            nc.vector.tensor_copy(identb[:], ident).then_inc(setup_dve, 1)
            dve.wait_ge(setup_act, 1)
            nc.vector.tensor_tensor(wdr[:, 1], down_in, wdr[:, 0].bitcast(F32), ALU.subtract).then_inc(small_split, 1)

            def split_x(b):
                for k in range(KD):
                    dve.wait_ge(xhi_done, b * KD + k + 1)
                    nc.vector.tensor_tensor(xl[:, k, :], ps[:, k, :], xh[:, k, :].bitcast(F32), ALU.subtract).then_inc(xlo_done, 1)

            split_x(0)
            NB = NQ + 2 * DIM
            b_up = braw[:, NB:NB + 2 * NK]
            b_up_hi = work[0:1, :, :].rearrange("p a t -> p (a t)")
            dve.wait_ge(braw_in, 16)
            dve.wait_ge(rows_zeroed, 1)
            nc.vector.tensor_copy(wB[64:65, :], b_up)
            nc.vector.tensor_copy(brow[0:1, 0:HD], braw[:, 0:HD]).then_inc(brow_done, 1)
            dve.wait_ge(brow_done, 1)
            nc.vector.tensor_tensor(brow[32:33, 0:HD], braw[:, 0:HD], brow[0:1, 0:HD].bitcast(F32), ALU.subtract)
            nc.vector.tensor_copy(b_up_hi, wB[64:65, :].bitcast(F32)).then_inc(brow_done, 1)
            dve.wait_ge(setup_act, 2)
            nc.vector.tensor_tensor(wB[0:LATENT, :], up_in[0:LATENT, :], wA[0:LATENT, :].bitcast(F32), ALU.subtract)
            dve.wait_ge(brow_done, 2)
            nc.vector.tensor_tensor(wB[96:97, :], b_up, b_up_hi, ALU.subtract).then_inc(brow_done, 1)

            def latent(b):
                dve.wait_ge(latf_done, b + 1)
                dve.wait_ge(v_mm, b * NT)
                nc.vector.tensor_copy(latA, latf).then_inc(latA_link, 1)
                dve.wait_ge(latA_link, b + 1)
                nc.vector.tensor_tensor(latA[LATENT:P, :], latf[LATENT:P, :], latA[LATENT:P, :].bitcast(F32),
                                        ALU.subtract).then_inc(latA_done, 1)

            latent(0)
            stage_k = stage.rearrange("p (k n) -> p k n", k=KD)
            dve.wait_ge(setup_act, 3)
            nc.vector.tensor_tensor(wql[:, :, 0:HD], stage_k[:, :, 0:HD], wqh[:, :, 0:HD].bitcast(F32),
                                    ALU.subtract).then_inc(wq_split, 1)
            dve.wait_ge(trig_loaded, 32)
            for w in (2, 3, 0, 1):
                m = nc.vector.tensor_tensor(rope[:, w], trig_in[:, w % 2],
                                            nw[:, w, :].unsqueeze(1).broadcast_to([P, NT, HD]), ALU.mult)
            m.then_inc(tables_done, 1)
            dve.wait_ge(tables_done, 1)

            def rest_of_biases():
                nc.vector.tensor_copy(brow[0:1, HD:NB], braw[:, HD:NB]).then_inc(brow_link, 1)
                dve.wait_ge(brow_link, 1)
                nc.vector.tensor_tensor(brow[32:33, HD:NB], braw[:, HD:NB], brow[0:1, HD:NB].bitcast(F32),
                                        ALU.subtract).then_inc(brow_done, 1)

            def rest_of_wq(k):
                dve.wait_ge(setup_act, 3 + k + 1)
                nc.vector.tensor_tensor(wql[:, k, HD:NQ], stage_k[:, k, HD:NQ], wqh[:, k, HD:NQ].bitcast(F32),
                                        ALU.subtract).then_inc(wq_split, 1)

            def rotate(dst0, src, h, which, j, first_sem=None):
                w = h * HD
                m = nc.vector.tensor_tensor(heads_view(t1[:, dst0:dst0 + w], h), heads_view(src, h),
                                            rope[:, which, j, :].unsqueeze(1).broadcast_to([P, h, HD]), ALU.mult)
                if first_sem:
                    m.then_inc(first_sem, 1)

            def partners(dst0, src, h, which, j, last_sem):
                w = h * HD
                for c in range(2):
                    m = nc.vector.tensor_tensor(blocks_view(t2[:, dst0:dst0 + w], h, c), blocks_view(src, h, 1 - c),
                                                table_blocks(which + 1, j, c, h), ALU.mult)
                if last_sem:
                    m.then_inc(last_sem, 1)

            def topk(tb, qt, first, end):
                w = P * (qt + 1)
                base = (tb * NT + qt) * TOPK_LINKS
                if first == 0:
                    dve.wait_ge(s_in[qt % 2], tb * 32 + 16 * (qt // 2) + 16)
                for h in range(first, min(end, 2 * ROUNDS)):
                    dve.wait_ge(topk_link, base + h)
                    dve.sem_inc(passed_dve, 1)
                    if h % 2 == 0:
                        nc.vector.max(top8[:], work[:, qt % 2, 0:w]).then_inc(topk_link, 1)
                    else:
                        nc.vector.match_replace(work[:, qt % 2, 0:w], top8[:], work[:, qt % 2, 0:w], TAKEN).then_inc(topk_link, 1)
                if end == ALL:
                    dve.wait_ge(topk_link, base + 2 * ROUNDS)
                    if not (isinstance(tb, int) and tb * NT + qt < 2):
                        dve.wait_ge(mt_done, tb * NT + qt - 1)
                    nc.vector.tensor_scalar(nsel[:, qt % 2, 0:w], work[:, qt % 2, 0:w], 0.5 * TAKEN, None, ALU.is_gt).then_inc(topk_link, 1)
                    dve.wait_ge(topk_link, base + TOPK_LINKS)
                    nc.vector.tensor_tensor(nsel[:, qt % 2, w - P:w], nsel[:, qt % 2, w - P:w], con[:, C_OFFDIAG:C_END],
                                            ALU.mult).then_inc(ns_done, 1)

            def keys(b, last):
                for j in range(NT + LAG):
                    i = b * NT + j
                    if j < NT:
                        k_bank, q_bank = K_BANKS[j % 2]
                        dve.wait_ge(ksq_done, i + 1)
                        if not (isinstance(i, int) and i == 0):
                            dve.wait_ge(krope_link, 3 * i - 2)
                        nc.vector.tensor_reduce(ssq[:, 0:NKV + 1], heads_view(sq[:], NKV + 1), AX_X, ALU.add).then_inc(kss_done, 1)
                        dve.wait_ge(krope_link, 3 * i)
                        rotate(0, ps[:, k_bank, :], NKV, 2, j)
                        rotate(NK, ps[:, q_bank, 0:HD], 1, 0, j)
                        partners(0, ps[:, k_bank, :], NKV, 2, j, None)
                        partners(NK, ps[:, q_bank, 0:HD], 1, 0, j, kt2_done)
                    elif j == NT and not last:
                        split_x(b + 1)
                    elif not last:
                        latent(b + 1)
                    if isinstance(b, int) and b == 0:
                        if j == 0:
                            rest_of_biases()
                        if j in (2, 3):
                            rest_of_wq(j - 2)
                    if last and j in FIRST_TOPK_KEYS:
                        topk(0, *FIRST_TOPK_KEYS[j])
                    if j >= LAG:
                        t, q = i - LAG, j - LAG
                        dve.wait_ge(s_mm, t + 1)
                        dve.wait_ge(s_out[q % 2], b * 32 + 16 * (q // 2))
                        w = P * q
                        if w:
                            nc.vector.tensor_copy(s_out_sb[:, q % 2, 0:w], ps[:, 2, 0:w])
                        nc.vector.tensor_tensor(s_out_sb[:, q % 2, w:w + P], ps[:, 2, w:w + P],
                                                con[:, C_CAUSAL:C_EYE], ALU.add).then_inc(s_ev, 1)

            batches(dve, keys, True)

            def store_mask(tb, qt):
                dve.wait_ge(mt_done, tb * NT + qt + 1)
                nc.vector.tensor_copy(nselT[:, 0:qt + 1, P * qt:P * (qt + 1)],
                                      x_ps.bitcast(BF16)[:, 0:P * (qt + 1)].rearrange("p (k q) -> p k q", q=P)).then_inc(mc_done, 1)

            def distances(tb, u_before):
                dve.wait_ge(mc_done, tb * NT + NT)
                dve.wait_ge(u_done, u_before)
                for kt in range(NT):
                    o = slice(OFF[kt], OFF[kt] + PIECE[kt])
                    m = nc.vector.scalar_tensor_tensor(D[:, o], nselT[:, kt, P * kt:T], BIG,
                                                       con[:, C_DIST + OFF[kt]:C_DIST + OFF[kt] + PIECE[kt]], ALU.mult, ALU.add)
                m.then_inc(D_done, 1)
                dve.wait_ge(D_done, tb + 1)

            def biased(b, s):
                n = b * STEPS + s
                dve.wait_ge(th_done, n + 1)
                nc.vector.scalar_tensor_tensor(th[:], D[:], -slope(s) / SOFTCAP, th[:], ALU.mult, ALU.add).then_inc(u_done, 1)

            def rotate_cos(m_, j):
                if isinstance(m_, int) and m_ < LEAD:
                    dve.wait_ge(ss_done, m_ + 1)
                else:
                    dve.wait_ge(sq_done, m_ - LEAD + 1)
                dve.wait_ge(rope_link, 3 * m_)
                rotate(0, z_ps, GROUP, 0, j, t1_done)

            def rotate_sin(m_, j):
                partners(0, z_ps, GROUP, 0, j, t2_done)

            def squares_summed(m_):
                dve.wait_ge(rope_link, 3 * m_)
                nc.vector.tensor_reduce(ssq[:, 0:GROUP], heads_view(sq[:, 0:NK], GROUP), AX_X, ALU.add).then_inc(ss_done, 1)

            def normalise(b, s):
                n = b * STEPS + s
                dve.wait_ge(pv_done, n + 1)
                dve.wait_ge(yq_done, n)
                nc.vector.reciprocal(den4[:, 0:NT - 1], y_ps[:, :, HD])
                nc.vector.reciprocal(den4[:, NT - 1:NT], y3_ps[:, HD:HD + 1]).then_inc(rden_link, 1)
                dve.wait_ge(rden_link, n + 1)
                dve.wait_ge(yt_done, n)
                nc.vector.tensor_tensor(yq[:, 0:NT - 1, :], y_ps[:, :, 0:HD],
                                        den4[:, 0:NT - 1].unsqueeze(2).broadcast_to([P, NT - 1, HD]), ALU.mult)
                nc.vector.tensor_scalar(yq[:, NT - 1, :], y3_ps[:, 0:HD], den4[:, NT - 1:NT], None, ALU.mult).then_inc(yq_done, 1)

            def gated(b, s):
                n = b * STEPS + s
                dve.wait_ge(gt_done, n + 1)
                dve.wait_ge(yn_done, n + 1)
                dve.wait_ge(wo_done, n)
                nc.vector.scalar_tensor_tensor(yg[:], gt[:], 1.0, yn[:], ALU.add, ALU.mult).then_inc(yg_done, 1)

            for m_ in range(LEAD):
                if m_ in FIRST_TOPK:
                    topk(0, *FIRST_TOPK[m_])
                rotate_cos(m_, m_ % NT)
                rotate_sin(m_, m_ % NT)
                if m_ in MASK_AFTER:
                    store_mask(0, MASK_AFTER[m_])
            distances(0, 0)
            biased(0, 0)

            def ternary(i):
                half, minus_half = wscale[:, i:i + 1], wscale[:, 2 + i:3 + i]
                dve.wait_ge(fsum_mm, i + 1)
                nc.vector.tensor_scalar(half, x_ps[:, 0:1], 1.0 / (DFF * DIM), QUANT_EPS, ALU.mult, ALU.max).then_inc(fscale_link, 1)
                dve.wait_ge(fscale_link, 2 * i + 1)
                nc.vector.tensor_scalar(minus_half, half, -0.5, None, ALU.mult)
                nc.vector.tensor_scalar(half, half, 0.5, None, ALU.mult).then_inc(fscale_link, 1)
                dve.wait_ge(fscale_link, 2 * i + 2)
                nc.vector.tensor_scalar(wscr, wraw, minus_half, None, ALU.is_lt).then_inc(ternary_link, 1)
                dve.wait_ge(ternary_link, i + 1)
                nc.vector.scalar_tensor_tensor(wql[:, i, :], wraw, half, wscr,
                                               ALU.is_gt, ALU.subtract).then_inc(ffnw_done, 1)

            def attended(b, j):
                return r1[:, bass.ds(b * NT + j, 1), :].rearrange("p a d -> p (a d)")

            def ln1_statistics(b):
                for j in range(NT):
                    m = nc.vector.bn_stats(stats[:, 0, j, :], attended(b, j))
                m.then_inc(ln1_link, 1)
                dve.wait_ge(ln1_link, b + 1)
                dve.wait_ge(fpool1_link, b)
                dve.sem_inc(passed_dve, 1)
                for j in range(NT):
                    m = nc.vector.bn_aggr(mv[:, 0, j, :], stats[:, 0, j, :])
                m.then_inc(st1_done, 1)

            def ln1(b):
                dve.wait_ge(frstd1_done, b + 1)
                dve.wait_ge(fxt_done, b * KD)
                for j in range(NT):
                    nc.vector.tensor_scalar(x1[:, j, :], attended(b, j), mv[:, 0, j, 0:1], rstd[:, j:j + 1],
                                            ALU.subtract, ALU.mult).then_inc(x1_done, 1)
                dve.wait_ge(x1_done, b * NT + NT)
                dve.sem_inc(passed_dve, 1)
                nc.vector.tensor_copy(r1[:, bass.ds(b * NT, NT), :], x1).then_inc(x1r_done, 1)

            def ln2_statistics(b):
                dve.wait_ge(r2_done, b * 2 + 2)
                for j in range(NT):
                    m = nc.vector.bn_stats(stats[:, 1, j, :], r2[:, j, :])
                m.then_inc(ln2_link, 1)
                dve.wait_ge(ln2_link, b + 1)
                dve.wait_ge(fpool2_link, b)
                dve.wait_ge(y_out, b * 16)
                dve.sem_inc(passed_dve, 1)
                for j in range(NT):
                    m = nc.vector.bn_aggr(mv[:, 1, j, :], stats[:, 1, j, :])
                m.then_inc(st2_done, 1)

            def ln2(b):
                dve.wait_ge(frstd2_done, b + 1)
                for j in range(NT):
                    nc.vector.tensor_scalar(ffn_y[:, j, :], r2[:, j, :], mv[:, 1, j, 0:1], rstd[:, 8 + j:9 + j],
                                            ALU.subtract, ALU.mult).then_inc(y_done, 1)

            def residual(b):
                dve.wait_ge(wo_done, b * STEPS + STEPS)
                dve.wait_ge(r1_in, 16)
                for a in range(2):
                    r = r1[:, bass.ds(b * NT + 2 * a, 2), :]
                    m = nc.vector.tensor_tensor(r, r, o_ps[:, a, :].rearrange("p (c d) -> p c d", c=2), ALU.add)
                m.then_inc(res_done, 1)

            def heads(b, last):
                first = isinstance(b, int) and b == 0
                for s in range(STEPS):
                    n = b * STEPS + s
                    if s >= 1:
                        gated(b, s - 1)
                    elif not first:
                        gated(b - 1, STEPS - 1)
                    if not last:
                        for part in EARLY.get(s, ()):
                            topk(b + 1, *part)
                        if s in TURN_AT:
                            store_mask(b + 1, TURN_AT[s])
                        if s == STEPS - 1:
                            distances(b + 1, n + 1)
                    if s + 1 < STEPS:
                        biased(b, s + 1)
                    elif not last:
                        biased(b + 1, 0)
                    normalise(b, s)
                    more = s + LEAD < STEPS or not last
                    if more:
                        rotate_cos(n + LEAD, (s + LEAD) % NT)
                        rotate_sin(n + LEAD, (s + LEAD) % NT)
                        squares_summed(n + LEAD)
                    if s == 0 and not first:
                        residual(b - 1)
                    if not last:
                        for part in LATE.get(s, ()):
                            topk(b + 1, *part)
                    if last and s in SCALE_AT:
                        ternary(SCALE_AT.index(s))
                    if last and s == STEPS - 2:
                        ln1_statistics(0)
                    if last and s == STEPS - 1:
                        ln1(0)
            batches(dve, heads, True)
            gated(B - 1, STEPS - 1)
            residual(B - 1)

            def split_x1(b):
                for k in range(KD):
                    dve.wait_ge(fxhi_done, b * KD + k + 1)
                    dve.wait_ge(h_mm, b * NF)
                    nc.vector.tensor_tensor(xl[:, k, :], ps[:, k, :], xh[:, k, :].bitcast(F32), ALU.subtract).then_inc(fxlo_done, 1)

            split_x1(0)

            def ffn(b, last):
                for f in range(NF):
                    i = b * NF + f
                    dve.wait_ge(h_done, i + 1)
                    dve.wait_ge(h2_done, i + 1)
                    if not (isinstance(i, int) and i < HSLOTS):
                        dve.wait_ge(f2_mm, i - HSLOTS + 1)
                    nc.vector.tensor_tensor(hr[:, f % HSLOTS, 1, :], hf[:, f % HSLOTS, :], hr[:, f % HSLOTS, 0, :].bitcast(F32),
                                            ALU.subtract).then_inc(hlo_done, 1)
                    if f == 1 and not (isinstance(b, int) and b == 0):
                        ln2(b - 1)
                    if f == 2 and not last:
                        ln1_statistics(b + 1)
                    if f == 4 and not last:
                        ln1(b + 1)
                if not last:
                    split_x1(b + 1)
                dve.wait_ge(f2_mm, b * NF + NF)
                dve.wait_ge(y_done, b * NT)
                dve.wait_ge(x1r_done, b + 1)
                for a in range(2):
                    nc.vector.tensor_tensor(r2[:, 2 * a:2 * a + 2, :], ps[:, 4 + a, :].rearrange("p (c d) -> p c d", c=2),
                                            r1[:, bass.ds(b * NT + 2 * a, 2), :], ALU.add).then_inc(r2_done, 1)
                ln2_statistics(b)

            batches(dve, ffn, True)
            ln2(B - 1)

        @block.gpsimd
        def _(pool):
            nc.gpsimd.memset(mhalf[:], -0.5).then_inc(setup_pool, 1)
            pool.wait_ge(setup_pool, 1)

            def keys(b, last):
                for j in range(NT):
                    i = b * NT + j
                    r = rstd[:, 8 * (j % 2):8 * (j % 2) + NKV + 1]
                    pool.wait_ge(kss_done, i + 1)
                    pool.wait_ge(krope_link, 3 * i)
                    pool.sem_inc(passed_pool, 1)
                    nc.gpsimd.tensor_scalar(msq[:, 0:NKV + 1], ssq[:, 0:NKV + 1], 1.0 / HD, RMS_EPS, ALU.mult,
                                            ALU.add).then_inc(krope_link, 1)
                    pool.wait_ge(krope_link, 3 * i + 1)
                    pool.wait_ge(kn_done, i - 1 if j else i)
                    nc.gpsimd.tensor_tensor(r, msq[:, 0:NKV + 1], mhalf[:, 0:NKV + 1], ALU.pow).then_inc(krope_link, 1)
                    pool.wait_ge(kt2_done, i + 1)
                    if not (isinstance(i, int) and i < 2):
                        pool.wait_ge(ktr_done, i - 1)
                    nc.gpsimd.tensor_tensor(QN[j % 2], t1[:], t2[:], ALU.add).then_inc(krope_link, 1)

            batches(pool, keys, True)

            def query_tile(m_):
                pool.wait_ge(ss_done, m_ + 1)
                pool.wait_ge(qn_done, m_)
                pool.sem_inc(passed_pool, 1)
                nc.gpsimd.tensor_scalar(msq[:, 0:GROUP], ssq[:, 0:GROUP], 1.0 / HD, RMS_EPS, ALU.mult,
                                        ALU.add).then_inc(rope_link, 1)
                pool.wait_ge(rope_link, 3 * m_ + 1)
                nc.gpsimd.tensor_tensor(rstd[:, 0:GROUP], msq[:, 0:GROUP], mhalf[:, 0:GROUP], ALU.pow).then_inc(rope_link, 1)
                pool.wait_ge(t2_done, m_ + 1)
                pool.wait_ge(tr_done, m_)
                nc.gpsimd.tensor_tensor(qn[:, 0:NK], t1[:, 0:NK], t2[:, 0:NK], ALU.add).then_inc(rope_link, 1)
                pool.wait_ge(rope_link, 3 * m_ + 3)
                nc.gpsimd.tensor_tensor(heads_view(qn[:, 0:NK], GROUP), heads_view(qn[:, 0:NK], GROUP),
                                        rstd[:, 0:GROUP].unsqueeze(2).broadcast_to([P, GROUP, HD]), ALU.mult).then_inc(qn_done, 1)

            pool.wait_ge(kn_done, B * NT)
            for m_ in range(LEAD - 1):
                query_tile(m_)

            def heads(b, last):
                for s in range(STEPS):
                    if s + LEAD - 1 < STEPS or not last:
                        query_tile(b * STEPS + s + LEAD - 1)

            batches(pool, heads, True)

            def rstd1(b):
                pool.wait_ge(st1_done, b + 1)
                pool.sem_inc(passed_pool, 1)
                nc.gpsimd.tensor_scalar(msq[:, 0:NT], mv[:, 0, :, 1], LN_EPS, None, ALU.add).then_inc(fpool1_link, 1)
                pool.wait_ge(fpool1_link, b + 1)
                nc.gpsimd.tensor_tensor(rstd[:, 0:NT], msq[:, 0:NT], mhalf[:, 0:NT], ALU.pow).then_inc(frstd1_done, 1)

            def rstd2(b):
                pool.wait_ge(st2_done, b + 1)
                pool.sem_inc(passed_pool, 1)
                nc.gpsimd.tensor_scalar(msq[:, 4:4 + NT], mv[:, 1, :, 1], LN_EPS, None, ALU.add).then_inc(fpool2_link, 1)
                pool.wait_ge(fpool2_link, b + 1)
                nc.gpsimd.tensor_tensor(rstd[:, 8:8 + NT], msq[:, 4:4 + NT], mhalf[:, 0:NT], ALU.pow).then_inc(frstd2_done, 1)

            rstd1(0)

            def ffn(b, last):
                if not last:
                    rstd1(b + 1)
                rstd2(b)

            batches(pool, ffn, True)


def kernel(**inputs):
    import concourse.bacc as bacc
    from concourse.bass_utils import run_bass_kernel_spmd

    a = {k[3:]: np.asarray(v) for k, v in inputs.items()}
    order, partner = np.array(ORDER), np.array(PARTNER)

    def by_head(v, n):
        h = v[..., :n * HD].reshape(*v.shape[:-1], n, HD)[..., order]
        return np.concatenate([h.reshape(*v.shape[:-1], n * HD), v[..., n * HD:]], -1)

    qn, kn = a["attn_qn_w"], a["attn_kn_w"]
    arrays = {
        "x": a["attn_x"],
        "w_q": by_head(a["attn_w_q"], HEADS),
        "w_down": a["attn_w_down"],
        "w_up": by_head(a["attn_w_up"], NKV),
        "w_o": a["attn_w_o"],
        "gate_w": a["attn_gate_w"],
        "w1": a["ffn_w1"].T,
        "w2": a["ffn_w2"].T,
        "biases": np.concatenate([by_head(a["attn_b_q"], HEADS), a["attn_b_o"], a["ffn_b2"],
                                  by_head(a["attn_b_up"], NKV)])[None],
        "gate_b": a["attn_gate_b"].T,
        "b_down": np.concatenate([a["attn_b_down"]] * 2)[:, None],
        "b1": a["ffn_b1"].reshape(NF, P).T,
        "norm_w": np.stack([qn[order], qn[partner], kn[order], kn[partner]]),
        "table": constants()[0],
        "trig": constants()[1],
    }
    arrays = {f"in_{k}": np.ascontiguousarray(v) for k, v in arrays.items()}
    nc = bacc.Bacc("TRN2", target_bir_lowering=False, num_devices=1)
    args = [nc.dram_tensor(k, v.shape, mybir.dt.from_np(v.dtype), kind="ExternalInput").ap() for k, v in arrays.items()]
    out = nc.dram_tensor("out", (B, T, DIM), F32, kind="ExternalOutput").ap()
    layer_program(nc, *args, out)
    r = run_bass_kernel_spmd(nc, [arrays], core_ids=[0])
    return r.results[0]["out"]
```

```python
from contextlib import ExitStack

import numpy as np

import concourse.bass as bass
from concourse import mybir

F32 = mybir.dt.float32
F32R = mybir.dt.float32r
BF16 = mybir.dt.bfloat16
ALU = mybir.AluOpType
ACT = mybir.ActivationFunctionType
AX_X = mybir.AxisListType.X

P = 128
B, T, DIM = 4, 512, 256
HEADS, HD = 16, 128
NKV = 4
GROUP = HEADS // NKV
LATENT = 64
TOPK = 64
SEL_DIM = 64
SOFTCAP = 30.0
RMS_EPS = 1e-6
LN_EPS = 1e-5
QUANT_EPS = 1e-8
DFF = 1024
NT = T // P
KD = DIM // P
NF = DFF // P
NQ = HEADS * HD
NK = NKV * HD
STEPS = HEADS
LEAD = 6
NTILES = B * HEADS
PIECE = [T - P * kt for kt in range(NT)]
OFF = [0, T, 2 * T, T + PIECE[1]]
CW = sum(PIECE)
BIG = 1.0e5
MASKED = -1.0e30
TAKEN = -3.0e38
ROUNDS = TOPK // 8
ORDER = [64 * a + 2 * i + c for a in range(2) for c in range(2) for i in range(32)]
PARTNER = [64 * a + 2 * i + 1 - c for a in range(2) for c in range(2) for i in range(32)]
C_DIST, C_CAUSAL, C_EYE, C_OFFDIAG = 0, CW, CW + P, CW + 2 * P
C_END = CW + 3 * P


def slope(h):
    start = 2.0 ** (-2.0 ** (-(np.log2(HEADS) - 3)))
    return float(start * start ** h)


def constants():
    t = np.zeros((P, C_END), np.float32)
    inv = (np.float32(1.0) / np.power(np.float32(10000.0), np.arange(0, HD, 2, dtype=np.float32) / np.float32(HD))).astype(np.float32)
    f = np.arange(T, dtype=np.float32)[:, None] * inv[None, :]
    emb = np.concatenate([f, f], -1)[:, 0::2].astype(np.float64)
    cos, sin = np.cos(emb), np.sin(emb)
    pair = np.array([ORDER[i] // 2 for i in range(HD)])
    odd = np.array([ORDER[i] % 2 for i in range(HD)])
    c = cos[:, pair]
    s = sin[:, pair] * np.where(odd, 1.0, -1.0)
    trig = np.stack([c, s]).reshape(2, NT, P, HD).transpose(2, 0, 1, 3).astype(np.float32)
    key = np.arange(P)[:, None]
    for kt in range(NT):
        d = np.arange(PIECE[kt])[None, :] - key
        t[:, C_DIST + OFF[kt]:C_DIST + OFF[kt] + PIECE[kt]] = np.where(d >= 0, d, BIG)
    t[:, C_CAUSAL:C_EYE] = np.where(np.arange(P)[None, :] > key, MASKED, 0.0)
    t[:, C_EYE:C_OFFDIAG] = np.eye(P)
    t[:, C_OFFDIAG:C_END] = 1.0 - np.eye(P)
    return t, trig


def layer_program(nc, x, w_q, w_down, w_up, w_o, gate_w, w1, w2, biases, gate_b, b_down, b1,
                  norm_w, table, trig, out):
    xs = nc.dram_tensor("xT_scratch", (B, P, 2, KD, T), F32, kind="Internal").ap()
    ks = nc.dram_tensor("kT_scratch", (B, P, NKV, T), F32, kind="Internal").ap()
    vs = nc.dram_tensor("v_scratch", (B, P, NT, NK), F32, kind="Internal").ap()
    ss = nc.dram_tensor("sel_scratch", (B, NT, P, T), F32, kind="Internal").ap()

    with ExitStack() as ctx:
        def sb(name, shape, dt=F32):
            return ctx.enter_context(nc.sbuf_tensor(name, shape, dt))

        def sem(name):
            return ctx.enter_context(nc.semaphore(name))

        wqh = sb("wq_hi", [P, KD, NQ], F32R)
        wql = sb("wq_lo", [P, KD, NQ], F32R)
        xh = sb("xT_hi", [P, KD, T], F32R)
        xl = sb("xT_lo", [P, KD, T], F32R)
        kT = sb("kT", [P, NKV, T])
        V = sb("V_and_twos", [P, NT, NKV, HD + 1])
        gw = sb("gate_w", [P, HEADS, HD])
        wol = sb("w_o_lo", [P, HEADS, DIM], F32R)
        qT = sb("qT", [P, 2, GROUP, T])
        D = sb("distance", [P, CW])
        nselT = sb("not_selected_T", [P, NT, T], BF16)
        nsel = sb("not_selected", [P, 2, T], BF16)
        work = sb("sel_work", [P, 2, T])
        th = sb("softcapped", [P, CW])
        pr = sb("probs", [P, 2, CW])
        sq = sb("squares", [P, NK + HD])
        t1 = sb("rot_cos", [P, NK + HD])
        t2 = sb("rot_sin", [P, NK + HD])
        qn = sb("rotated", [P, NK + HD])
        yn = sb("y_T", [P, T])
        yq = sb("y_rows", [P, NT, HD])
        gt = sb("gate_tanh", [P, T])
        yg = sb("y_gated", [P, T])
        ygh = sb("y_gated_hi", [P, T], F32R)
        ygl = sb("y_gated_lo", [P, T], F32R)
        r1 = sb("residual", [P, B * NT, DIM])
        con = sb("constants", [P, C_END])
        rope = sb("rope_tables", [P, 4, NT, HD])
        brow = sb("bias_rows", [64, NQ + 2 * DIM], F32R)
        onesr = sb("ones_r", [64, P], F32R)
        fw = sb("small_weights_r", [P, 4096], F32R)
        identb = sb("ident_bf16", [P, P], BF16)
        gb = sb("gate_bias_half", [P, HEADS])
        bd = sb("b_down", [P, 1])
        b1s = sb("b1", [P, NF])
        ssq = sb("sum_squares", [P, 8])
        msq = sb("mean_squares", [P, 8])
        rstd = sb("rstd", [P, 16])
        mhalf = sb("minus_half", [P, 8])
        den4 = sb("recip_den", [P, NT])
        top8 = sb("top8", [P, 8])
        stats = sb("bn_stats", [P, 2, NT, 6])
        mv = sb("mean_var", [P, 2, NT, 2])
        wsum = sb("w_abs_sums", [P, 2])
        wscale = sb("w_half_scale", [P, 4])
        onesq = sb("ones_square", [P, P])

        ident = con[:, C_EYE:C_OFFDIAG]
        stage = r1[:, :, :].rearrange("p a d -> p (a d)")
        prf = pr[:, :, :].rearrange("p a c -> p (a c)")
        up_in = prf[:, 0:2 * NK]
        down_in = prf[:, 2 * NK:2 * NK + KD * P].rearrange("p (k n) -> p k n", k=KD)
        xin = prf[:, CW:CW + NT * DIM].rearrange("p (j d) -> p j d", j=NT)
        braw = qT[0:1, :, :, :].rearrange("p a g t -> p (a g t)")
        s_out_sb = (gt[:, :], yq[:, :, :].rearrange("p j d -> p (j d)"))
        wA, wB = fw[:, 0:2 * NK], fw[:, 2 * NK:4 * NK]
        latA, latB = fw[:, 4 * NK:4 * NK + T], fw[:, 4 * NK + T:4 * NK + 2 * T]
        wdr = fw[:, 4 * NK + 2 * T:4 * NK + 2 * T + 2 * KD * P].rearrange("p (a k n) -> p a k n", a=2, k=KD)
        latf = yn[:, :]
        nw = gt[:, :].rearrange("p (w d) -> p w d", w=4)
        q0T = yg[:, :]
        LAG = 2
        QN = (qn[:, :], th[:, 0:NK + HD])
        T1 = (t1[:, :], prf[:, 0:NK + HD])
        T2 = (t2[:, :], prf[:, NK + HD:2 * (NK + HD)])
        K_BANKS = ((3, 5), (0, 1))
        woh = fw[:, :].rearrange("p (h n) -> p h n", h=HEADS)
        wo_raw = stage.rearrange("p (h n) -> p h n", h=HEADS)
        qT_flat = qT[:, :, :, :].rearrange("p a g t -> p (a g t)")
        wraw = rope[:, :, :, :].rearrange("p w j d -> p (w j d)")
        w1q = wql[:, 0, :].rearrange("p (k f) -> p k f", k=KD)
        w2q = wql[:, 1, :].rearrange("p (k n) -> p k n", k=NF)
        wscr = nselT[:, :, :].rearrange("p k t -> p (k t)")
        trig_in = D[:, 0:2 * NT * HD].rearrange("p (c j d) -> p c j d", c=2, j=NT)
        x1 = work[:, :, :].rearrange("p a (c d) -> p (a c) d", d=DIM)
        hr = wqh[:, :, :].rearrange("p s (a c t) -> p (s a) c t", a=2, c=2)
        HSLOTS, FFN_LAG = 4, 2
        H_BANKS = (2, 3, 6, 7)
        hf = prf[:, 0:HSLOTS * T].rearrange("p (s t) -> p s t", s=HSLOTS)
        gw_flat = gw[:, :, :].rearrange("p h e -> p (h e)")
        r2 = gw_flat[:, 0:NT * DIM].rearrange("p (j d) -> p j d", j=NT)
        ffn_y = gw_flat[:, NT * DIM:].rearrange("p (j d) -> p j d", j=NT)

        ps = ctx.enter_context(nc.psum_tensor("psum", [P, 8, 512], F32))
        sc_ps = ps[:, 0:3, :].rearrange("p a b -> p (a b)")
        z_ps, x_ps = ps[:, 3, :], ps[:, 4, :]
        y_ps = ps[:, 5, 0:(NT - 1) * (HD + 1)].rearrange("p (j d) -> p j d", j=NT - 1)
        y3_ps = x_ps[:, 0:HD + 1]
        o_ps = ps[:, 6:8, :]

        w_in = sem("w_in")
        con_in = sem("con_in")
        trig_loaded = sem("trig_loaded")
        misc_in = sem("misc_in")
        small_in = sem("small_in")
        braw_in = sem("braw_in")
        wo_in = sem("wo_in")
        gw_in = sem("gw_in")
        r1_in = sem("r1_in")
        x_in = sem("x_in")
        wq_split = sem("wq_split")
        setup_act = sem("setup_act")
        setup_dve = sem("setup_dve")
        setup_pool = sem("setup_pool")
        tables_done = sem("tables_done")
        rows_zeroed = sem("rows_zeroed")
        brow_done = sem("brow_done")
        brow_link = sem("brow_link")
        xtr_done = sem("xtr_done")
        xhi_done = sem("xhi_done")
        xlo_done = sem("xlo_done")
        lat_mm = sem("lat_mm")
        latf_done = sem("latf_done")
        latB_done = sem("latB_done")
        latA_link = sem("latA_link")
        latA_done = sem("latA_done")
        k_mm = sem("k_mm")
        v_mm = sem("v_mm")
        q0_mm = sem("q0_mm")
        ksq_done = sem("ksq_done")
        kss_done = sem("kss_done")
        kt2_done = sem("kt2_done")
        v_ev = sem("v_ev")
        krope_link = sem("krope_link")
        kn_done = sem("kn_done")
        ktr_done = sem("ktr_done")
        ktr_ev = sem("ktr_ev")
        s_mm = sem("s_mm")
        s_ev = sem("s_ev")
        xs_out = sem("xs_out")
        small_split = sem("small_split")
        ks_out = sem("ks_out")
        vs_out = sem("vs_out")
        qp_done = sem("qp_done")
        sq_done = sem("sq_done")
        ss_done = sem("ss_done")
        qadd_done = sem("qadd_done")
        t2_done = sem("t2_done")
        qn_done = sem("qn_done")
        rope_link = sem("rope_link")
        tr_done = sem("tr_done")
        qT_done = sem("qT_done")
        sc_done = sem("sc_done")
        th_done = sem("th_done")
        u_done = sem("u_done")
        p_done = sem("p_done")
        pv_done = sem("pv_done")
        rden_link = sem("rden_link")
        yq_done = sem("yq_done")
        yt_done = sem("yt_done")
        yn_done = sem("yn_done")
        gate_done = sem("gate_done")
        gt_done = sem("gt_done")
        yg_done = sem("yg_done")
        wo_done = sem("wo_done")
        wo_hi = sem("wo_hi")
        wo_split = sem("wo_split")
        ygh_done = sem("ygh_done")
        ygl_done = sem("ygl_done")
        res_done = sem("res_done")
        topk_link = sem("topk_link")
        ns_done = sem("ns_done")
        mt_done = sem("mt_done")
        mc_done = sem("mc_done")
        D_done = sem("D_done")
        fw_in = sem("fw_in")
        fabs_done = sem("fabs_done")
        fsum_mm = sem("fsum_mm")
        fscale_link = sem("fscale_link")
        ternary_link = sem("ternary_link")
        ffnw_done = sem("ffnw_done")
        ln1_link = sem("ln1_link")
        ln2_link = sem("ln2_link")
        st1_done = sem("st1_done")
        frstd1_done = sem("frstd1_done")
        fpool1_link = sem("fpool1_link")
        fpool2_link = sem("fpool2_link")
        x1r_done = sem("x1r_done")
        x1_done = sem("x1_done")
        fxt_done = sem("fxt_done")
        fxhi_done = sem("fxhi_done")
        fxlo_done = sem("fxlo_done")
        h_mm = sem("h_mm")
        h_done = sem("h_done")
        h2_done = sem("h2_done")
        hlo_done = sem("hlo_done")
        f2_mm = sem("f2_mm")
        r2_done = sem("r2_done")
        st2_done = sem("st2_done")
        frstd2_done = sem("frstd2_done")
        y_done = sem("y_done")
        y_out = sem("y_out")
        passed_dve = sem("passed_dve")
        passed_pool = sem("passed_pool")
        xT_in = [sem(f"xT_in{j}") for j in range(NT)]
        kT_in = [sem(f"kT_in{g}") for g in range(NKV)]
        v_in = [sem(f"v_in{g}") for g in range(NKV)]
        s_in = [sem(f"s_in{i}") for i in range(2)]
        s_out = [sem(f"s_out{i}") for i in range(2)]

        block = ctx.enter_context(nc.Block())

        def batches(eng, body, split_last):
            n = B - 1 if split_last else B
            body(0, False)
            with eng.Fori(1, n) as b:
                body(b, False)
            if split_last:
                body(B - 1, True)

        def heads_view(ap, h):
            return ap.rearrange("p (h d) -> p h d", h=h)

        def blocks_view(ap, h, c):
            return ap.rearrange("p (h a c i) -> p h a c i", h=h, a=2, c=2)[:, :, :, c, :]

        def table_blocks(which, j, c, h):
            v = rope[:, which, j, :].rearrange("p (a c i) -> p a c i", a=2, c=2)[:, :, c, :]
            return v.unsqueeze(1).broadcast_to([P, h, 2, 32])

        def query_bank(m):
            return ps[:, 5, :] if isinstance(m, int) and m < LEAD and m % 2 else z_ps

        first_masks = D[:].bitcast(BF16)[:, 0:NT * T].rearrange("p (k t) -> p k t", k=NT)

        def mask_rows(batch, qt):
            return first_masks[:, qt, :] if isinstance(batch, int) and batch == 0 else nsel[:, qt % 2, :]

        ALL = 2 * ROUNDS + 1
        EARLY = {1: [(0, 3, 7)], 2: [(0, 11, 15)], 3: [(1, 1, 4)], 4: [(1, 8, 11)], 5: [(1, 15, ALL)],
                 6: [(2, 3, 5)], 7: [(2, 8, 10)], 8: [(2, 13, 15)], 9: [(3, 1, 2)], 10: [(3, 4, 6)],
                 11: [(3, 8, 10)], 12: [(3, 12, 14)]}
        LATE = {0: [(0, 0, 3)], 1: [(0, 7, 11)], 2: [(0, 15, ALL), (1, 0, 1)], 3: [(1, 4, 8)], 4: [(1, 11, 15)],
                5: [(2, 0, 3)], 6: [(2, 5, 8)], 7: [(2, 10, 13)], 8: [(2, 15, ALL), (3, 0, 1)], 9: [(3, 2, 4)],
                10: [(3, 6, 8)], 11: [(3, 10, 12)], 12: [(3, 14, ALL)]}
        FIRST_HALVES = [(qt, h) for qt in range(NT) for h in range(2 * ROUNDS + 1)]
        PER_ITERATION = [0] + [6, 5, 5, 5, 3, 3] + [4, 4, 4, 4, 3, 3] + [4, 3, 3, 3, 3, 3]
        assert sum(PER_ITERATION) == len(FIRST_HALVES)
        MASK_AFTER = {1: 0, 2: 1, 3: 2, 4: 3}
        TURN_AT = {3: 0, 6: 1, 9: 2, 13: 3}
        TOPK_LINKS = 2 * ROUNDS + 1
        LN_AT = 10
        SCALE_AT = (12, 14)

        @block.sync
        def _(sp):
            def load_batch(b):
                sp.dma_start(xin, x[bass.ds(b, 1)].rearrange("a (j p) d -> p (a j) d", p=P)).then_inc(x_in, 16)

            load_batch(0)
            sp.dma_start(con[:], table).then_inc(con_in, 16)
            sp.dma_start(down_in[:, :, 0:LATENT], w_down.rearrange("(k p) n -> p k n", p=P)).then_inc(small_in, 16)
            sp.dma_start(down_in[:, :, LATENT:P], w_down.rearrange("(k p) n -> p k n", p=P)).then_inc(small_in, 16)
            sp.dma_start(up_in[0:LATENT, :], w_up).then_inc(small_in, 16)
            sp.dma_start(up_in[LATENT:P, :], w_up).then_inc(small_in, 16)
            sp.dma_start(bd[:], b_down).then_inc(small_in, 16)
            sp.dma_start(braw[:, 0:biases.shape[1]], biases).then_inc(braw_in, 16)
            sp.dma_start(trig_in, trig).then_inc(trig_loaded, 16)
            sp.dma_start(nw, norm_w.partition_broadcast(P)).then_inc(trig_loaded, 16)
            sp.dma_start(stage.rearrange("p (k n) -> p k n", k=KD),
                         w_q.rearrange("(k p) n -> p k n", p=P)).then_inc(w_in, 16)
            sp.dma_start(gb[:], gate_b).then_inc(misc_in, 16)
            sp.dma_start(b1s[:], b1).then_inc(misc_in, 16)
            sp.dma_start(gw[:], gate_w.rearrange("h d e -> d h e")).then_inc(gw_in, 16)

            def load_x(b, j):
                sp.dma_start(xh[:, :, P * j:P * (j + 1)].bitcast(F32),
                             xs[bass.ds(b, 1), :, 0, :, P * j:P * (j + 1)].rearrange("a p k t -> p (a k) t")).then_inc(xT_in[j], 16)
                sp.dma_start(xl[:, :, P * j:P * (j + 1)].bitcast(F32),
                             xs[bass.ds(b, 1), :, 1, :, P * j:P * (j + 1)].rearrange("a p k t -> p (a k) t")).then_inc(xT_in[j], 16)

            def load_s(b, qt):
                w = P * (qt + 1)
                sp.dma_start(work[:, qt % 2, 0:w],
                             ss[bass.ds(b, 1), qt, :, 0:w].rearrange("a p t -> (a p) t")).then_inc(s_in[qt % 2], 16)

            def keys(b, last):
                sp.wait_ge(xlo_done, b * KD + KD)
                sp.dma_start(xs[bass.ds(b, 1), :, 0].rearrange("a p k t -> p (a k) t"), xh[:].bitcast(F32)).then_inc(xs_out, 16)
                sp.dma_start(xs[bass.ds(b, 1), :, 1].rearrange("a p k t -> p (a k) t"), xl[:].bitcast(F32)).then_inc(xs_out, 16)
                if not last:
                    load_batch(b + 1)
                if b == 1:
                    sp.wait_ge(wq_split, KD + 1)
                    sp.dma_start(wo_raw, w_o.rearrange("(h d) n -> d h n", d=HD)).then_inc(wo_in, 16)
                for j in range(NT):
                    if b == 0 and j >= 2:
                        sp.wait_ge(s_out[j - 2], 16)
                        load_s(0, j - 2)
                    if b in (1, 2) and j == NT - 1:
                        sp.wait_ge(ns_done, b)
                        sp.wait_ge(s_out[(b + 1) % 2], 32)
                        load_s(0, b + 1)
                    if j == NT - 1:
                        sp.wait_ge(ktr_ev, b * NT + NT)
                        sp.dma_start(ks[bass.ds(b, 1)].rearrange("a p g t -> p (a g) t"), kT[:]).then_inc(ks_out, 16)
                    sp.wait_ge(s_ev, b * NT + j + 1)
                    sp.dma_start(ss[bass.ds(b, 1), j, :, 0:P * (j + 1)].rearrange("a p t -> (a p) t"),
                                 s_out_sb[j % 2][:, 0:P * (j + 1)]).then_inc(s_out[j % 2], 16)
                    if j == 1:
                        sp.wait_ge(v_ev, b * NT + NT)
                        sp.dma_start(vs[bass.ds(b, 1)].rearrange("a p k (g d) -> p (a k) g d", g=NKV),
                                     V[:, :, :, 0:HD]).then_inc(vs_out, 16)
                    if last and j == 1:
                        sp.wait_ge(xs_out, 32 * B)
                        sp.wait_ge(q0_mm, B * NT)
                        for t in range(NT):
                            load_x(0, t)

            for b in range(B):
                keys(b, b == B - 1)

            def load_k(b, g):
                sp.dma_start(kT[:, g, :], ks[bass.ds(b, 1), :, g].rearrange("a p t -> (a p) t")).then_inc(kT_in[g], 16)

            def load_v(b, g):
                sp.dma_start(V[:, :, g, 0:HD],
                             vs[bass.ds(b, 1), :, :, HD * g:HD * (g + 1)].rearrange("a p k n -> p (a k) n")).then_inc(v_in[g], 16)

            sp.wait_ge(xs_out, 32 * B)
            for i in range(2):
                sp.wait_ge(s_out[i], 16 * (NT // 2) * B)
            sp.wait_ge(vs_out, 16 * B)
            sp.wait_ge(ks_out, 16 * B)
            load_k(0, 0)
            load_v(0, 0)
            for g in range(1, NKV):
                load_k(0, g)
                load_v(0, g)
            for i in range(2):
                sp.wait_ge(ns_done, 3 + i)
                load_s(1, i)
            sp.wait_ge(wo_split, NKV)
            sp.dma_start(r1[:], x.rearrange("b (j p) d -> p (b j) d", p=P)).then_inc(r1_in, 16)

            def heads(b, last):
                if last:
                    return
                n = b * STEPS
                if not (isinstance(b, int) and b == 0):
                    sp.wait_ge(ns_done, b * NT + 3)
                    load_s(b + 1, 0)
                    sp.wait_ge(ns_done, b * NT + 4)
                    load_s(b + 1, 1)
                sp.wait_ge(sc_done, n + 4)
                load_k(b + 1, 0)
                sp.wait_ge(ns_done, b * NT + NT + 1)
                load_s(b + 1, 2)
                sp.wait_ge(pv_done, n + 4)
                load_v(b + 1, 0)
                sp.wait_ge(ns_done, b * NT + NT + 2)
                load_s(b + 1, 3)
                for j in range(NT):
                    sp.wait_ge(qp_done, n + 12 + j + 1)
                    load_x(b + 1, j)
                    if j == 1:
                        sp.wait_ge(sc_done, n + 8)
                        load_k(b + 1, 1)
                        sp.wait_ge(pv_done, n + 8)
                        load_v(b + 1, 1)
                for g in range(2, NKV):
                    sp.wait_ge(sc_done, n + GROUP * (g + 1))
                    load_k(b + 1, g)
                    sp.wait_ge(pv_done, n + GROUP * (g + 1))
                    load_v(b + 1, g)

            batches(sp, heads, True)

            sp.wait_ge(t2_done, NTILES)
            sp.dma_start(wraw.rearrange("p (k f) -> p k f", k=KD),
                         w1.rearrange("(k p) f -> p k f", p=P)).then_inc(fw_in, 16)
            sp.wait_ge(ffnw_done, 1)
            sp.dma_start(wraw.rearrange("p (k n) -> p k n", k=NF),
                         w2.rearrange("(k p) n -> p k n", p=P)).then_inc(fw_in, 16)

            def ffn(b, last):
                sp.wait_ge(y_done, b * NT + NT)
                sp.dma_start(out[bass.ds(b, 1)].rearrange("a (j p) d -> p (a j) d", p=P),
                             ffn_y).then_inc(y_out, 16)

            batches(sp, ffn, False)
            sp.wait_ge(y_out, 16 * B)

        @block.tensor
        def _(pe):
            def mm(o, lhsT, rhs, start, stop):
                return pe.matmul(o, lhsT, rhs, start=start, stop=stop, skip_group_check=True)

            def project(o, cols, j, bias_cols):
                tok = slice(P * j, P * (j + 1))
                for k in range(KD):
                    mm(o, xh[:, k, tok], wqh[:, k, cols], k == 0, False)
                    mm(o, xl[:, k, tok], wqh[:, k, cols], False, False)
                    mm(o, xh[:, k, tok], wql[:, k, cols], False, False)
                return mm(o, onesr[:], brow[:, bias_cols], False, True)

            pe.wait_ge(con_in, 16)

            def turn_x(b):
                pe.wait_ge(x_in, b * 16 + 16)
                pe.wait_ge(xlo_done, b * KD)
                pe.wait_ge(kt2_done, b * NT)
                for k in range(KD):
                    for j in range(NT):
                        m = pe.transpose(ps[:, k, P * j:P * (j + 1)], xin[:, j, P * k:P * (k + 1)], ident)
                    m.then_inc(xtr_done, 1)

            def latent(b):
                pe.wait_ge(xlo_done, b * KD + KD)
                for k in range(KD):
                    mm(ps[:, 5, :], wdr[:, 0, k, :], xh[:, k, :], k == 0, False)
                    mm(ps[:, 5, :], wdr[:, 1, k, :], xh[:, k, :], False, False)
                    m = mm(ps[:, 5, :], wdr[:, 0, k, :], xl[:, k, :], False, k == KD - 1)
                m.then_inc(lat_mm, 1)

            turn_x(0)
            pe.wait_ge(small_split, 1)
            latent(0)
            pe.wait_ge(setup_act, 3)
            pe.wait_ge(wq_split, 1)
            pe.wait_ge(brow_done, 3)

            def query(b, s, m_):
                j, u = s % NT, s // NT
                pe.wait_ge(xT_in[j], b * 32 + 32)
                if isinstance(m_, int) and m_ < LEAD:
                    pe.wait_ge(kt2_done, B * NT)
                    if m_ >= 2:
                        pe.wait_ge(t2_done, m_ - 1)
                else:
                    pe.wait_ge(gt_done, m_ - LEAD)
                    pe.wait_ge(t2_done, m_)
                cols = slice(GROUP * HD * u, GROUP * HD * (u + 1))
                project(query_bank(m_), cols, j, cols).then_inc(qp_done, 1)

            def selection_scores(b, j):
                t = b * NT + j
                pe.wait_ge(ktr_ev, t + 1)
                pe.wait_ge(s_ev, t)
                mm(ps[:, 2, 0:P * (j + 1)], q0T[0:SEL_DIM, P * j:P * (j + 1)], kT[0:SEL_DIM, 0, 0:P * (j + 1)],
                   True, True).then_inc(s_mm, 1)

            def keys(b, last):
                pe.wait_ge(latA_done, b + 1)
                pe.wait_ge(latB_done, b + 1)
                for j in range(NT + LAG):
                    i = b * NT + j
                    tok = slice(P * j, P * (j + 1))
                    if j == NT + 1 and not last:
                        latent(b + 1)
                    if j < NT:
                        k_bank, q_bank = K_BANKS[j % 2]
                        if not (isinstance(i, int) and i < 2):
                            pe.wait_ge(kt2_done, i - 1)
                        mm(ps[:, k_bank, :], latA[:, tok], wA[:, 0:NK], True, False)
                        mm(ps[:, k_bank, :], latB[:, tok], wB[:, 0:NK], False, True).then_inc(k_mm, 1)
                    if j >= LAG:
                        t = i - LAG
                        pe.wait_ge(kn_done, t + 1)
                        pe.wait_ge(ktr_ev, t)
                        rotated = QN[j % 2]
                        for g in range(NKV):
                            pe.transpose(ps[:, 6, P * g:P * (g + 1)], rotated[:, HD * g:HD * (g + 1)], ident)
                        pe.transpose(ps[:, 7, 0:P], rotated[:, NK:NK + HD], ident).then_inc(ktr_done, 1)
                    if j < NT:
                        project(ps[:, q_bank, 0:HD], slice(0, HD), j, slice(0, HD)).then_inc(q0_mm, 1)
                        pe.wait_ge(v_ev, i)
                        mm(ps[:, 4, :], latA[:, tok], wA[:, NK:2 * NK], True, False)
                        mm(ps[:, 4, :], latB[:, tok], wB[:, NK:2 * NK], False, True).then_inc(v_mm, 1)
                    elif j == NT and not last:
                        turn_x(b + 1)
                    if LAG <= j <= NT or last and j > NT:
                        selection_scores(b, j - LAG)
                    if j == 0 and b >= 1:
                        selection_scores(b - 1, NT - 1)
                    if last and j >= NT:
                        if j == NT:
                            pe.wait_ge(brow_done, 4)
                            pe.wait_ge(wq_split, KD + 1)
                        query(0, j - NT, j - NT)

            for b in range(B):
                keys(b, b == B - 1)

            def scores(b, s):
                g, n = s // GROUP, b * STEPS + s
                pe.wait_ge(qT_done, b * STEPS + GROUP * (g + 1))
                pe.wait_ge(kT_in[g], b * 16 + 16)
                pe.wait_ge(th_done, n)
                for kt in range(NT):
                    m = mm(sc_ps[:, OFF[kt]:OFF[kt] + PIECE[kt]], kT[:, g, P * kt:P * (kt + 1)],
                           qT[:, g % 2, s % GROUP, P * kt:T], True, True)
                m.then_inc(sc_done, 1)

            def values(b, s, last):
                g, n = s // GROUP, b * STEPS + s
                pe.wait_ge(p_done, n + 1)
                pe.wait_ge(v_in[g], b * 16 + 16)
                pe.wait_ge(yq_done, n)
                for qt in range(NT):
                    if qt == NT - 1:
                        pe.wait_ge(qT_done, n + LEAD - 1 if not last or s + LEAD - 1 <= STEPS else NTILES)
                        if s in TURN_AT and not last:
                            pe.wait_ge(mc_done, b * NT + NT + TURN_AT[s] + 1)
                    for kt in range(qt + 1):
                        q = OFF[kt] + P * (qt - kt)
                        m = mm(y_ps[:, qt, :] if qt < NT - 1 else y3_ps, pr[:, s % 2, q:q + P], V[:, kt, g, :],
                               kt == 0, kt == qt)
                m.then_inc(pv_done, 1)

            def turn_y(b, s):
                n = b * STEPS + s
                pe.wait_ge(yq_done, n + 1)
                for qt in range(NT):
                    m = pe.transpose(x_ps[:, P * qt:P * (qt + 1)], yq[:, qt, :], ident)
                m.then_inc(yt_done, 1)

            def output(b, s, part):
                n = b * STEPS + s
                if s == 0 and part == 0:
                    pe.wait_ge(res_done, b)
                    for a in range(2):
                        mm(o_ps[:, a, :].rearrange("p (c d) -> p c d", c=2), onesr[:],
                           brow[:, NQ:NQ + DIM].unsqueeze(1).broadcast_to([64, 2, DIM]), True, False)
                pe.wait_ge(ygl_done, n + 1)
                for j in ((0,), (1, 2, 3))[part]:
                    o, tok = o_ps[:, j // 2, DIM * (j % 2):DIM * (j % 2 + 1)], slice(P * j, P * (j + 1))
                    mm(o, ygh[:, tok], woh[:, s, :], False, False)
                    mm(o, ygl[:, tok], woh[:, s, :], False, False)
                    m = mm(o, ygh[:, tok], wol[:, s, :], False, s == STEPS - 1)
                if part:
                    m.then_inc(wo_done, 1)

            def turn_queries(m_, after):
                pe.wait_ge(qn_done, m_ + 1)
                pe.wait_ge(qT_done, m_)
                pe.wait_ge(yn_done, after)
                for h in range(GROUP):
                    m = pe.transpose(x_ps[:, P * h:P * (h + 1)], qn[:, HD * h:HD * (h + 1)], ident)
                m.then_inc(tr_done, 1)

            def gate(b, s, last):
                n = b * STEPS + s
                if isinstance(n, int) and n == 0:
                    pe.wait_ge(gw_in, 16)
                pe.wait_ge(yn_done, n + 1)
                pe.wait_ge(t2_done, n + LEAD + 1 if not last or s + LEAD < STEPS else NTILES)
                mm(z_ps, gw[:, s, :], yn[:], True, True).then_inc(gate_done, 1)

            def turn_x1(b):
                pe.wait_ge(x1_done, b * NT + NT)
                pe.wait_ge(fxlo_done, b * KD)
                for k in range(KD):
                    for j in range(NT):
                        m = pe.transpose(ps[:, k, P * j:P * (j + 1)], x1[:, j, P * k:P * (k + 1)], ident)
                    m.then_inc(fxt_done, 1)

            def turn_mask(tile, qt, evacs):
                pe.wait_ge(ns_done, tile + 1)
                pe.wait_ge(qT_done, evacs)
                xb = x_ps.bitcast(BF16)
                mask = mask_rows(0 if isinstance(tile, int) and tile < NT else 1, qt)
                for kt in range(qt + 1):
                    m = pe.transpose(xb[:, P * kt:P * (kt + 1)], mask[:, P * kt:P * (kt + 1)], identb[:])
                m.then_inc(mt_done, 1)

            pe.wait_ge(v_ev, B * NT)
            for m_ in range(LEAD):
                if m_ >= LAG:
                    query(0, m_, m_)
                if m_ >= 1:
                    pe.wait_ge(mc_done, sum(k < m_ for k in MASK_AFTER))
                    turn_queries(m_ - 1, 0)
                    if m_ in MASK_AFTER:
                        if m_ == 1:
                            pe.wait_ge(setup_dve, 1)
                        turn_mask(MASK_AFTER[m_], MASK_AFTER[m_], m_)
                    if m_ == NT:
                        scores(0, 0)

            def heads(b, last):
                first = isinstance(b, int) and b == 0
                for s in range(STEPS):
                    n = b * STEPS + s
                    if s + 1 < STEPS:
                        scores(b, s + 1)
                    elif not last:
                        scores(b + 1, 0)
                    if s == 0 and first:
                        pe.wait_ge(t2_done, LEAD)
                    if s == 1 and first:
                        pe.wait_ge(wo_split, NKV)
                    if s in TURN_AT and not last:
                        turn_mask(b * NT + NT + TURN_AT[s], TURN_AT[s], n + LEAD - 1)
                    values(b, s, last)
                    if s + LEAD < STEPS:
                        query(b, s + LEAD, n + LEAD)
                    elif not last:
                        query(b + 1, s + LEAD - STEPS, n + LEAD)
                    if s >= 1:
                        output(b, s - 1, 0)
                    elif not first:
                        output(b - 1, STEPS - 1, 0)
                    if last and s in SCALE_AT:
                        i = SCALE_AT.index(s)
                        pe.wait_ge(fabs_done, i + 1)
                        pe.wait_ge(yq_done, n + 1)
                        mm(x_ps[:, 0:1], onesq[:], wsum[:, i:i + 1], True, True).then_inc(fsum_mm, 1)
                        pe.wait_ge(fscale_link, 2 * i + 1)
                    turn_y(b, s)
                    if s >= 1:
                        output(b, s - 1, 1)
                    elif not first:
                        output(b - 1, STEPS - 1, 1)
                    if s + LEAD - 1 < STEPS or not last:
                        turn_queries(n + LEAD - 1, n + 1)
                    if last and s == STEPS - 1:
                        pe.wait_ge(th_done, NTILES)
                        turn_x1(0)
                    gate(b, s, last)

            batches(pe, heads, True)

            pe.wait_ge(ffnw_done, 2)
            pe.wait_ge(yq_done, NTILES)

            def ffn(b, last):
                pe.wait_ge(fxlo_done, b * KD + KD)
                for f in range(NF + FFN_LAG):
                    i = b * NF + f
                    if f < NF:
                        if f == 1 and isinstance(b, int) and b == 0:
                            pe.wait_ge(gt_done, NTILES)
                        if f == 2 and isinstance(b, int) and b == 0:
                            output(B - 1, STEPS - 1, 0)
                            output(B - 1, STEPS - 1, 1)
                            pe.wait_ge(res_done, B)
                        if not (isinstance(i, int) and i < HSLOTS):
                            pe.wait_ge(h2_done, i - HSLOTS + 1)
                        for k in range(KD):
                            mm(ps[:, H_BANKS[f % HSLOTS], :], w1q[:, k, P * f:P * (f + 1)], xh[:, k, :], k == 0, False)
                            m = mm(ps[:, H_BANKS[f % HSLOTS], :], w1q[:, k, P * f:P * (f + 1)], xl[:, k, :], False, k == KD - 1)
                        m.then_inc(h_mm, 1)
                    elif f == NF and not last:
                        turn_x1(b + 1)
                    if f == FFN_LAG:
                        pe.wait_ge(r2_done, b * 2)
                        for a in range(2):
                            mm(ps[:, 4 + a, :].rearrange("p (c d) -> p c d", c=2), onesr[:],
                               brow[:, NQ + DIM:NQ + 2 * DIM].unsqueeze(1).broadcast_to([64, 2, DIM]), True, False)
                    if f >= FFN_LAG:
                        g = f - FFN_LAG
                        pe.wait_ge(hlo_done, i - FFN_LAG + 1)
                        for j in range(NT):
                            for part in range(2):
                                m = mm(ps[:, 4 + j // 2, DIM * (j % 2):DIM * (j % 2 + 1)],
                                       hr[:, g % HSLOTS, part, P * j:P * (j + 1)], w2q[:, g, :], False, g == NF - 1)
                        m.then_inc(f2_mm, 1)

            batches(pe, ffn, True)

        @block.scalar
        def _(act):
            def split_wq(k, cols):
                nc.scalar.activation(wqh[:, k, cols], stage[:, NQ * k + cols.start:NQ * k + cols.stop], ACT.Copy).then_inc(setup_act, 1)

            def split_x(b):
                act.wait_ge(xs_out, b * 32)
                act.wait_ge(q0_mm, b * NT)
                for k in range(KD):
                    act.wait_ge(xtr_done, b * KD + k + 1)
                    nc.scalar.activation(xh[:, k, :], ps[:, k, :], ACT.Copy).then_inc(xhi_done, 1)

            act.wait_ge(small_in, 16 * 5)
            nc.scalar.activation(wdr[:, 0], down_in, ACT.Copy).then_inc(setup_act, 1)
            split_x(0)
            nc.scalar.activation(wA, up_in, ACT.Copy).then_inc(setup_act, 1)

            def latent(b):
                act.wait_ge(lat_mm, b + 1)
                act.wait_ge(latA_done, b)
                act.wait_ge(latB_done, b)
                nc.scalar.activation(latf, ps[:, 5, :], ACT.Identity, bias=bd[:]).then_inc(latf_done, 1)
                act.wait_ge(latf_done, b + 1)
                act.wait_ge(v_mm, b * NT)
                nc.scalar.activation(latB[0:LATENT, :], latf[0:LATENT, :], ACT.Copy).then_inc(latB_done, 1)

            latent(0)
            act.wait_ge(w_in, 16)
            nc.scalar.activation(wqh[:, :, 0:HD], stage.rearrange("p (k n) -> p k n", k=KD)[:, :, 0:HD],
                                 ACT.Copy).then_inc(setup_act, 1)

            def sums_of_squares(m_):
                act.wait_ge(qp_done, m_ + 1)
                if m_ == 0:
                    act.wait_ge(kss_done, B * NT)
                    act.wait_ge(krope_link, 3 * B * NT - 2)
                else:
                    act.wait_ge(rope_link, 3 * m_ - 2)
                act.wait_ge(ss_done, m_)
                for h in range(GROUP):
                    m = nc.scalar.activation(sq[:, HD * h:HD * (h + 1)], query_bank(m_)[:, HD * h:HD * (h + 1)], ACT.Square,
                                             accum_out=ssq[:, h:h + 1])
                m.then_inc(ss_done, 1)


            def keys(b, last):
                for j in range(NT + LAG):
                    i = b * NT + j
                    if j == NT + 1 and not last:
                        latent(b + 1)
                    if j < NT:
                        k_bank, q_bank = K_BANKS[j % 2]
                        act.wait_ge(k_mm, i + 1)
                        act.wait_ge(kss_done, i)
                        if i >= 1:
                            act.wait_ge(krope_link, 3 * i - 2)
                        for h in range(NKV):
                            m = nc.scalar.activation(sq[:, HD * h:HD * (h + 1)], ps[:, k_bank, HD * h:HD * (h + 1)], ACT.Square,
                                                 accum_out=ssq[:, h:h + 1])
                        m.then_inc(ksq_done, 1)
                    if j >= LAG:
                        t = i - LAG
                        act.wait_ge(ktr_done, t + 1)
                        act.wait_ge(ks_out, b * 16)
                        act.wait_ge(s_mm, t)
                        tok = slice(P * (j - LAG), P * (j - LAG + 1))
                        nc.scalar.activation(kT[:, :, tok], heads_view(ps[:, 6, :], NKV), ACT.Copy)
                        nc.scalar.activation(q0T[:, tok], ps[:, 7, 0:P], ACT.Copy).then_inc(ktr_ev, 1)
                    if j == NT and not last:
                        split_x(b + 1)
                    if 1 <= j <= NT:
                        act.wait_ge(krope_link, 3 * i)
                        rotated = QN[(j - 1) % 2]
                        for h in range(NKV + 1):
                            m = nc.scalar.mul(rotated[:, HD * h:HD * (h + 1)], rotated[:, HD * h:HD * (h + 1)],
                                              rstd[:, 8 * ((j - 1) % 2) + h:8 * ((j - 1) % 2) + h + 1])
                        m.then_inc(kn_done, 1)
                    if j < NT:
                        act.wait_ge(q0_mm, i + 1)
                        nc.scalar.activation(sq[:, NK:], ps[:, q_bank, 0:HD], ACT.Square,
                                             accum_out=ssq[:, NKV:NKV + 1]).then_inc(kss_done, 1)
                        act.wait_ge(v_mm, i + 1)
                        act.wait_ge(vs_out, b * 16)
                        nc.scalar.activation(V[:, j, :, 0:HD], heads_view(ps[:, 4, :], NKV), ACT.Copy).then_inc(v_ev, 1)
                    if last and j >= NT:
                        sums_of_squares(j - NT)
                    if b == 0 and 1 <= j <= KD:
                        split_wq(j - 1, slice(HD, NQ))

            for b in range(B):
                keys(b, b == B - 1)

            def softcap(b, s):
                n = b * STEPS + s
                act.wait_ge(sc_done, n + 1)
                act.wait_ge(p_done, n)
                nc.scalar.activation(th[:], sc_ps[:, 0:CW], ACT.Tanh,
                                     scale=1.0 / (SOFTCAP * HD ** 0.5)).then_inc(th_done, 1)

            def exps(b, s):
                n = b * STEPS + s
                act.wait_ge(u_done, n + 1)
                if not (isinstance(n, int) and n < 2):
                    act.wait_ge(pv_done, n - 1)
                nc.scalar.activation(pr[:, s % 2, :], th[:], ACT.Exp, scale=SOFTCAP).then_inc(p_done, 1)

            def squares(m_):
                act.wait_ge(qp_done, m_ + 1)
                act.wait_ge(ss_done, m_)
                nc.scalar.activation(sq[:, 0:NK], z_ps, ACT.Square).then_inc(sq_done, 1)

            def store_y(b, s):
                n = b * STEPS + s
                act.wait_ge(yt_done, n + 1)
                act.wait_ge(gate_done, n)
                act.wait_ge(yg_done, n)
                nc.scalar.activation(yn[:], x_ps, ACT.Copy).then_inc(yn_done, 1)

            def store_queries(m_, u, j, scores_before):
                act.wait_ge(tr_done, m_ + 1)
                act.wait_ge(sc_done, scores_before)
                nc.scalar.activation(qT[:, u % 2, :, P * j:P * (j + 1)], heads_view(x_ps, GROUP),
                                     ACT.Copy).then_inc(qT_done, 1)

            def gated_hi(b, s):
                n = b * STEPS + s
                act.wait_ge(yg_done, n + 1)
                act.wait_ge(wo_done, n)
                nc.scalar.activation(ygh[:], yg[:], ACT.Copy).then_inc(ygh_done, 1)

            def split_x1(b):
                for k in range(KD):
                    act.wait_ge(fxt_done, b * KD + k + 1)
                    act.wait_ge(h_mm, b * NF)
                    nc.scalar.activation(xh[:, k, :], ps[:, k, :], ACT.Copy).then_inc(fxhi_done, 1)

            def gate_tanh(b, s):
                n = b * STEPS + s
                act.wait_ge(gate_done, n + 1)
                act.wait_ge(yg_done, n)
                nc.scalar.activation(gt[:], z_ps, ACT.Tanh, bias=gb[:, s:s + 1]).then_inc(gt_done, 1)

            act.wait_ge(misc_in, 32)
            nc.scalar.mul(gb[:], gb[:], 0.5).then_inc(setup_act, 1)
            act.wait_ge(setup_act, 3 + KD + 1)
            for m_ in range(LEAD):
                if m_ >= LAG:
                    sums_of_squares(m_)
                if m_ >= 1:
                    store_queries(m_ - 1, (m_ - 1) // NT, (m_ - 1) % NT, 0)
                if m_ >= LAG:
                    g = slice(GROUP * (m_ - LAG), GROUP * (m_ - LAG + 1))
                    if m_ == LAG:
                        act.wait_ge(wo_in, 16)
                        act.wait_ge(v_mm, B * NT)
                    nc.scalar.activation(woh[:, g, :], wo_raw[:, g, :], ACT.Copy).then_inc(wo_hi, 1)
                if m_ == NT:
                    softcap(0, 0)
            exps(0, 0)

            def heads(b, last):
                first = isinstance(b, int) and b == 0
                for s in range(STEPS):
                    n = b * STEPS + s
                    if s >= 1:
                        gated_hi(b, s - 1)
                    elif not first:
                        gated_hi(b - 1, STEPS - 1)
                    if s + 1 < STEPS:
                        softcap(b, s + 1)
                    elif not last:
                        softcap(b + 1, 0)
                    if last and s in SCALE_AT:
                        i = SCALE_AT.index(s)
                        act.wait_ge(fw_in, 16 * i + 16)
                        act.wait_ge(D_done, B)
                        act.wait_ge(ternary_link, i)
                        nc.scalar.activation(wscr, wraw, ACT.Abs, accum_out=wsum[:, i:i + 1]).then_inc(fabs_done, 1)
                    if s + LEAD < STEPS or not last:
                        squares(n + LEAD)
                    store_y(b, s)
                    if s + 1 < STEPS:
                        exps(b, s + 1)
                    elif not last:
                        exps(b + 1, 0)
                    if s + LEAD - 1 < STEPS or not last:
                        m_ = s + LEAD - 1
                        store_queries(n + LEAD - 1, m_ // NT, m_ % NT, b * STEPS + NT * (m_ // NT) - NT)
                    if last and s == STEPS - 1:
                        split_x1(0)
                    gate_tanh(b, s)

            batches(act, heads, True)
            gated_hi(B - 1, STEPS - 1)

            def ffn(b, last):
                for f in range(NF):
                    i = b * NF + f
                    act.wait_ge(h_mm, i + 1)
                    if not (isinstance(i, int) and i < HSLOTS):
                        act.wait_ge(hlo_done, i - HSLOTS + 1)
                    nc.scalar.activation(hf[:, f % HSLOTS, :], ps[:, H_BANKS[f % HSLOTS], :], ACT.Gelu, bias=b1s[:, f:f + 1]).then_inc(h_done, 1)
                    if not (isinstance(i, int) and i < HSLOTS):
                        act.wait_ge(f2_mm, i - HSLOTS + 1)
                    nc.scalar.activation(hr[:, f % HSLOTS, 0, :], ps[:, H_BANKS[f % HSLOTS], :], ACT.Gelu, bias=b1s[:, f:f + 1]).then_inc(h2_done, 1)
                if not last:
                    split_x1(b + 1)

            batches(act, ffn, True)

        @block.vector
        def _(dve):
            nc.vector.memset(V[:, :, :, HD:HD + 1], 2.0)
            nc.vector.memset(wB[LATENT:P, :].bitcast(F32), 0.0)
            nc.vector.memset(latB[LATENT:P, :].bitcast(F32), 1.0)
            nc.vector.memset(onesr[:].bitcast(F32), 1.0)
            nc.vector.memset(onesq[:], 1.0)
            nc.vector.memset(brow[:].bitcast(F32), 0.0).then_inc(rows_zeroed, 1)
            dve.wait_ge(con_in, 16)
            nc.vector.tensor_copy(identb[:], ident).then_inc(setup_dve, 1)
            dve.wait_ge(setup_act, 1)
            nc.vector.tensor_tensor(wdr[:, 1], down_in, wdr[:, 0].bitcast(F32), ALU.subtract).then_inc(small_split, 1)

            def split_x(b):
                for k in range(KD):
                    dve.wait_ge(xhi_done, b * KD + k + 1)
                    nc.vector.tensor_tensor(xl[:, k, :], ps[:, k, :], xh[:, k, :].bitcast(F32), ALU.subtract).then_inc(xlo_done, 1)

            split_x(0)
            NB = NQ + 2 * DIM
            b_up = braw[:, NB:NB + 2 * NK]
            b_up_hi = work[0:1, :, :].rearrange("p a t -> p (a t)")
            dve.wait_ge(braw_in, 16)
            dve.wait_ge(rows_zeroed, 1)
            nc.vector.tensor_copy(wB[64:65, :], b_up)
            nc.vector.tensor_copy(brow[0:1, 0:HD], braw[:, 0:HD]).then_inc(brow_done, 1)
            dve.wait_ge(brow_done, 1)
            nc.vector.tensor_tensor(brow[32:33, 0:HD], braw[:, 0:HD], brow[0:1, 0:HD].bitcast(F32), ALU.subtract)
            nc.vector.tensor_copy(b_up_hi, wB[64:65, :].bitcast(F32)).then_inc(brow_done, 1)
            dve.wait_ge(setup_act, 2)
            nc.vector.tensor_tensor(wB[0:LATENT, :], up_in[0:LATENT, :], wA[0:LATENT, :].bitcast(F32), ALU.subtract)
            dve.wait_ge(brow_done, 2)
            nc.vector.tensor_tensor(wB[96:97, :], b_up, b_up_hi, ALU.subtract).then_inc(brow_done, 1)

            def latent(b):
                dve.wait_ge(latf_done, b + 1)
                dve.wait_ge(v_mm, b * NT)
                nc.vector.tensor_copy(latA, latf).then_inc(latA_link, 1)
                dve.wait_ge(latA_link, b + 1)
                nc.vector.tensor_tensor(latA[LATENT:P, :], latf[LATENT:P, :], latA[LATENT:P, :].bitcast(F32),
                                        ALU.subtract).then_inc(latA_done, 1)

            latent(0)
            stage_k = stage.rearrange("p (k n) -> p k n", k=KD)
            dve.wait_ge(setup_act, 3)
            nc.vector.tensor_tensor(wql[:, :, 0:HD], stage_k[:, :, 0:HD], wqh[:, :, 0:HD].bitcast(F32),
                                    ALU.subtract).then_inc(wq_split, 1)
            dve.wait_ge(trig_loaded, 32)
            for w in (2, 3, 0, 1):
                m = nc.vector.tensor_tensor(rope[:, w], trig_in[:, w % 2],
                                            nw[:, w, :].unsqueeze(1).broadcast_to([P, NT, HD]), ALU.mult)
            m.then_inc(tables_done, 1)
            dve.wait_ge(tables_done, 1)

            def rest_of_biases():
                nc.vector.tensor_copy(brow[0:1, HD:NB], braw[:, HD:NB]).then_inc(brow_link, 1)
                dve.wait_ge(brow_link, 1)
                nc.vector.tensor_tensor(brow[32:33, HD:NB], braw[:, HD:NB], brow[0:1, HD:NB].bitcast(F32),
                                        ALU.subtract).then_inc(brow_done, 1)

            def rest_of_wq(k):
                dve.wait_ge(setup_act, 3 + k + 1)
                nc.vector.tensor_tensor(wql[:, k, HD:NQ], stage_k[:, k, HD:NQ], wqh[:, k, HD:NQ].bitcast(F32),
                                        ALU.subtract).then_inc(wq_split, 1)

            def rotate(dst, src, h, which, j, done=None):
                m = nc.vector.tensor_tensor(heads_view(dst, h), heads_view(src, h),
                                            rope[:, which, j, :].unsqueeze(1).broadcast_to([P, h, HD]), ALU.mult)
                if done:
                    m.then_inc(done, 1)

            def partners(dst, src, h, which, j, done):
                for c in range(2):
                    m = nc.vector.tensor_tensor(blocks_view(dst, h, c), blocks_view(src, h, 1 - c),
                                                table_blocks(which + 1, j, c, h), ALU.mult)
                if done:
                    m.then_inc(done, 1)

            def topk(tb, qt, first, end):
                w = P * (qt + 1)
                base = (tb * NT + qt) * TOPK_LINKS
                if first == 0:
                    dve.wait_ge(s_in[qt % 2], tb * 32 + 16 * (qt // 2) + 16)
                for h in range(first, min(end, 2 * ROUNDS)):
                    dve.wait_ge(topk_link, base + h)
                    dve.sem_inc(passed_dve, 1)
                    if h % 2 == 0:
                        nc.vector.max(top8[:], work[:, qt % 2, 0:w]).then_inc(topk_link, 1)
                    else:
                        nc.vector.match_replace(work[:, qt % 2, 0:w], top8[:], work[:, qt % 2, 0:w], TAKEN).then_inc(topk_link, 1)
                if end == ALL:
                    dve.wait_ge(topk_link, base + 2 * ROUNDS)
                    if not (isinstance(tb, int) and tb == 0):
                        dve.wait_ge(mt_done, tb * NT + qt - 1)
                    mask = mask_rows(tb, qt)
                    nc.vector.tensor_scalar(mask[:, 0:w], work[:, qt % 2, 0:w], 0.5 * TAKEN, None, ALU.is_gt).then_inc(topk_link, 1)
                    dve.wait_ge(topk_link, base + TOPK_LINKS)
                    nc.vector.tensor_tensor(mask[:, w - P:w], mask[:, w - P:w], con[:, C_OFFDIAG:C_END],
                                            ALU.mult).then_inc(ns_done, 1)

            def rotate_cos(m_, j):
                if isinstance(m_, int) and m_ < LEAD:
                    dve.wait_ge(ss_done, m_ + 1)
                    dve.wait_ge(krope_link, 3 * B * NT)
                else:
                    dve.wait_ge(sq_done, m_ - LEAD + 1)
                dve.wait_ge(rope_link, 3 * m_)
                rotate(t1[:, 0:NK], query_bank(m_), GROUP, 0, j)

            def rotate_sin(m_, j):
                partners(t2[:, 0:NK], query_bank(m_), GROUP, 0, j, t2_done)
                if isinstance(m_, int) and m_ < LEAD:
                    dve.wait_ge(t2_done, m_ + 1)
                    dve.wait_ge(tr_done, m_)
                    dve.wait_ge(ktr_done, B * NT)
                    nc.vector.tensor_tensor(qn[:, 0:NK], t1[:, 0:NK], t2[:, 0:NK], ALU.add).then_inc(qadd_done, 1)

            def store_scores(b, q):
                dve.wait_ge(s_mm, b * NT + q + 1)
                dve.wait_ge(s_out[q % 2], b * 32 + 16 * (q // 2))
                w = P * q
                if w:
                    nc.vector.tensor_copy(s_out_sb[q % 2][:, 0:w], ps[:, 2, 0:w])
                nc.vector.tensor_tensor(s_out_sb[q % 2][:, w:w + P], ps[:, 2, w:w + P],
                                        con[:, C_CAUSAL:C_EYE], ALU.add).then_inc(s_ev, 1)

            def first_topk(b, j, k):
                at = max(0, (b - 1) * (NT + LAG) + j + 1) if b else 0
                if k < PER_ITERATION[at]:
                    qt, h = FIRST_HALVES[sum(PER_ITERATION[:at]) + k]
                    topk(0, qt, h, h + 1)

            def keys(b, last):
                for j in range(NT + LAG):
                    i = b * NT + j
                    if j < NT:
                        k_bank, q_bank = K_BANKS[j % 2]
                        first_topk(b, j, 0)
                        dve.wait_ge(ksq_done, i + 1)
                        if i >= 1:
                            dve.wait_ge(krope_link, 3 * i - 3)
                        rotate(T1[j % 2][:, 0:NK], ps[:, k_bank, :], NKV, 2, j)
                        first_topk(b, j, 1)
                        partners(T2[j % 2][:, 0:NK], ps[:, k_bank, :], NKV, 2, j, None)
                        first_topk(b, j, 2)
                        dve.wait_ge(kss_done, i + 1)
                        rotate(T1[j % 2][:, NK:], ps[:, q_bank, 0:HD], 1, 0, j)
                        partners(T2[j % 2][:, NK:], ps[:, q_bank, 0:HD], 1, 0, j, kt2_done)
                        first_topk(b, j, 3)
                        first_topk(b, j, 4)
                        first_topk(b, j, 5)
                    else:
                        first_topk(b, j, 0)
                        if not last:
                            (split_x, latent)[j - NT](b + 1)
                        first_topk(b, j, 1)
                    if b == 0:
                        if j == 0:
                            rest_of_biases()
                        if j in (2, 3):
                            rest_of_wq(j - 2)
                    if LAG <= j <= NT or last and j > NT:
                        store_scores(b, j - LAG)
                    if j == 0 and b >= 1:
                        store_scores(b - 1, NT - 1)
                    if j >= NT:
                        first_topk(b, j, 2)
                    if last and j >= NT:
                        rotate_cos(j - NT, j - NT)
                        rotate_sin(j - NT, j - NT)

            for b in range(B):
                keys(b, b == B - 1)

            def store_mask(tb, qt):
                dve.wait_ge(mt_done, tb * NT + qt + 1)
                nc.vector.tensor_copy(nselT[:, 0:qt + 1, P * qt:P * (qt + 1)],
                                      x_ps.bitcast(BF16)[:, 0:P * (qt + 1)].rearrange("p (k q) -> p k q", q=P)).then_inc(mc_done, 1)

            def distances(tb, u_before):
                dve.wait_ge(mc_done, tb * NT + NT)
                dve.wait_ge(u_done, u_before)
                for kt in range(NT):
                    o = slice(OFF[kt], OFF[kt] + PIECE[kt])
                    m = nc.vector.scalar_tensor_tensor(D[:, o], nselT[:, kt, P * kt:T], BIG,
                                                       con[:, C_DIST + OFF[kt]:C_DIST + OFF[kt] + PIECE[kt]], ALU.mult, ALU.add)
                m.then_inc(D_done, 1)
                dve.wait_ge(D_done, tb + 1)

            def biased(b, s):
                n = b * STEPS + s
                dve.wait_ge(th_done, n + 1)
                nc.vector.scalar_tensor_tensor(th[:], D[:], -slope(s) / SOFTCAP, th[:], ALU.mult, ALU.add).then_inc(u_done, 1)

            def squares_summed(m_):
                dve.wait_ge(rope_link, 3 * m_)
                nc.vector.tensor_reduce(ssq[:, 0:GROUP], heads_view(sq[:, 0:NK], GROUP), AX_X, ALU.add).then_inc(ss_done, 1)

            def normalise(b, s):
                n = b * STEPS + s
                dve.wait_ge(pv_done, n + 1)
                dve.wait_ge(yq_done, n)
                nc.vector.reciprocal(den4[:, 0:NT - 1], y_ps[:, :, HD])
                nc.vector.reciprocal(den4[:, NT - 1:NT], y3_ps[:, HD:HD + 1]).then_inc(rden_link, 1)
                dve.wait_ge(rden_link, n + 1)
                dve.wait_ge(yt_done, n)
                nc.vector.tensor_tensor(yq[:, 0:NT - 1, :], y_ps[:, :, 0:HD],
                                        den4[:, 0:NT - 1].unsqueeze(2).broadcast_to([P, NT - 1, HD]), ALU.mult)
                nc.vector.tensor_scalar(yq[:, NT - 1, :], y3_ps[:, 0:HD], den4[:, NT - 1:NT], None, ALU.mult).then_inc(yq_done, 1)

            def gated(b, s):
                n = b * STEPS + s
                dve.wait_ge(gt_done, n + 1)
                dve.wait_ge(yn_done, n + 1)
                dve.wait_ge(ygl_done, n)
                nc.vector.scalar_tensor_tensor(yg[:], gt[:], 1.0, yn[:], ALU.add, ALU.mult).then_inc(yg_done, 1)

            for m_ in range(LEAD):
                if m_ >= LAG:
                    rotate_cos(m_, m_ % NT)
                    rotate_sin(m_, m_ % NT)
                if m_ in MASK_AFTER:
                    store_mask(0, MASK_AFTER[m_])
                if m_ >= LAG:
                    g = slice(GROUP * (m_ - LAG), GROUP * (m_ - LAG + 1))
                    dve.wait_ge(wo_hi, m_ - LAG + 1)
                    nc.vector.tensor_tensor(wol[:, g, :], wo_raw[:, g, :], woh[:, g, :].bitcast(F32), ALU.subtract).then_inc(wo_split, 1)
                if m_ == NT:
                    distances(0, 0)
                    biased(0, 0)

            def ternary(i):
                half, minus_half = wscale[:, i:i + 1], wscale[:, 2 + i:3 + i]
                dve.wait_ge(fsum_mm, i + 1)
                nc.vector.tensor_scalar(half, x_ps[:, 0:1], 1.0 / (DFF * DIM), QUANT_EPS, ALU.mult, ALU.max).then_inc(fscale_link, 1)
                dve.wait_ge(fscale_link, 2 * i + 1)
                nc.vector.tensor_scalar(minus_half, half, -0.5, None, ALU.mult)
                nc.vector.tensor_scalar(half, half, 0.5, None, ALU.mult).then_inc(fscale_link, 1)
                dve.wait_ge(fscale_link, 2 * i + 2)
                nc.vector.tensor_scalar(wscr, wraw, minus_half, None, ALU.is_lt).then_inc(ternary_link, 1)
                dve.wait_ge(ternary_link, i + 1)
                nc.vector.scalar_tensor_tensor(wql[:, i, :], wraw, half, wscr,
                                               ALU.is_gt, ALU.subtract).then_inc(ffnw_done, 1)

            def split_x1(b):
                for k in range(KD):
                    dve.wait_ge(fxhi_done, b * KD + k + 1)
                    dve.wait_ge(h_mm, b * NF)
                    nc.vector.tensor_tensor(xl[:, k, :], ps[:, k, :], xh[:, k, :].bitcast(F32), ALU.subtract).then_inc(fxlo_done, 1)

            def attended(b, j):
                return r1[:, bass.ds(b * NT + j, 1), :].rearrange("p a d -> p (a d)")

            def ln1_statistics(b):
                for j in range(NT):
                    m = nc.vector.bn_stats(stats[:, 0, j, :], attended(b, j))
                m.then_inc(ln1_link, 1)
                dve.wait_ge(ln1_link, b + 1)
                dve.wait_ge(fpool1_link, b)
                dve.sem_inc(passed_dve, 1)
                for j in range(NT):
                    m = nc.vector.bn_aggr(mv[:, 0, j, :], stats[:, 0, j, :])
                m.then_inc(st1_done, 1)

            def ln1(b):
                dve.wait_ge(frstd1_done, b + 1)
                dve.wait_ge(fxt_done, b * KD)
                dve.wait_ge(x1r_done, b)
                for j in range(NT):
                    nc.vector.tensor_scalar(x1[:, j, :], attended(b, j), mv[:, 0, j, 0:1], rstd[:, j:j + 1],
                                            ALU.subtract, ALU.mult).then_inc(x1_done, 1)

            def ln2_statistics(b):
                dve.wait_ge(r2_done, b * 2 + 2)
                for j in range(NT):
                    m = nc.vector.bn_stats(stats[:, 1, j, :], r2[:, j, :])
                m.then_inc(ln2_link, 1)
                dve.wait_ge(ln2_link, b + 1)
                dve.sem_inc(passed_dve, 1)
                for j in range(NT):
                    m = nc.vector.bn_aggr(mv[:, 1, j, :], stats[:, 1, j, :])
                m.then_inc(st2_done, 1)

            def ln2(b):
                dve.wait_ge(frstd2_done, b + 1)
                for j in range(NT):
                    nc.vector.tensor_scalar(ffn_y[:, j, :], r2[:, j, :], mv[:, 1, j, 0:1], rstd[:, 8 + j:9 + j],
                                            ALU.subtract, ALU.mult).then_inc(y_done, 1)

            def residual(b):
                dve.wait_ge(wo_done, b * STEPS + STEPS)
                dve.wait_ge(r1_in, 16)
                for a in range(2):
                    r = r1[:, bass.ds(b * NT + 2 * a, 2), :]
                    m = nc.vector.tensor_tensor(r, r, o_ps[:, a, :].rearrange("p (c d) -> p c d", c=2), ALU.add)
                m.then_inc(res_done, 1)

            def heads(b, last):
                first = isinstance(b, int) and b == 0
                for s in range(STEPS):
                    n = b * STEPS + s
                    if s >= 1:
                        gated(b, s - 1)
                    elif not first:
                        gated(b - 1, STEPS - 1)
                    if not last:
                        for part in EARLY.get(s, ()):
                            topk(b + 1, *part)
                        if s in TURN_AT:
                            store_mask(b + 1, TURN_AT[s])
                        if s == STEPS - 1:
                            distances(b + 1, n + 1)
                    if s + 1 < STEPS:
                        biased(b, s + 1)
                    elif not last:
                        biased(b + 1, 0)
                    normalise(b, s)
                    more = s + LEAD < STEPS or not last
                    if more:
                        rotate_cos(n + LEAD, (s + LEAD) % NT)
                        rotate_sin(n + LEAD, (s + LEAD) % NT)
                        squares_summed(n + LEAD)
                    if s == 0 and not first:
                        residual(b - 1)
                    if not last:
                        for part in LATE.get(s, ()):
                            topk(b + 1, *part)
                    if last and s in SCALE_AT:
                        ternary(SCALE_AT.index(s))
                    if last and s == LN_AT:
                        ln1_statistics(0)
                    if last and s == LN_AT + 1:
                        ln1(0)
                    if last and s == STEPS - 1:
                        split_x1(0)
            batches(dve, heads, True)
            gated(B - 1, STEPS - 1)
            residual(B - 1)

            def ffn(b, last):
                for f in range(NF):
                    i = b * NF + f
                    dve.wait_ge(h_done, i + 1)
                    dve.wait_ge(h2_done, i + 1)
                    if not (isinstance(i, int) and i < HSLOTS):
                        dve.wait_ge(f2_mm, i - HSLOTS + 1)
                    nc.vector.tensor_tensor(hr[:, f % HSLOTS, 1, :], hf[:, f % HSLOTS, :], hr[:, f % HSLOTS, 0, :].bitcast(F32),
                                            ALU.subtract).then_inc(hlo_done, 1)
                    first = isinstance(b, int) and b == 0
                    if f == 1 and not first:
                        ln2_statistics(b - 1)
                    if f == 2 and not last:
                        ln1_statistics(b + 1)
                    if f == 3 and not first:
                        ln2(b - 1)
                    if f == 5 and not last:
                        ln1(b + 1)
                if not last:
                    split_x1(b + 1)
                dve.wait_ge(f2_mm, b * NF + NF)
                dve.wait_ge(y_done, b * NT)
                dve.wait_ge(x1r_done, b + 1)
                for a in range(2):
                    nc.vector.tensor_tensor(r2[:, 2 * a:2 * a + 2, :], ps[:, 4 + a, :].rearrange("p (c d) -> p c d", c=2),
                                            r1[:, bass.ds(b * NT + 2 * a, 2), :], ALU.add).then_inc(r2_done, 1)
                if not (isinstance(b, int) and b == 0):
                    dve.wait_ge(y_out, b * 16)

            batches(dve, ffn, True)
            ln2_statistics(B - 1)
            ln2(B - 1)

        @block.gpsimd
        def _(pool):
            nc.gpsimd.memset(mhalf[:], -0.5).then_inc(setup_pool, 1)
            pool.wait_ge(setup_pool, 1)

            def keys(b, last):
                for j in range(NT):
                    i = b * NT + j
                    r = rstd[:, 8 * (j % 2):8 * (j % 2) + NKV + 1]
                    pool.wait_ge(kss_done, i + 1)
                    pool.wait_ge(krope_link, 3 * i)
                    pool.sem_inc(passed_pool, 1)
                    nc.gpsimd.tensor_scalar(msq[:, 0:NKV + 1], ssq[:, 0:NKV + 1], 1.0 / HD, RMS_EPS, ALU.mult,
                                            ALU.add).then_inc(krope_link, 1)
                    pool.wait_ge(krope_link, 3 * i + 1)
                    pool.wait_ge(kn_done, i - 1 if j else i)
                    nc.gpsimd.tensor_tensor(r, msq[:, 0:NKV + 1], mhalf[:, 0:NKV + 1], ALU.pow).then_inc(krope_link, 1)
                    pool.wait_ge(kt2_done, i + 1)
                    if not (isinstance(i, int) and i < 2):
                        pool.wait_ge(ktr_done, i - 1)
                    nc.gpsimd.tensor_tensor(QN[j % 2], T1[j % 2], T2[j % 2], ALU.add).then_inc(krope_link, 1)

            for b in range(B):
                keys(b, b == B - 1)

            def query_tile(m_):
                pool.wait_ge(ss_done, m_ + 1)
                pool.wait_ge(qn_done, m_)
                pool.sem_inc(passed_pool, 1)
                nc.gpsimd.tensor_scalar(msq[:, 0:GROUP], ssq[:, 0:GROUP], 1.0 / HD, RMS_EPS, ALU.mult,
                                        ALU.add).then_inc(rope_link, 1)
                pool.wait_ge(rope_link, 3 * m_ + 1)
                nc.gpsimd.tensor_tensor(rstd[:, 0:GROUP], msq[:, 0:GROUP], mhalf[:, 0:GROUP], ALU.pow).then_inc(rope_link, 1)
                if isinstance(m_, int) and m_ < LEAD:
                    pool.wait_ge(qadd_done, m_ + 1)
                    pool.sem_inc(rope_link, 1)
                else:
                    pool.wait_ge(t2_done, m_ + 1)
                    pool.wait_ge(tr_done, m_)
                    nc.gpsimd.tensor_tensor(qn[:, 0:NK], t1[:, 0:NK], t2[:, 0:NK], ALU.add).then_inc(rope_link, 1)
                pool.wait_ge(rope_link, 3 * m_ + 3)
                nc.gpsimd.tensor_tensor(heads_view(qn[:, 0:NK], GROUP), heads_view(qn[:, 0:NK], GROUP),
                                        rstd[:, 0:GROUP].unsqueeze(2).broadcast_to([P, GROUP, HD]), ALU.mult).then_inc(qn_done, 1)

            pool.wait_ge(kn_done, B * NT)
            for m_ in range(LEAD - 1):
                query_tile(m_)

            def gated_lo(b, s):
                n = b * STEPS + s
                pool.wait_ge(ygh_done, n + 1)
                pool.wait_ge(wo_done, n)
                nc.gpsimd.tensor_tensor(ygl[:], yg[:], ygh[:].bitcast(F32), ALU.subtract).then_inc(ygl_done, 1)

            def rstd1(b):
                pool.wait_ge(st1_done, b + 1)
                pool.sem_inc(passed_pool, 1)
                nc.gpsimd.tensor_scalar(msq[:, 0:NT], mv[:, 0, :, 1], LN_EPS, None, ALU.add).then_inc(fpool1_link, 1)
                pool.wait_ge(fpool1_link, b + 1)
                nc.gpsimd.tensor_tensor(rstd[:, 0:NT], msq[:, 0:NT], mhalf[:, 0:NT], ALU.pow).then_inc(frstd1_done, 1)

            def keep_x1(b):
                pool.wait_ge(x1_done, b * NT + NT)
                pool.sem_inc(passed_pool, 1)
                nc.gpsimd.tensor_copy(r1[:, bass.ds(b * NT, NT), :], x1).then_inc(x1r_done, 1)

            def heads(b, last):
                first = isinstance(b, int) and b == 0
                for s in range(STEPS):
                    if s + LEAD - 1 < STEPS or not last:
                        query_tile(b * STEPS + s + LEAD - 1)
                    if s >= 1:
                        gated_lo(b, s - 1)
                    elif not first:
                        gated_lo(b - 1, STEPS - 1)
                    if last and s == LN_AT:
                        rstd1(0)
                    if last and s == LN_AT + 2:
                        keep_x1(0)

            batches(pool, heads, True)

            def rstd2(b):
                pool.wait_ge(st2_done, b + 1)
                pool.sem_inc(passed_pool, 1)
                nc.gpsimd.tensor_scalar(msq[:, 4:4 + NT], mv[:, 1, :, 1], LN_EPS, None, ALU.add).then_inc(fpool2_link, 1)
                pool.wait_ge(fpool2_link, b + 1)
                nc.gpsimd.tensor_tensor(rstd[:, 8:8 + NT], msq[:, 4:4 + NT], mhalf[:, 0:NT], ALU.pow).then_inc(frstd2_done, 1)

            gated_lo(B - 1, STEPS - 1)

            def ffn(b, last):
                if not (isinstance(b, int) and b == 0):
                    rstd2(b - 1)
                if not last:
                    rstd1(b + 1)
                    keep_x1(b + 1)

            batches(pool, ffn, True)
            rstd2(B - 1)


def kernel(**inputs):
    import concourse.bacc as bacc
    from concourse.bass_utils import run_bass_kernel_spmd

    a = {k[3:]: np.asarray(v) for k, v in inputs.items()}
    order, partner = np.array(ORDER), np.array(PARTNER)

    def by_head(v, n):
        h = v[..., :n * HD].reshape(*v.shape[:-1], n, HD)[..., order]
        return np.concatenate([h.reshape(*v.shape[:-1], n * HD), v[..., n * HD:]], -1)

    qn, kn = a["attn_qn_w"], a["attn_kn_w"]
    arrays = {
        "x": a["attn_x"],
        "w_q": by_head(a["attn_w_q"], HEADS),
        "w_down": a["attn_w_down"],
        "w_up": by_head(a["attn_w_up"], NKV),
        "w_o": a["attn_w_o"],
        "gate_w": a["attn_gate_w"],
        "w1": a["ffn_w1"].T,
        "w2": a["ffn_w2"].T,
        "biases": np.concatenate([by_head(a["attn_b_q"], HEADS), a["attn_b_o"], a["ffn_b2"],
                                  by_head(a["attn_b_up"], NKV)])[None],
        "gate_b": a["attn_gate_b"].T,
        "b_down": np.concatenate([a["attn_b_down"]] * 2)[:, None],
        "b1": a["ffn_b1"].reshape(NF, P).T,
        "norm_w": np.stack([qn[order], qn[partner], kn[order], kn[partner]]),
        "table": constants()[0],
        "trig": constants()[1],
    }
    arrays = {f"in_{k}": np.ascontiguousarray(v) for k, v in arrays.items()}
    nc = bacc.Bacc("TRN2", target_bir_lowering=False, num_devices=1)
    args = [nc.dram_tensor(k, v.shape, mybir.dt.from_np(v.dtype), kind="ExternalInput").ap() for k, v in arrays.items()]
    out = nc.dram_tensor("out", (B, T, DIM), F32, kind="ExternalOutput").ap()
    layer_program(nc, *args, out)
    r = run_bass_kernel_spmd(nc, [arrays], core_ids=[0])
    return r.results[0]["out"]
```
